# Optimizing a Trainium2 kernel written in Bass

```python
import numpy as np
import jax
import jax.numpy as jnp

def _softmax(x, axis=-1):
    return jax.nn.softmax(x, axis=axis)

def _gelu(x):
    return jax.nn.gelu(x, approximate=True)

def _silu(x):
    return jax.nn.silu(x)

def _sigmoid(x):
    return jax.nn.sigmoid(x)

def _layernorm(x, axis=-1, eps=1e-05):
    m = jnp.mean(x, axis=axis, keepdims=True)
    v = jnp.var(x, axis=axis, keepdims=True)
    return (x - m) / jnp.sqrt(v + eps)

def _scatter_add(tgt, idx, src, axis=0):
    return tgt.at[idx].add(src)

def _segment_sum(src, seg, n):
    return jax.ops.segment_sum(src, seg, n)
kernel_name = 'mk_gnn_resnorm_d4_gnn_r32_a93b61'

def setup_inputs(seed: int=0):
    np.random.seed(seed)
    _w = jnp.asarray

    def _rec_inputs():
        import jax
        import jax.numpy as jnp
        _gk = jax.random.key(seed)
        x = -0.0003929 + 0.9999 * jax.random.normal(jax.random.fold_in(_gk, 1), (3125, 256), jnp.float32)
        src = jax.random.randint(jax.random.fold_in(_gk, 2), (50000,), 0, 3125, jnp.int32)
        dst = jnp.minimum((3125 * jax.random.uniform(jax.random.fold_in(_gk, 3), (50000,)) ** 2.0).astype(jnp.int32), 99999)
        _o = jnp.argsort(dst, stable=True)
        src = src[_o]
        dst = dst[_o]
        edge_attr_50 = 0.000154925 + 1.00009 * jax.random.normal(jax.random.fold_in(_gk, 13), (50000, 50), jnp.float32)
        edge_type_2 = jax.random.randint(jax.random.fold_in(_gk, 15), (50000,), 0, 2, jnp.int32)
        edge_weight = 0.00540447 + 1.00226 * jax.random.normal(jax.random.fold_in(_gk, 16), (50000,), jnp.float32)
        return (x, src, dst, edge_attr_50, edge_type_2, edge_weight)
    x, src, dst, edge_attr_50, edge_type_2, edge_weight = _rec_inputs()

    def _L0_gnn_setup():
        import jax, jax.numpy as jnp
        import numpy as np
        from itertools import combinations
        NDIM = 256
        BATCH = 2048

        def _build_mat(rots, idx_i, idx_j, ndim):

            def step(mat, t):
                i, j, theta = t
                c = jnp.cos(theta)
                s = jnp.sin(theta)
                ri = mat[i]
                rj = mat[j]
                mat = mat.at[i].set(c * ri - s * rj)
                mat = mat.at[j].set(s * ri + c * rj)
                return (mat, None)
            mat0 = jnp.eye(ndim, dtype=rots.dtype)
            mat, _ = jax.lax.scan(step, mat0, (idx_i, idx_j, rots))
            return mat.T
        key = jax.random.key(seed)
        k1, k2 = jax.random.split(key)
        pairs = np.array(list(combinations(range(NDIM), 2)), dtype=np.int32)
        return {'x': jax.random.normal(k1, (BATCH, NDIM), dtype=jnp.float32), 'rots': jax.random.normal(k2, (pairs.shape[0],), dtype=jnp.float32), 'idx_i': jnp.asarray(pairs[:, 0]), 'idx_j': jnp.asarray(pairs[:, 1])}
    _L0_gnn_all = _L0_gnn_setup()
    _L0_gnn_in = {k: v for k, v in _L0_gnn_all.items() if k in ()}
    del _L0_gnn_all

    def _L1_gnn_setup():
        import jax, jax.numpy as jnp
        import numpy as np
        N, E, B = (1250, 10000, 64)
        D = 256
        HID = 128
        H = 4
        SLOPE = 0.2

        def _segment_softmax(alpha, dst, n):
            amax = jax.lax.stop_gradient(jax.ops.segment_max(alpha, dst, num_segments=n))
            ex = jnp.exp(alpha - amax[dst])
            den = jax.ops.segment_sum(ex, dst, num_segments=n)
            return ex / (den[dst] + 1e-16)

        def _rgat(x, src, dst, etype, W, Q, K, b, heads, out_ch, n):
            xw = jnp.einsum('ni,rio->rno', x, W)
            out_i = xw[etype, dst]
            out_j = xw[etype, src]
            alpha = jax.nn.leaky_relu(out_i @ Q + out_j @ K, SLOPE)
            alpha = _segment_softmax(alpha, dst, n)
            msg = (out_j.reshape(-1, heads, out_ch) * alpha[..., None]).reshape(-1, heads * out_ch)
            return jax.ops.segment_sum(msg, dst, num_segments=n) + b
        key = jax.random.key(seed)
        ks = jax.random.split(key, 20)
        s = 0.05
        return {'x': jax.random.normal(ks[0], (N, D), jnp.float32), 'query': jax.random.normal(ks[1], (B, D), jnp.float32), 'edge_index': jax.random.randint(ks[2], (2, E), 0, N), 'edge_type': jax.random.randint(ks[3], (E,), 0, 2), 'batch': jnp.sort(jax.random.randint(ks[4], (N,), 0, B)), 'gate_w1': jax.random.normal(ks[5], (2 * D, D), jnp.float32) * s, 'gate_b1': jnp.zeros((D,), jnp.float32), 'gate_w2': jax.random.normal(ks[6], (D, D), jnp.float32) * s, 'gate_b2': jnp.zeros((D,), jnp.float32), 'W1': jax.random.normal(ks[7], (2, 3 * D, H * HID), jnp.float32) * s, 'q1': jax.random.normal(ks[8], (H * HID, H), jnp.float32) * s, 'k1': jax.random.normal(ks[9], (H * HID, H), jnp.float32) * s, 'b1': jnp.zeros((H * HID,), jnp.float32), 'W2': jax.random.normal(ks[10], (2, H * HID, H * HID), jnp.float32) * s, 'q2': jax.random.normal(ks[11], (H * HID, H), jnp.float32) * s, 'k2': jax.random.normal(ks[12], (H * HID, H), jnp.float32) * s, 'b2': jnp.zeros((H * HID,), jnp.float32), 'W3': jax.random.normal(ks[13], (2, H * HID, HID), jnp.float32) * s, 'q3': jax.random.normal(ks[14], (HID, 1), jnp.float32) * s, 'k3': jax.random.normal(ks[15], (HID, 1), jnp.float32) * s, 'b3': jnp.zeros((HID,), jnp.float32), 'proj_w': jax.random.normal(ks[16], (HID, D), jnp.float32) * s, 'proj_b': jnp.zeros((D,), jnp.float32)}
    _L1_gnn_all = _L1_gnn_setup()
    _L1_gnn_in = {k: v for k, v in _L1_gnn_all.items() if k in ('query', 'gate_w1', 'gate_b1', 'gate_w2', 'gate_b2', 'W1', 'q1', 'k1', 'b1', 'W2', 'q2', 'k2', 'b2', 'W3', 'q3', 'k3', 'b3', 'proj_w', 'proj_b')}
    del _L1_gnn_all

    def _L2_gnn_setup():
        import jax, jax.numpy as jnp
        import numpy as np
        N, E, H, G = (50000, 25000, 256, 50)
        CUTOFF = 10.0
        PI = float(np.pi)
        LOG2 = float(np.log(2.0))

        def ssp(x):
            return jax.nn.softplus(x) - LOG2
        key = jax.random.key(seed)
        ks = jax.random.split(key, 16)

        def lin(kw, kb, fan_in, fan_out):
            s = float(np.sqrt(6.0 / (fan_in + fan_out)))
            W = jax.random.uniform(kw, (fan_in, fan_out), minval=-s, maxval=s, dtype=jnp.float32)
            b = jnp.zeros((fan_out,), jnp.float32)
            return (W, b)
        h = jax.random.normal(ks[0], (N, H), dtype=jnp.float32)
        edge_index = jax.random.randint(ks[1], (2, E), 0, N, dtype=jnp.int64)
        edge_weight = jax.random.uniform(ks[2], (E,), dtype=jnp.float32) * CUTOFF
        edge_attr = jax.random.normal(ks[3], (E, G), dtype=jnp.float32)
        aw_W, aw_b = lin(ks[4], ks[5], H, H)
        m1_W, m1_b = lin(ks[6], ks[7], G, H)
        m2_W, m2_b = lin(ks[8], ks[9], H, H)
        o1_W, o1_b = lin(ks[10], ks[11], H, H)
        o2_W, o2_b = lin(ks[12], ks[13], H, H)
        return {'h': h, 'edge_index': edge_index, 'edge_weight': edge_weight, 'edge_attr': edge_attr, 'aw_W': aw_W, 'aw_b': aw_b, 'm1_W': m1_W, 'm1_b': m1_b, 'm2_W': m2_W, 'm2_b': m2_b, 'o1_W': o1_W, 'o1_b': o1_b, 'o2_W': o2_W, 'o2_b': o2_b}
    _L2_gnn_all = _L2_gnn_setup()
    _L2_gnn_in = {k: v for k, v in _L2_gnn_all.items() if k in ('aw_W', 'aw_b', 'm1_W', 'm1_b', 'm2_W', 'm2_b', 'o1_W', 'o1_b', 'o2_W', 'o2_b')}
    del _L2_gnn_all

    def _L3_gnn_setup():
        import jax, jax.numpy as jnp
        import numpy as np
        N_NODES = 3125
        IN_FEATS = 256
        OUT_FEATS = 256
        N_EDGES = 100000
        key = jax.random.key(seed)
        k1, k2, k3, k4 = jax.random.split(key, 4)
        x = jax.random.normal(k1, (N_NODES, IN_FEATS), dtype=jnp.float32)
        edge_index = jax.random.randint(k2, (2, N_EDGES), 0, N_NODES, dtype=jnp.int64)
        scale = 1.0 / np.sqrt(IN_FEATS)
        W = jax.random.uniform(k3, (IN_FEATS, OUT_FEATS), dtype=jnp.float32, minval=-scale, maxval=scale)
        b = jax.random.uniform(k4, (OUT_FEATS,), dtype=jnp.float32, minval=-scale, maxval=scale)
        return {'x': x, 'edge_index': edge_index, 'W': W, 'b': b}
    _L3_gnn_all = _L3_gnn_setup()
    _L3_gnn_in = {k: v for k, v in _L3_gnn_all.items() if k in ('W', 'b')}
    del _L3_gnn_all
    return {'x': x, 'src': src, 'dst': dst, 'edge_attr_50': edge_attr_50, 'edge_type_2': edge_type_2, 'edge_weight': edge_weight, 'L1_gnn_query': _L1_gnn_in['query'], 'L1_gnn_gate_w1': _L1_gnn_in['gate_w1'], 'L1_gnn_gate_b1': _L1_gnn_in['gate_b1'], 'L1_gnn_gate_w2': _L1_gnn_in['gate_w2'], 'L1_gnn_gate_b2': _L1_gnn_in['gate_b2'], 'L1_gnn_W1': _L1_gnn_in['W1'], 'L1_gnn_q1': _L1_gnn_in['q1'], 'L1_gnn_k1': _L1_gnn_in['k1'], 'L1_gnn_b1': _L1_gnn_in['b1'], 'L1_gnn_W2': _L1_gnn_in['W2'], 'L1_gnn_q2': _L1_gnn_in['q2'], 'L1_gnn_k2': _L1_gnn_in['k2'], 'L1_gnn_b2': _L1_gnn_in['b2'], 'L1_gnn_W3': _L1_gnn_in['W3'], 'L1_gnn_q3': _L1_gnn_in['q3'], 'L1_gnn_k3': _L1_gnn_in['k3'], 'L1_gnn_b3': _L1_gnn_in['b3'], 'L1_gnn_proj_w': _L1_gnn_in['proj_w'], 'L1_gnn_proj_b': _L1_gnn_in['proj_b'], 'L2_gnn_aw_W': _L2_gnn_in['aw_W'], 'L2_gnn_aw_b': _L2_gnn_in['aw_b'], 'L2_gnn_m1_W': _L2_gnn_in['m1_W'], 'L2_gnn_m1_b': _L2_gnn_in['m1_b'], 'L2_gnn_m2_W': _L2_gnn_in['m2_W'], 'L2_gnn_m2_b': _L2_gnn_in['m2_b'], 'L2_gnn_o1_W': _L2_gnn_in['o1_W'], 'L2_gnn_o1_b': _L2_gnn_in['o1_b'], 'L2_gnn_o2_W': _L2_gnn_in['o2_W'], 'L2_gnn_o2_b': _L2_gnn_in['o2_b'], 'L3_gnn_W': _L3_gnn_in['W'], 'L3_gnn_b': _L3_gnn_in['b']}

def reference(x, src, dst, edge_attr_50, edge_type_2, edge_weight, L1_gnn_query, L1_gnn_gate_w1, L1_gnn_gate_b1, L1_gnn_gate_w2, L1_gnn_gate_b2, L1_gnn_W1, L1_gnn_q1, L1_gnn_k1, L1_gnn_b1, L1_gnn_W2, L1_gnn_q2, L1_gnn_k2, L1_gnn_b2, L1_gnn_W3, L1_gnn_q3, L1_gnn_k3, L1_gnn_b3, L1_gnn_proj_w, L1_gnn_proj_b, L2_gnn_aw_W, L2_gnn_aw_b, L2_gnn_m1_W, L2_gnn_m1_b, L2_gnn_m2_W, L2_gnn_m2_b, L2_gnn_o1_W, L2_gnn_o1_b, L2_gnn_o2_W, L2_gnn_o2_b, L3_gnn_W, L3_gnn_b):
    import jax
    import jax.numpy as jnp

    def _L0_gnn_ref(x, rots, idx_i, idx_j):
        import jax, jax.numpy as jnp
        import numpy as np
        from itertools import combinations
        NDIM = 256
        BATCH = 2048

        def _build_mat(rots, idx_i, idx_j, ndim):

            def step(mat, t):
                i, j, theta = t
                c = jnp.cos(theta)
                s = jnp.sin(theta)
                ri = mat[i]
                rj = mat[j]
                mat = mat.at[i].set(c * ri - s * rj)
                mat = mat.at[j].set(s * ri + c * rj)
                return (mat, None)
            mat0 = jnp.eye(ndim, dtype=rots.dtype)
            mat, _ = jax.lax.scan(step, mat0, (idx_i, idx_j, rots))
            return mat.T
        m = _build_mat(rots, idx_i, idx_j, x.shape[-1])
        return x @ m

    def _L1_gnn_ref(x, query, edge_index, edge_type, batch, gate_w1, gate_b1, gate_w2, gate_b2, W1, q1, k1, b1, W2, q2, k2, b2, W3, q3, k3, b3, proj_w, proj_b):
        import jax, jax.numpy as jnp
        import numpy as np
        N, E, B = (1250, 10000, 64)
        D = 256
        HID = 128
        H = 4
        SLOPE = 0.2

        def _segment_softmax(alpha, dst, n):
            amax = jax.lax.stop_gradient(jax.ops.segment_max(alpha, dst, num_segments=n))
            ex = jnp.exp(alpha - amax[dst])
            den = jax.ops.segment_sum(ex, dst, num_segments=n)
            return ex / (den[dst] + 1e-16)

        def _rgat(x, src, dst, etype, W, Q, K, b, heads, out_ch, n):
            xw = jnp.einsum('ni,rio->rno', x, W)
            out_i = xw[etype, dst]
            out_j = xw[etype, src]
            alpha = jax.nn.leaky_relu(out_i @ Q + out_j @ K, SLOPE)
            alpha = _segment_softmax(alpha, dst, n)
            msg = (out_j.reshape(-1, heads, out_ch) * alpha[..., None]).reshape(-1, heads * out_ch)
            return jax.ops.segment_sum(msg, dst, num_segments=n) + b
        n = x.shape[0]
        src, dst = (edge_index[0], edge_index[1])
        q_node = query[batch]
        interaction = x * q_node
        gh = jax.nn.relu(jnp.concatenate([x, q_node], axis=-1) @ gate_w1 + gate_b1)
        gate = jax.nn.sigmoid(gh @ gate_w2 + gate_b2)
        x0 = x * gate
        h = jnp.concatenate([x0, q_node, interaction], axis=-1)
        h = jax.nn.relu(_rgat(h, src, dst, edge_type, W1, q1, k1, b1, H, HID, n))
        h = h + jax.nn.relu(_rgat(h, src, dst, edge_type, W2, q2, k2, b2, H, HID, n))
        h = jax.nn.relu(_rgat(h, src, dst, edge_type, W3, q3, k3, b3, 1, HID, n))
        out = h @ proj_w + proj_b + x0
        nrm = jnp.linalg.norm(out, axis=-1, keepdims=True)
        return out / jnp.maximum(nrm, 1e-12)

    def _L2_gnn_ref(h, edge_index, edge_weight, edge_attr, aw_W, aw_b, m1_W, m1_b, m2_W, m2_b, o1_W, o1_b, o2_W, o2_b):
        import jax, jax.numpy as jnp
        import numpy as np
        N, E, H, G = (50000, 25000, 256, 50)
        CUTOFF = 10.0
        PI = float(np.pi)
        LOG2 = float(np.log(2.0))

        def ssp(x):
            return jax.nn.softplus(x) - LOG2
        n_nodes = h.shape[0]
        h1 = h @ aw_W + aw_b
        C = 0.5 * (jnp.cos(edge_weight * (PI / CUTOFF)) + 1.0)
        Wf = ssp(ssp(edge_attr @ m1_W + m1_b) @ m2_W + m2_b)
        Wf = Wf * C[:, None]
        src, dst = (edge_index[0], edge_index[1])
        msg = h1[src] * Wf
        agg = jax.ops.segment_sum(msg, dst, num_segments=n_nodes)
        out = ssp(agg @ o1_W + o1_b) @ o2_W + o2_b
        return out

    def _L3_gnn_ref(x, edge_index, W, b):
        import jax, jax.numpy as jnp
        import numpy as np
        N_NODES = 3125
        IN_FEATS = 256
        OUT_FEATS = 256
        N_EDGES = 100000
        n = x.shape[0]
        row = edge_index[0]
        col = edge_index[1]
        h = x @ W + b
        agg = jax.ops.segment_sum(h[col], row, num_segments=n)
        deg = jax.ops.segment_sum(jnp.ones((edge_index.shape[1],), dtype=h.dtype), row, num_segments=n)
        inv_deg = jnp.where(deg > 0, 1.0 / jnp.where(deg > 0, deg, 1.0), 0.0)
        return agg * inv_deg[:, None]
    edge_index = jnp.stack([src, dst])
    batch0 = jnp.zeros((3125,), jnp.int32)
    x = _layernorm(x + _L0_gnn_ref(x, edge_weight, src, dst), axis=-1)
    x = _layernorm(x + _L1_gnn_ref(x, L1_gnn_query, edge_index, edge_type_2, batch0, L1_gnn_gate_w1, L1_gnn_gate_b1, L1_gnn_gate_w2, L1_gnn_gate_b2, L1_gnn_W1, L1_gnn_q1, L1_gnn_k1, L1_gnn_b1, L1_gnn_W2, L1_gnn_q2, L1_gnn_k2, L1_gnn_b2, L1_gnn_W3, L1_gnn_q3, L1_gnn_k3, L1_gnn_b3, L1_gnn_proj_w, L1_gnn_proj_b), axis=-1)
    x = _layernorm(x + _L2_gnn_ref(x, edge_index, edge_weight, edge_attr_50, L2_gnn_aw_W, L2_gnn_aw_b, L2_gnn_m1_W, L2_gnn_m1_b, L2_gnn_m2_W, L2_gnn_m2_b, L2_gnn_o1_W, L2_gnn_o1_b, L2_gnn_o2_W, L2_gnn_o2_b), axis=-1)
    x = _layernorm(x + _L3_gnn_ref(x, edge_index, L3_gnn_W, L3_gnn_b), axis=-1)
    return x

_drawn_inputs = setup_inputs


def setup_inputs(seed=0):
    import zlib

    import numpy as np

    out = dict(_drawn_inputs(seed))
    spreads = {'L1_gnn_gate_b1': (0.0, 2.0),
     'L1_gnn_gate_b2': (0.0, 2.0),
     'L1_gnn_b1': (0.0, 2.0),
     'L1_gnn_b2': (0.0, 2.0),
     'L1_gnn_b3': (0.0, 2.0),
     'L1_gnn_proj_b': (0.0, 2.0),
     'L2_gnn_aw_b': (0.0, 0.1),
     'L2_gnn_m1_b': (0.0, 0.1),
     'L2_gnn_m2_b': (0.0, 0.1),
     'L2_gnn_o1_b': (0.0, 0.1),
     'L2_gnn_o2_b': (0.0, 0.1)}
    factors = {'L1_gnn_query': 3.284,
     'L1_gnn_gate_w1': 4.755,
     'L1_gnn_gate_w2': 3.77,
     'L1_gnn_W1': 3.187,
     'L1_gnn_q1': 8.0,
     'L1_gnn_k1': 8.0,
     'L1_gnn_W2': 6.216,
     'L1_gnn_q2': 8.0,
     'L1_gnn_k2': 8.0,
     'L1_gnn_q3': 42.182,
     'L1_gnn_k3': 8.0}
    for name, (base, spread) in spreads.items():
        noise = np.random.default_rng([zlib.crc32(name.encode()), seed]).standard_normal(out[name].shape)
        drawn = base * np.exp(spread * noise) if base else spread * noise
        out[name] = jnp.asarray(drawn.astype(out[name].dtype))
    for name, factor in factors.items():
        out[name] = (out[name] * factor).astype(out[name].dtype)
    return out
```

```python
from contextlib import ExitStack

import numpy as np

import concourse.bass as bass
from concourse import mybir

F32 = mybir.dt.float32
I32 = mybir.dt.int32
ALU = mybir.AluOpType
ACT = mybir.ActivationFunctionType
AX = mybir.AxisListType

N, E, D = 3125, 50000, 256
P = 125
NT, ET = N // P, E // P
EC = 100
NEC = ET // EC

K = 64
R = 2 * K
CP, CA = 112, 7
NCH = CP * CA
G = 4
NG = NCH // G
STAGES = NG + 2
NCOL = (STAGES + 2) * G
LV = 6
TWO_PI_HI, TWO_PI_LO = 6.28125, 0.0019353071795864769
ROUND = 12582912.0
PI_SAFE = 3.1415925
BIG = 1.0e30


def host_constants():
    t = np.arange(R) % K
    masks = np.zeros((128, LV + 1, G, 128), np.float32)
    for lv in range(LV):
        b = t // (1 << lv)
        masks[:, lv] = ((b[:, None] + 1 == b[None, :]) & (b[None, :] % 2 == 1))[:, None, :]
    ident = np.eye(128, dtype=np.float32)
    masks[:, LV] = ident[:, None, :]
    iota = np.broadcast_to(np.arange(512, dtype=np.float32), (128, 512))
    column = np.stack([np.arange(128), np.arange(128) + 128, np.arange(128) + N], 1).astype(np.float32)
    tri = (np.arange(128)[:, None] < np.arange(128)[None, :]).astype(np.float32)
    return dict(c_masks=masks, c_ident=ident, c_iota=np.ascontiguousarray(iota), c_column=column, c_tri=tri,
                c_low=np.ascontiguousarray(tri.T))


class Mem:

    def __init__(self, nc, phase):
        self.nc, self.phase, self.ctx, self.sems = nc, phase, ExitStack(), []

    def __enter__(self):
        return self

    def __exit__(self, *a):
        if self.sems:
            self.nc.clear_and_free_semaphores(self.sems)
            self.nc.all_engine_barrier()
        self.ctx.close()

    def sb(self, name, shape, dt=F32):
        return self.ctx.enter_context(self.nc.sbuf_tensor(f"{self.phase}_{name}_sb", shape, dt))

    def ps(self, name, shape=(128, 512)):
        return self.ctx.enter_context(self.nc.psum_tensor(f"{self.phase}_{name}_ps", list(shape), F32))

    def sem(self, name):
        self.sems.append(self.nc.alloc_semaphore(f"{self.phase}_{name}"))
        return self.sems[-1]


def layer0_prepare(nc, mem, dr, col):
    W = CA * K
    si, di, th = mem.sb("si", [CP, W], I32), mem.sb("di", [CP, W], I32), mem.sb("th", [CP, W])
    fi, fj = mem.sb("fi", [CP, W]), mem.sb("fj", [CP, W])
    k1, k2, y1, y2 = (mem.sb(n, [CP, W]) for n in ("k1", "k2", "y1", "y2"))
    sn, cs, v1, v2 = (mem.sb(n, [CP, W]) for n in ("sn", "cs", "v1", "v2"))
    pk = mem.sb("pk", [CP, 4, CA, R])
    rh = mem.sb("rh", [CP, CA, R])
    ident = mem.sb("ident0", [128, 128])
    pst = [mem.ps(f"t0{q}", [128, 4, 128]) for q in range(2)]
    blank, landed, angles, sines = mem.sem("blank"), mem.sem("landed"), mem.sem("angles"), mem.sem("sines")
    packed, stored, turned, copied = mem.sem("packed"), mem.sem("stored"), mem.sem("turned"), mem.sem("copied")
    full, rest = CP - 1, E - (CP - 1) * W
    vec = nc.vector

    def steps(t):
        return t[:].rearrange("p (a k) -> p a k", k=K)

    with nc.Block() as block:
        @block.sync
        def _(sp):
            sp.wait_ge(blank, 3)
            for t, name in ((si, "src"), (di, "dst"), (th, "edge_weight")):
                sp.dma_start(t[0:full, :], dr[name][0:full * W].rearrange("(p w) -> p w", w=W)).then_inc(landed, 16)
                sp.dma_start(t[full:CP, 0:rest], dr[name][full * W:E].rearrange("(p w) -> p w", p=1)).then_inc(landed, 16)
            sp.dma_start(ident[:], dr["c_ident"]).then_inc(landed, 16)
            sp.wait_ge(packed, 1)
            sp.dma_start(dr["rho"][0:NCH, :].rearrange("(p a) r -> p (a r)", a=CA),
                         rh[:].rearrange("p a r -> p (a r)")).then_inc(stored, 16)
            sp.wait_ge(packed, 2)
            sp.dma_start(dr["rho"][NCH:NCOL, :], fi[0:NCOL - NCH, 0:R]).then_inc(stored, 16)
            sp.wait_ge(stored, 32)

        @block.vector
        def _(dve):
            vec.memset(si[:], 9999).then_inc(blank, 1)
            vec.memset(di[:], 9999).then_inc(blank, 1)
            vec.memset(th[:], 0.0).then_inc(blank, 1)
            dve.wait_ge(landed, 16 * 7)
            vec.tensor_copy(fi[:], si[:])
            vec.tensor_copy(fj[:], di[:])
            vec.tensor_scalar(k1[:], th[:], 1 / (2 * np.pi), ROUND, ALU.mult, ALU.add)
            vec.tensor_scalar(k2[:], th[:], 1 / (2 * np.pi), 0.25, ALU.mult, ALU.add)
            dve.drain()
            vec.tensor_scalar(k2[:], k2[:], ROUND, None, ALU.add)
            vec.tensor_scalar(k1[:], k1[:], -ROUND, None, ALU.add)
            dve.drain()
            vec.tensor_scalar(k2[:], k2[:], -ROUND, None, ALU.add)
            vec.scalar_tensor_tensor(y1[:], k1[:], -TWO_PI_HI, th[:], ALU.mult, ALU.add)
            dve.drain()
            vec.scalar_tensor_tensor(y2[:], k2[:], -TWO_PI_HI, th[:], ALU.mult, ALU.add)
            vec.scalar_tensor_tensor(v1[:], k1[:], -TWO_PI_LO, y1[:], ALU.mult, ALU.add)
            dve.drain()
            vec.tensor_scalar(y2[:], y2[:], float(np.pi / 2), None, ALU.add)
            vec.tensor_scalar(y1[:], v1[:], PI_SAFE, -PI_SAFE, ALU.min, ALU.max)
            dve.drain()
            vec.scalar_tensor_tensor(v2[:], k2[:], -TWO_PI_LO, y2[:], ALU.mult, ALU.add)
            dve.drain()
            vec.tensor_scalar(y2[:], v2[:], PI_SAFE, -PI_SAFE, ALU.min, ALU.max).then_inc(angles, 1)
            vec.tensor_scalar(rh[:, :, 0:K], steps(fi), 255.0, None, ALU.min)
            vec.tensor_scalar(rh[:, :, K:R], steps(fj), 255.0, None, ALU.min).then_inc(packed, 1)
            dve.drain()
            vec.tensor_tensor(v1[:], fi[:], fj[:], ALU.not_equal)
            vec.tensor_scalar(v2[:], fj[:], 256.0, None, ALU.is_lt)
            dve.drain()
            vec.scalar_tensor_tensor(k1[:], fi[:], 256.0, v1[:], ALU.is_lt, ALU.mult)
            vec.scalar_tensor_tensor(k2[:], fj[:], 1.0, v2[:], ALU.add, ALU.mult)
            dve.drain()
            vec.scalar_tensor_tensor(v1[:], fi[:], 1.0, k1[:], ALU.add, ALU.mult)
            for side in range(2):
                vec.tensor_scalar(pk[:, 2, :, side * K:side * K + K], steps(k2), -1.0, None, ALU.add)
            dve.drain()
            for side in range(2):
                vec.tensor_scalar(pk[:, 0, :, side * K:side * K + K], steps(v1), -1.0, None, ALU.add)
            vec.memset(fi[:], 0.0)
            vec.memset(col[:, :, NCH:NCOL], -1.0)
            dve.drain()
            for kind in (1, 3):
                vec.memset(col[:, kind, NCH:NCOL], 0.0)
            dve.drain()
            dve.nop().then_inc(packed, 1)
            dve.wait_ge(sines, 2)
            vec.tensor_scalar(pk[:, 1, :, 0:K], steps(cs), -1.0, None, ALU.add)
            vec.tensor_scalar(pk[:, 1, :, K:R], steps(sn), -1.0, None, ALU.mult)
            vec.tensor_copy(pk[:, 3, :, 0:K], steps(sn))
            vec.tensor_scalar(pk[:, 3, :, K:R], steps(cs), -1.0, None, ALU.add)
            dve.drain()
            dve.nop().then_inc(packed, 1)
            for a in range(CA):
                dve.wait_ge(turned, a + 1)
                vec.tensor_copy(col[:, :, a:NCH:CA], pst[a % 2][:, :, 0:CP]).then_inc(copied, 1)

        @block.scalar
        def _(act):
            act.wait_ge(angles, 1)
            nc.scalar.activation(sn[:], y1[:], ACT.Sin).then_inc(sines, 1)
            nc.scalar.activation(cs[:], y2[:], ACT.Sin).then_inc(sines, 1)

        @block.tensor
        def _(pe):
            pe.wait_ge(packed, 3)
            pe.wait_ge(landed, 16 * 7)
            for a in range(CA):
                if a >= 2:
                    pe.wait_ge(copied, a - 1)
                for kind in range(4):
                    last = nc.tensor.transpose(pst[a % 2][:, kind, 0:CP], pk[:, kind, a, :], ident[0:CP, 0:CP])
                last.then_inc(turned, 1)


def layer0_turn(nc, mem, dr, col, mt):
    masks = mem.sb("masks", [128, LV + 1, G, 128])
    ident = mem.sb("ident1", [128, 128])
    iota = mem.sb("iota1", [128, 512])
    column = mem.sb("column1", [128, 3])
    rb = [mem.sb(f"rb{q}", [128, G, R]) for q in range(2)]
    sc = mem.sb("sc", [128, 4, G])
    lta, ltb, lt = mem.sb("lta", [128, G, R]), mem.sb("ltb", [128, G, R]), mem.sb("lt", [128, G, R])
    wta, wtb = mem.sb("wta", [128, G, D]), mem.sb("wtb", [128, G, D])
    wt = [mem.sb(f"wt{q}", [128, G, D]) for q in range(2)]
    lm = [mem.sb(f"lm{q}", [128, LV, G, R]) for q in range(2)]
    st = [mem.sb(f"st{q}", [128, 2, G, R]) for q in range(2)]
    wx = [mem.sb(f"wx{q}", [128, G, D]) for q in range(2)]
    xt = [mem.sb(f"xt{q}", [128, G, R]) for q in range(2)]
    xx, ysb = mem.sb("xx", [128, G, R]), mem.sb("ysb", [128, G, R])
    rs = mem.sb("rs", [128, D])
    m = mem.sb("m", [128, 2, D])
    psy, psz, pszt, psr, psu = (mem.ps(n) for n in ("y", "z", "zt", "r", "u"))
    psw = mem.ps("w", [128, G, D])
    sems = {n: mem.sem(n) for n in (
        "consts", "levels", "rb_in0", "rb_in1", "rb_free", "lt_made", "lt_masked", "w_parts", "w_made", "st_made",
        "x_made", "y_made", "y_copied", "z_made", "x_grown", "wx_made", "wx_copied", "r_made", "r_copied", "u_made",
        "m_grown", "m_turned")}
    vec = nc.vector
    YS = LV

    with nc.Block() as block:
        @block.sync
        def _(sp):
            sp.dma_start(masks[:], dr["c_masks"]).then_inc(sems["consts"], 16)
            sp.dma_start(ident[:], dr["c_ident"]).then_inc(sems["consts"], 16)
            sp.dma_start(iota[:], dr["c_iota"]).then_inc(sems["consts"], 16)
            sp.dma_start(column[:], dr["c_column"]).then_inc(sems["consts"], 16)

            def load(group, q):
                rows = dr["rho"].rearrange("c r -> (c r)")[bass.ds(group * (G * R), G * R)]
                sp.dma_start(rb[q][:].rearrange("p g r -> p (g r)"), rows.partition_broadcast(128)).then_inc(
                    (sems["rb_in0"], sems["rb_in1"])[q], 16)
            load(0, 0)
            load(1, 1)
            with sp.Fori(0, STAGES // 2) as i:
                for u in range(2):
                    sp.wait_ge(sems["rb_free"], 2 * i + u + 1)
                    if u == 0:
                        load(2 * i + 2, 0)
                    else:
                        load(2 * i + 3, 1)
            sp.wait_ge(sems["rb_in0"], 16 * (STAGES // 2 + 1))
            sp.wait_ge(sems["rb_in1"], 16 * (STAGES // 2 + 1))

        @block.vector
        def _(dve):
            def build(group, q, landed, parts):
                if 0 in parts:
                    dve.wait_ge((sems["rb_in0"], sems["rb_in1"])[q], landed)
                    vec.tensor_copy(sc[:], col[:, :, bass.ds(group * G, G)])
                    dve.drain()
                    if not isinstance(group, int):
                        dve.wait_ge(sems["w_made"], group)
                for g in parts:
                    a = (sc[:, 0, g:g + 1], sc[:, 1, g:g + 1], ALU.is_equal, ALU.mult)
                    b = (sc[:, 2, g:g + 1], sc[:, 3, g:g + 1], ALU.is_equal, ALU.mult)
                    vec.tensor_scalar(lta[:, g, :], rb[q][:, g, :], *a)
                    vec.tensor_scalar(ltb[:, g, :], rb[q][:, g, :], *b)
                    vec.tensor_scalar(wta[:, g, :], iota[:, 0:D], *a)
                    last = vec.tensor_scalar(wtb[:, g, :], iota[:, 0:D], *b)
                if G - 1 in parts:
                    last.then_inc(sems["w_parts"], 1)
                    dve.drain()
                    if not isinstance(group, int):
                        dve.wait_ge(sems["lt_masked"], group)
                    vec.tensor_tensor(lt[:], lta[:], ltb[:], ALU.add).then_inc(sems["lt_made"], 1)

            def pick(q):
                vec.tensor_scalar(st[q][:, 0], rb[q][:], column[:, 0:1], None, ALU.is_equal)
                vec.tensor_scalar(st[q][:, 1], rb[q][:], column[:, 1:2], None, ALU.is_equal)
                dve.drain()
                dve.nop().then_inc(sems["st_made"], 1)
                dve.nop().then_inc(sems["rb_free"], 1)

            def grow_x(k, q, lv):
                dve.wait_ge(sems["z_made"], k * (LV - 1) + lv)
                last = vec.tensor_tensor(xx[:], psz[:].rearrange("p (g r) -> p g r", g=G), xx[:], ALU.add)
                if lv < LV - 1:
                    last = vec.tensor_tensor(xt[q][:], pszt[:].rearrange("p (g r) -> p g r", g=G), xt[q][:], ALU.add)
                last.then_inc(sems["x_grown"], 1)
                dve.drain()

            def grow_m(k, c):
                dve.wait_ge(sems["u_made"], k * G + c + 1)
                vec.tensor_tensor(m[:].rearrange("p h c -> p (h c)"), psu[:], m[:].rearrange("p h c -> p (h c)"),
                                  ALU.add).then_inc(sems["m_grown"], 1)
                dve.drain()

            dve.wait_ge(sems["consts"], 64)
            vec.memset(m[:], 0.0)
            for q in range(2):
                vec.memset(st[q][:], 0.0)
                vec.memset(wx[q][:], 0.0)
            dve.drain()
            for h in range(2):
                vec.tensor_copy(m[:, h, 128 * h:128 * h + 128], ident[:])
            dve.drain()
            dve.nop().then_inc(sems["m_grown"], 1)
            dve.nop().then_inc(sems["st_made"], 1)
            dve.nop().then_inc(sems["x_grown"], 1)
            build(0, 0, 16, range(G))
            with dve.Fori(0, STAGES // 2) as i:
                for u in range(2):
                    k = 2 * i + u
                    landed = i * 16 + 16 + 16 * u
                    grow_x(k, u, 1)
                    build(k + 1, 1 - u, landed, (0, 1))
                    grow_m(k, 0)
                    grow_x(k, u, 2)
                    build(k + 1, 1 - u, landed, (2, 3))
                    grow_m(k, 1)
                    grow_x(k, u, 3)
                    grow_m(k, 2)
                    grow_x(k, u, 4)
                    grow_m(k, 3)
                    pick(u)
                    grow_x(k, u, 5)
            for kh in range(2):
                dve.wait_ge(sems["m_turned"], kh + 1)
                vec.tensor_copy(mt[:, kh, :], (psy, psz)[kh][:, 0:D])

        @block.gpsimd
        def _(pool):
            tt = nc.gpsimd.tensor_tensor

            def mask(j, q):
                pool.wait_ge(sems["lt_made"], j + 1)
                pool.wait_ge(sems["wx_made"], j if not isinstance(j, int) else 1)
                tt(lm[q][:, 0], lt[:], masks[:, 0], ALU.mult).then_inc(sems["levels"], 1)
                for lv in range(1, LV):
                    last = tt(lm[q][:, lv], lt[:], masks[:, lv], ALU.mult)
                last.then_inc(sems["lt_masked"], 1)
                pool.wait_ge(sems["levels"], j + 1)
                tt(xt[q][:], lm[q][:, 0], masks[:, LV], ALU.add).then_inc(sems["x_made"], 1)
                pool.wait_ge(sems["w_parts"], j + 1)
                tt(wt[q][:], wta[:], wtb[:], ALU.add).then_inc(sems["w_made"], 1)

            pool.wait_ge(sems["consts"], 64)
            pool.nop().then_inc(sems["wx_made"], 1)
            mask(0, 0)
            with pool.Fori(0, STAGES // 2) as i:
                for u in range(2):
                    mask(2 * i + u + 1, 1 - u)

        @block.scalar
        def _(act):
            act.nop().then_inc(sems["y_copied"], 1)
            act.nop().then_inc(sems["wx_copied"], 1)

            def copy_y(k, n):
                act.wait_ge(sems["y_made"], k * LV + n + 1)
                dst = xx if n == 0 else ysb
                nc.scalar.copy(dst[:].rearrange("p g r -> p (g r)"), psy[:]).then_inc(sems["y_copied"], 1)

            def copy_r(k, c):
                act.wait_ge(sems["r_made"], k * G + c + 1)
                nc.scalar.copy(rs[:], psr[:, 0:D]).then_inc(sems["r_copied"], 1)

            with act.Fori(0, STAGES // 2) as i:
                for u in range(2):
                    k = 2 * i + u
                    copy_y(k, 0)
                    for lv in range(1, LV):
                        copy_y(k, lv)
                        if lv <= G:
                            copy_r(k, lv - 1)
                    act.wait_ge(sems["wx_made"], k + 2)
                    for h in range(2):
                        last = nc.scalar.copy(wx[u][:, 2 * h:2 * h + 2, :], psw[:, 2 * h:2 * h + 2, :])
                    last.then_inc(sems["wx_copied"], 1)

        @block.tensor
        def _(pe):
            mm = nc.tensor.matmul

            def start_x(k, q):
                pe.wait_ge(sems["x_made"], k + 1)
                pe.wait_ge(sems["y_copied"], k * LV + 1)
                for g in range(G):
                    last = nc.tensor.transpose(psy[:, g * R:g * R + R], xt[q][:, g, :], ident[:])
                last.then_inc(sems["y_made"], 1)

            def make_y(k, q, lv):
                if lv == 1:
                    pe.wait_ge(sems["lt_masked"], k + 1)
                else:
                    pe.wait_ge(sems["x_grown"], k * (LV - 1) + lv)
                pe.wait_ge(sems["y_copied"], k * LV + lv + 1)
                for g in range(G):
                    last = mm(psy[:, g * R:g * R + R], lm[q][:, lv, g, :], xx[:, g, :], start=True, stop=True)
                last.then_inc(sems["y_made"], 1)

            def make_z(k, q, lv):
                pe.wait_ge(sems["y_copied"], k * LV + lv + 2)
                if lv == 1:
                    pe.wait_ge(sems["x_grown"], k * (LV - 1) + 1)
                for g in range(G):
                    last = mm(psz[:, g * R:g * R + R], xt[q][:, g, :], ysb[:, g, :], start=True, stop=True)
                if lv < LV - 1:
                    for g in range(G):
                        last = mm(pszt[:, g * R:g * R + R], ysb[:, g, :], xt[q][:, g, :], start=True, stop=True)
                last.then_inc(sems["z_made"], 1)

            def make_r(k, q, c):
                pe.wait_ge(sems["m_grown"], k * G + c + 1)
                if c == 0:
                    pe.wait_ge(sems["st_made"], k + 1)
                for h in range(2):
                    last = mm(psr[:, 0:D], st[q][:, h, c, :], m[:, h, :], start=(h == 0), stop=(h == 1))
                last.then_inc(sems["r_made"], 1)

            def make_u(k, q, c):
                pe.wait_ge(sems["r_copied"], k * G + c + 1)
                if c == 0:
                    pe.wait_ge(sems["wx_copied"], k + 1)
                for h in range(2):
                    last = mm(psu[:, h * D:h * D + D], wx[q][:, c, 128 * h:128 * h + 128], rs[:], start=True, stop=True)
                last.then_inc(sems["u_made"], 1)

            pe.wait_ge(sems["consts"], 64)
            with pe.Fori(0, STAGES // 2) as i:
                for u in range(2):
                    k = 2 * i + u
                    start_x(k, u)
                    for lv in range(1, LV):
                        make_y(k, u, lv)
                        if lv <= G:
                            make_r(k, 1 - u, lv - 1)
                        make_z(k, u, lv)
                        if lv <= G:
                            make_u(k, 1 - u, lv - 1)
                    pe.wait_ge(sems["x_grown"], k * (LV - 1) + LV)
                    pe.wait_ge(sems["w_made"], k + 1)
                    pe.wait_ge(sems["wx_copied"], k + 1)
                    for g in range(G):
                        last = mm(psw[:, g, :], xx[:, g, :], wt[u][:, g, :], start=True, stop=True)
                    last.then_inc(sems["wx_made"], 1)
            pe.wait_ge(sems["m_grown"], STAGES * G + 1)
            pe.wait_ge(sems["y_copied"], STAGES * LV + 1)
            for kh in range(2):
                for h in range(2):
                    last = nc.tensor.transpose((psy, psz)[kh][:, 128 * h:128 * h + 128],
                                               m[:, h, 128 * kh:128 * kh + 128], ident[:])
                last.then_inc(sems["m_turned"], 1)


KS = ET + NT - 1
U = 8
HF = U // 2
NODE_SHIFT = 0.5 / P - 0.5


def edge_lists(mem):
    shape = [EC, NEC, P]
    k = {n: mem.sb("k_" + n, shape) for n in ("nf", "nb", "nfirst", "nlast")}
    k["member"] = mem.sb("k_member", [EC, NEC, KS])
    k["nk"] = mem.sb("k_nk", [1, KS], I32)
    k["etile"] = mem.sb("k_etile", [1, KS + U], I32)
    k["cut"] = mem.sb("k_cut", [P, KS])
    k["dloc"] = mem.sb("k_dloc", [P, KS + U])
    k["w"] = mem.sb("k_w", [P, KS + U, 4])
    for n in ("row_step", "src_step"):
        k[n] = mem.sb("k_" + n, [P, KS], I32)
    for n in ("row_tile", "drow_tile", "src_tile", "dst_tile"):
        k[n] = mem.sb("k_" + n, [P, ET], I32)
    k["ncont"] = mem.sb("k_ncont", [4, ET + 1])
    k["ntile"] = mem.sb("k_ntile", [4, 2, ET])
    return k


def edge_order(nc, mem, dr, keep):
    shape = [EC, NEC, P]
    ints = {n: mem.sb("i_" + n, shape, I32) for n in ("src", "dst", "edge_type_2")}
    f = {n: mem.sb("f_" + n, shape) for n in ints}
    ew, row, drow, d1, tmp, tmp2 = (mem.sb(n, shape) for n in ("ew", "row", "drow", "d1", "tmp", "tmp2"))
    cut, one = mem.sb("cut", shape), mem.sb("one", shape)
    lo, hi, cnt, start, end, gap = (mem.sb(n, [EC, NEC]) for n in ("lo", "hi", "cnt", "start", "end", "gap"))
    gapb, eid = mem.sb("gapb", shape), mem.sb("eid", shape)
    column = mem.sb("column", [128, 3])
    ident, tri, ones = mem.sb("ident2", [128, 128]), mem.sb("tri", [128, 128]), mem.sb("ones2", [128, 128])
    iota = mem.sb("iota2", [128, 512])
    at_or_past = mem.sb("atp", [EC, NEC, KS])
    nk, valid, steps = mem.sb("nk", [P, KS]), mem.sb("valid", [P, KS]), mem.sb("stepf", [P, KS])
    edges = mem.sb("edges", [4, 2, ET])
    cont, single, both = mem.sb("cont", [4, ET + 1]), mem.sb("single", [4, ET]), mem.sb("both", [4, 2, ET])
    ps_start, pst, pss = mem.ps("start"), [mem.ps(f"t2{q}") for q in range(2)], [mem.ps(f"s2{q}") for q in range(2)]
    landed, floats, counted, placed = (mem.sem("o_" + n) for n in ("landed", "floats", "counted", "placed"))
    stored, back, turned, copied = (mem.sem("o_" + n) for n in ("stored", "back", "turned", "copied"))
    member, summed, taken, cosine = (mem.sem("o_" + n) for n in ("member", "summed", "taken", "cosine"))
    vec = nc.vector

    def tiles(name):
        return dr[name].rearrange("(c p l) -> p c l", p=EC, l=P)

    with nc.Block() as block:
        @block.sync
        def _(sp):
            for n, t in list(ints.items()) + [("edge_weight", ew)]:
                sp.dma_start(t[:], tiles(n)).then_inc(landed, 16)
            sp.dma_start(ident[:], dr["c_ident"]).then_inc(landed, 16)
            sp.dma_start(tri[:], dr["c_tri"]).then_inc(landed, 16)
            sp.dma_start(iota[:], dr["c_iota"]).then_inc(landed, 16)
            sp.dma_start(column[:], dr["c_column"]).then_inc(landed, 16)
            sp.wait_ge(floats, 1)
            with nc.allow_non_contiguous_dma(reason="one word per edge tile"):
                sp.dma_start(dr["ends"][0].rearrange("(c p) -> p c", p=EC), f["dst"][:, :, 0]).then_inc(stored, 16)
                sp.dma_start(dr["ends"][1].rearrange("(c p) -> p c", p=EC), f["dst"][:, :, P - 1]).then_inc(stored, 16)
            sp.wait_ge(stored, 32)
            sp.dma_start(edges[:].rearrange("h s e -> h (s e)"),
                         dr["ends"].rearrange("s e -> (s e)").partition_broadcast(4)).then_inc(back, 16)

        @block.vector
        def _(dve):
            dve.wait_ge(landed, 16 * 8)
            vec.memset(keep["dloc"][:], -1.0)
            vec.memset(keep["w"][:], 0.0)
            for n in ints:
                vec.tensor_copy(f[n][:], ints[n][:])
            vec.memset(ones[:], 1.0)
            vec.memset(one[:], 1.0)
            vec.memset(keep["etile"][:], 0)
            dve.drain()
            dve.nop().then_inc(floats, 1)
            fd = f["dst"]
            vec.scalar_tensor_tensor(row[:], f["edge_type_2"][:], float(N), f["src"][:], ALU.mult, ALU.add)
            vec.scalar_tensor_tensor(drow[:], f["edge_type_2"][:], float(N), fd[:], ALU.mult, ALU.add)
            vec.tensor_scalar(d1[:], fd[:], 1.0, None, ALU.add)
            vec.tensor_scalar(lo[:], fd[:, :, 0], 1.0 / P, NODE_SHIFT, ALU.mult, ALU.add)
            vec.tensor_scalar(hi[:], fd[:, :, P - 1], 1.0 / P, NODE_SHIFT, ALU.mult, ALU.add)
            dve.drain()
            vec.tensor_scalar(lo[:], lo[:], ROUND, -ROUND, ALU.add, ALU.add)
            vec.tensor_scalar(hi[:], hi[:], ROUND, -ROUND, ALU.add, ALU.add)
            dve.drain()
            vec.tensor_tensor(cnt[:], hi[:], lo[:], ALU.subtract)
            dve.drain()
            vec.tensor_scalar(cnt[:], cnt[:], 1.0, None, ALU.add)
            dve.drain()
            dve.nop().then_inc(counted, 1)
            nf, nb, nfirst, nlast = (keep[n] for n in ("nf", "nb", "nfirst", "nlast"))
            for t in (nf, nb):
                vec.memset(t[:], 0.0)
            dve.drain()
            vec.tensor_tensor(nf[:, :, 1:P], fd[:, :, 1:P], fd[:, :, 0:P - 1], ALU.not_equal)
            vec.tensor_tensor(nb[:, :, 0:P - 1], fd[:, :, 1:P], fd[:, :, 0:P - 1], ALU.not_equal)
            for c in range(NEC):
                vec.tensor_scalar(nfirst[:, c], fd[:, c], fd[:, c, 0:1], -BIG, ALU.not_equal, ALU.mult)
                vec.tensor_scalar(nlast[:, c], fd[:, c], fd[:, c, P - 1:P], -BIG, ALU.not_equal, ALU.mult)
            dve.drain()
            vec.tensor_scalar(nf[:], nf[:], -BIG, None, ALU.mult)
            vec.tensor_scalar(nb[:], nb[:], -BIG, None, ALU.mult)
            vec.tensor_scalar(tmp[:], ew[:], 0.05, 0.25, ALU.mult, ALU.add)
            dve.drain()
            vec.tensor_scalar(tmp[:], tmp[:], ROUND, None, ALU.add)
            dve.drain()
            vec.tensor_scalar(tmp[:], tmp[:], -ROUND, None, ALU.add)
            vec.tensor_scalar(ew[:], ew[:], float(np.float32(np.pi / 10.0)), float(np.pi / 2), ALU.mult, ALU.add)
            dve.drain()
            vec.scalar_tensor_tensor(tmp2[:], tmp[:], -TWO_PI_HI, ew[:], ALU.mult, ALU.add)
            dve.drain()
            vec.scalar_tensor_tensor(ew[:], tmp[:], -TWO_PI_LO, tmp2[:], ALU.mult, ALU.add)
            dve.drain()
            vec.tensor_scalar(ew[:], ew[:], PI_SAFE, -PI_SAFE, ALU.min, ALU.max)
            dve.drain()
            dve.nop().then_inc(cosine, 1)
            dve.wait_ge(placed, 1)
            vec.tensor_copy(start[:], ps_start[0:EC, 0:NEC])
            dve.drain()
            vec.tensor_tensor(end[:], start[:], cnt[:], ALU.add)
            vec.tensor_tensor(gap[:], lo[:], start[:], ALU.subtract)
            dve.drain()
            for c in range(NEC):
                vec.tensor_scalar(at_or_past[:, c], iota[0:EC, 0:KS], start[:, c:c + 1], None, ALU.is_ge)
                vec.tensor_scalar(gapb[:, c], one[:, c], gap[:, c:c + 1], None, ALU.mult)
                vec.tensor_scalar(eid[:, c], one[:, c], column[0:EC, 0:1], float(EC * c - 1), ALU.add, ALU.add)
            dve.drain()
            for c in range(NEC):
                vec.scalar_tensor_tensor(keep["member"][:, c], iota[0:EC, 0:KS], end[:, c:c + 1], at_or_past[:, c],
                                         ALU.is_lt, ALU.mult)
            dve.wait_ge(cosine, 2)
            vec.tensor_scalar(cut[:], cut[:], 1.0, 0.5, ALU.add, ALU.mult)
            dve.drain()
            dve.nop().then_inc(member, 1)
            for n, dst in enumerate((nk, valid, steps, None, None, keep["cut"], None)):
                dve.wait_ge(summed, n + 1)
                ps = pss[n % 2][0:P, 0:KS]
                if n == 0:
                    vec.tensor_tensor(nk[:], ps, iota[0:P, 0:KS], ALU.add).then_inc(taken, 1)
                elif n == 1:
                    vec.tensor_copy(valid[:], ps).then_inc(taken, 1)
                    dve.drain()
                    vec.tensor_tensor(nk[:], nk[:], valid[:], ALU.mult)
                    dve.drain()
                    vec.tensor_copy(keep["nk"][:], nk[0:1, :])
                elif n == 2:
                    vec.scalar_tensor_tensor(steps[:], nk[:], -float(P), ps, ALU.mult, ALU.add).then_inc(taken, 1)
                    dve.drain()
                    vec.tensor_scalar(keep["dloc"][:, 0:KS], steps[:], -1.0, None, ALU.add)
                elif n == 6:
                    vec.tensor_copy(keep["etile"][0:1, 0:KS], ps[0:1, :]).then_inc(taken, 1)
                elif n in (3, 4):
                    vec.tensor_copy(keep[("row_step", "src_step")[n - 3]][:], ps).then_inc(taken, 1)
                else:
                    vec.tensor_copy(dst[:], ps).then_inc(taken, 1)
            for n in range(4 * NEC):
                dve.wait_ge(turned, n + 1)
                name = ("row_tile", "drow_tile", "src_tile", "dst_tile")[n // NEC]
                c = n % NEC
                vec.tensor_copy(keep[name][:, c * EC:c * EC + EC], pst[n % 2][0:P, 0:EC]).then_inc(copied, 1)
            dve.wait_ge(back, 16)
            vec.memset(cont[:], 0.0)
            vec.tensor_tensor(single[:], edges[:, 0, :], edges[:, 1, :], ALU.is_equal)
            dve.drain()
            vec.tensor_tensor(cont[:, 1:ET], edges[:, 1, 0:ET - 1], edges[:, 0, 1:ET], ALU.is_equal)
            dve.drain()
            for s in range(2):
                vec.tensor_tensor(both[:, s], single[:], cont[:, s:ET + s], ALU.mult)
            vec.tensor_scalar(keep["ncont"][:], cont[:], BIG, -BIG, ALU.mult, ALU.add)
            dve.drain()
            for s in range(2):
                vec.tensor_scalar(keep["ntile"][:, s], both[:, s], BIG, -BIG, ALU.mult, ALU.add)

        @block.scalar
        def _(act):
            act.wait_ge(cosine, 1)
            nc.scalar.activation(cut[:], ew[:], ACT.Sin).then_inc(cosine, 1)

        @block.tensor
        def _(pe):
            mm = nc.tensor.matmul
            pe.wait_ge(landed, 16 * 8)
            pe.wait_ge(counted, 1)
            for c in range(NEC):
                last = mm(ps_start[0:EC, c:c + 1], tri[0:EC, 0:EC], cnt[:, c:c + 1], start=True, stop=(c == 0))
                for b in range(c):
                    last = mm(ps_start[0:EC, c:c + 1], ones[0:EC, 0:EC], cnt[:, b:b + 1], start=False, stop=(b == c - 1))
            last.then_inc(placed, 1)
            pe.wait_ge(member, 1)
            for n, src in enumerate((gapb, one, d1, row, f["src"], cut, eid)):
                if n >= 2:
                    pe.wait_ge(taken, n - 1)
                for c in range(NEC):
                    last = mm(pss[n % 2][0:P, 0:KS], src[:, c, :], keep["member"][:, c, :], start=(c == 0), stop=(c == NEC - 1))
                last.then_inc(summed, 1)
            for n in range(4 * NEC):
                src = (row, drow, f["src"], f["dst"])[n // NEC]
                if n >= 2:
                    pe.wait_ge(copied, n - 1)
                nc.tensor.transpose(pst[n % 2][0:P, 0:EC], src[:, n % NEC, :], ident[0:EC, 0:EC]).then_inc(turned, 1)


def attention_weights(nc, mem, dr, keep, heads, layer):
    H = heads
    kt, qt = dr["kt"] if H == 4 else dr["kt1"], dr["qt"] if H == 4 else dr["qt1"]
    idx = mem.sb("idx", [P, 2, U], I32)
    gk, gq = mem.sb("gk", [P, U, H]), mem.sb("gq", [P, U, H])
    raw = mem.sb("raw", [P, U, H])
    al = mem.sb("al", [P, ET, H])
    a, fw, amax, wt = (mem.sb(n, [EC, NEC, H, P]) for n in ("a", "fw", "amax", "wt"))
    ident = mem.sb("ident3", [128, 128])
    ends = mem.sb("ends", [4, 2, ET])
    state = mem.sb("state", [4, 2, ET])
    carry = mem.sb("carry", [4, 2, ET])
    carried = mem.sb("carried", [EC, 2, NEC, H])
    pst = [mem.ps(f"t3{q}") for q in range(2)]
    psw = [mem.ps(f"w3{q}") for q in range(2)]
    nm = lambda n: mem.sem(f"a{layer}_{n}")
    nopped = nm("nopped")
    listed, k_in, q_in, used = nm("listed"), [nm("k0"), nm("k1")], [nm("q0"), nm("q1")], [nm("u0"), nm("u1")]
    scored, turned, copied, landed = nm("scored"), nm("turned"), nm("copied"), nm("landed")
    summary, back, ready, exped, summed, taken = (nm(n) for n in ("summary", "back", "ready", "exped", "summed", "taken"))
    vec = nc.vector

    with nc.Block() as block:
        @block.gpsimd
        def _(pool):
            pool.wait_ge(landed, 16)
            with pool.Fori(0, ET // U) as i:
                for q in range(2):
                    half = slice(HF * q, HF * q + HF)
                    pool.wait_ge(used[q], i + 1)
                    for n, name in enumerate(("row_tile", "drow_tile")):
                        last = nc.gpsimd.tensor_copy(idx[:, n, half], keep[name][:, bass.ds(i * U + HF * q, HF)])
                        last.then_inc(listed, 1)
                    pool.wait_ge(listed, 4 * i + 2 * q + 2)
                    pool.nop().then_inc(nopped, 1)
                    for j in range(HF * q, HF * q + HF):
                        for n, (g, tab, sem) in enumerate(((gk, kt, k_in[q]), (gq, qt, q_in[q]))):
                            nc.gpsimd.indirect_dma_start(
                                out=g[:, j, :], out_offset=None, in_=tab,
                                in_offset=bass.IndirectOffsetOnAxis(ap=idx[:, n, j:j + 1], axis=0)).then_inc(sem, 16)

        @block.vector
        def _(dve):
            for q in range(2):
                dve.nop().then_inc(used[q], 1)
            with dve.Fori(0, ET // U) as i:
                for q in range(2):
                    half = slice(HF * q, HF * q + HF)
                    dve.wait_ge(k_in[q], (i + 1) * (16 * HF))
                    dve.wait_ge(q_in[q], (i + 1) * (16 * HF))
                    vec.tensor_tensor(raw[:, half], gk[:, half], gq[:, half], ALU.add).then_inc(used[q], 1)
                    dve.drain()
                    vec.scalar_tensor_tensor(al[:, bass.ds(i * U + HF * q, HF), :], raw[:, half], 0.2, raw[:, half],
                                             ALU.mult, ALU.max)
                    dve.drain()
            dve.nop().then_inc(scored, 1)
            for c in range(NEC):
                dve.wait_ge(turned, c + 1)
                vec.tensor_copy(a[:, c].rearrange("p h l -> p (h l)"), pst[c % 2][0:EC, 0:H * P]).then_inc(copied, 1)
            dve.drain()
            for c in range(NEC):
                for h in range(H):
                    vec.tensor_tensor_scan(fw[:, c, h], keep["nf"][:, c], a[:, c, h], -BIG, ALU.add, ALU.max)
            dve.drain()
            for c in range(NEC):
                for h in range(H):
                    vec.tensor_tensor_scan(amax[:, c, h, ::-1], keep["nb"][:, c, ::-1], fw[:, c, h, ::-1], -BIG,
                                           ALU.add, ALU.max)
            dve.drain()
            dve.nop().then_inc(summary, 1)
            dve.wait_ge(back, 16 * 2)
            vec.tensor_tensor_scan(state[0:H, 0], keep["ntile"][0:H, 0], ends[0:H, 1], -BIG, ALU.add, ALU.max)
            vec.tensor_tensor_scan(state[0:H, 1, ::-1], keep["ntile"][0:H, 1, ::-1], ends[0:H, 0, ::-1], -BIG,
                                   ALU.add, ALU.max)
            vec.memset(carry[:], -BIG)
            dve.drain()
            vec.tensor_tensor(carry[0:H, 0, 1:ET], state[0:H, 0, 0:ET - 1], keep["ncont"][0:H, 1:ET], ALU.add)
            vec.tensor_tensor(carry[0:H, 1, 0:ET - 1], state[0:H, 1, 1:ET], keep["ncont"][0:H, 1:ET], ALU.add)
            dve.drain()
            dve.nop().then_inc(summary, 1)
            dve.wait_ge(back, 16 * (2 + 2 * NEC))
            for s, mask in ((0, "nfirst"), (1, "nlast")):
                for c in range(NEC):
                    for h in range(H):
                        vec.scalar_tensor_tensor(amax[:, c, h], keep[mask][:, c], carried[:, s, c, h:h + 1],
                                                 amax[:, c, h], ALU.add, ALU.max)
                dve.drain()
            vec.tensor_tensor(fw[:], a[:], amax[:], ALU.subtract).then_inc(ready, 1)
            for h in range(H):
                dve.wait_ge(summed, h + 1)
                vec.tensor_copy(keep["w"][:, 0:KS, h], psw[h % 2][0:P, 0:KS]).then_inc(taken, 1)

        @block.sync
        def _(sp):
            sp.dma_start(ident[:], dr["c_ident"]).then_inc(landed, 16)
            sp.wait_ge(summary, 1)
            cd = dr["carry"]
            with nc.allow_non_contiguous_dma(reason="one word per edge tile and head"):
                for s, lane in ((0, 0), (1, P - 1)):
                    for c in range(NEC):
                        sp.dma_start(cd[s, 0:H, c * EC:c * EC + EC].rearrange("h p -> p h"), amax[:, c, :, lane]).then_inc(
                            landed, 16)
                sp.wait_ge(landed, 16 * (1 + 2 * NEC))
                for s in range(2):
                    sp.dma_start(ends[0:H, s], cd[s, 0:H]).then_inc(back, 16)
                sp.wait_ge(summary, 2)
                for s in range(2):
                    sp.dma_start(cd[2 + s, 0:H], carry[0:H, s]).then_inc(landed, 16)
                sp.wait_ge(landed, 16 * (3 + 2 * NEC))
                for s in range(2):
                    for c in range(NEC):
                        sp.dma_start(carried[:, s, c, :], cd[2 + s, 0:H, c * EC:c * EC + EC].rearrange("h p -> p h")).then_inc(
                            back, 16)

        @block.scalar
        def _(act):
            act.wait_ge(ready, 1)
            nc.scalar.activation(wt[:], fw[:], ACT.Exp).then_inc(exped, 1)

        @block.tensor
        def _(pe):
            pe.wait_ge(landed, 16)
            pe.wait_ge(scored, 1)
            for c in range(NEC):
                if c >= 2:
                    pe.wait_ge(copied, c - 1)
                for h in range(H):
                    last = nc.tensor.transpose(pst[c % 2][0:EC, h * P:h * P + P], al[:, c * EC:c * EC + EC, h],
                                               ident[0:P, 0:P])
                last.then_inc(turned, 1)
            pe.wait_ge(exped, 1)
            for h in range(H):
                if h >= 2:
                    pe.wait_ge(taken, h - 1)
                for c in range(NEC):
                    last = nc.tensor.matmul(psw[h % 2][0:P, 0:KS], wt[:, c, h, :], keep["member"][:, c, :],
                                            start=(c == 0), stop=(c == NEC - 1))
                last.then_inc(summed, 1)


def attention_sum(nc, mem, dr, keep, agg, table, heads, width, layer):
    H, F = heads, width
    V = 2 * 2
    idx = mem.sb("idx", [P, U], I32)
    gx, ms = mem.sb("gx", [P, U, F]), mem.sb("ms", [P, HF, F])
    wl, dl = mem.sb("wl", [P, U, H]), mem.sb("dl", [P, U])
    sel = mem.sb("sel", [P, U, P])
    iota = mem.sb("iota4", [128, 512])
    psa = [mem.ps(f"a4{q}") for q in range(HF)]
    psd = [mem.ps(f"d4{q}") for q in range(HF)]
    nm = lambda n: mem.sem(f"b{layer}_{n}")
    listed, nopped, x_in, used = nm("listed"), nm("nopped"), [nm("x0"), nm("x1")], [nm("u0"), nm("u1")]
    landed, picked, weighed, summed, added = (nm(n) for n in ("landed", "picked", "weighed", "summed", "added"))
    vec = nc.vector

    with nc.Block() as block:
        @block.sync
        def _(sp):
            sp.dma_start(iota[:], dr["c_iota"]).then_inc(landed, 16)

        @block.gpsimd
        def _(pool):
            pool.wait_ge(landed, 16)
            with pool.Fori(0, KS // U) as i:
                for q in range(2):
                    pool.wait_ge(used[q], i + 1)
                    pool.nop().then_inc(nopped, 1)
                    nc.gpsimd.tensor_copy(idx[:, HF * q:HF * q + HF],
                                          keep["row_step"][:, bass.ds(i * U + HF * q, HF)]).then_inc(listed, 1)
                    pool.wait_ge(listed, 2 * i + q + 1)
                    pool.nop().then_inc(nopped, 1)
                    for j in range(HF * q, HF * q + HF):
                        nc.gpsimd.indirect_dma_start(
                            out=gx[:, j, :], out_offset=None, in_=table,
                            in_offset=bass.IndirectOffsetOnAxis(ap=idx[:, j:j + 1], axis=0)).then_inc(x_in[q], 16)

        @block.scalar
        def _(act):
            for q in range(2):
                act.nop().then_inc(used[q], 1)
            with act.Fori(0, KS // U) as i:
                for q in range(2):
                    act.wait_ge(x_in[q], (i + 1) * (16 * HF))
                    act.wait_ge(picked, i * 2 + q + 1)
                    for j in range(HF):
                        act.wait_ge(summed, i * U + q * HF + j + 1)
                        for h in range(H):
                            w = F // H
                            last = nc.scalar.activation(ms[:, j, h * w:h * w + w], gx[:, q * HF + j, h * w:h * w + w],
                                                        ACT.Copy, scale=wl[:, q * HF + j, h:h + 1])
                        last.then_inc(weighed, 1)
                    act.drain()
                    act.nop().then_inc(used[q], 1)

        @block.tensor
        def _(pe):
            for j in range(HF):
                pe.nop().then_inc(summed, 1)
            with pe.Fori(0, KS // U) as i:
                for q in range(2):
                    for j in range(HF):
                        n = i * U + q * HF + j
                        if j == 0:
                            pe.wait_ge(picked, i * 2 + q + 1)
                        pe.wait_ge(added, n + 1)
                        nc.tensor.matmul(psd[j][0:P, 0:H], sel[:, q * HF + j, :], wl[:, q * HF + j, :], start=True, stop=True)
                        pe.wait_ge(weighed, n + 1)
                        nc.tensor.matmul(psa[j][0:P, 0:F], sel[:, q * HF + j, :], ms[:, j, :], start=True,
                                         stop=True).then_inc(summed, 1)

        @block.vector
        def _(dve):
            for t in range(0, NT, 5):
                vec.memset(agg[:, t:t + 5, 0:F + H], 0.0)
            for j in range(HF):
                dve.nop().then_inc(added, 1)
            dve.wait_ge(landed, 16)
            dve.drain()

            def pick(first, q):
                half = slice(q * HF, q * HF + HF)
                vec.tensor_copy(wl[:, half, :], keep["w"][:, bass.ds(first, HF), 0:H])
                vec.tensor_copy(dl[:, half], keep["dloc"][:, bass.ds(first, HF)])
                dve.drain()
                for j in range(HF):
                    vec.tensor_scalar(sel[:, q * HF + j, :], iota[0:P, 0:P], dl[:, q * HF + j:q * HF + j + 1], None,
                                      ALU.is_equal)
                dve.drain()
                dve.nop().then_inc(picked, 1)

            def add(n, j):
                tile = vec.value_load(keep["nk"][0:1, bass.ds(n, 1)], min_val=0, max_val=NT - 1)
                dve.wait_ge(summed, n + HF + 1)
                here = agg[:, bass.ds(tile, 1), 0:F].rearrange("p o f -> p (o f)")
                vec.tensor_tensor(here, psa[j][0:P, 0:F], here, ALU.add)
                here = agg[:, bass.ds(tile, 1), F:F + H].rearrange("p o f -> p (o f)")
                vec.tensor_tensor(here, psd[j][0:P, 0:H], here, ALU.add)
                dve.drain()
                dve.nop().then_inc(added, 1)

            pick(0, 0)
            with dve.Fori(0, KS // U) as i:
                pick(i * U + HF, 1)
                for j in range(HF):
                    add(i * U + j, j)
                dve.wait_ge(used[0], i + 2)
                pick(i * U + U, 0)
                for j in range(HF):
                    add(i * U + HF + j, j)
                dve.wait_ge(used[1], i + 2)


def rows(ap, t, base=0):
    return ap[bass.ds(t * P + base, P), :]


def norm_buffers(mem):
    return dict(stats=mem.sb("stats", [P, 6]), mv=mem.sb("mv", [P, 2]), var=mem.sb("var", [P, 1]),
                sd=mem.sb("sd", [P, 1]), rsd=mem.sb("rsd", [P, 1]), var_made=mem.sem("var_made"),
                sd_made=mem.sem("sd_made"))


def norm_statistics(nc, dve, nl, x):
    vec = nc.vector
    dve.drain()
    vec.bn_stats(nl["stats"][:], x)
    dve.drain()
    vec.bn_aggr(nl["mv"][:], nl["stats"][:])
    dve.drain()
    vec.tensor_scalar(nl["var"][:], nl["mv"][:, 1:2], 1e-5, None, ALU.add).then_inc(nl["var_made"], 1)


def norm_root(nc, act, nl, t):
    act.wait_ge(nl["var_made"], t + 1)
    nc.scalar.activation(nl["sd"][:], nl["var"][:], ACT.Sqrt).then_inc(nl["sd_made"], 1)


def norm_scale(nc, dve, nl, t, out, x):
    vec = nc.vector
    dve.wait_ge(nl["sd_made"], t + 1)
    vec.reciprocal(nl["rsd"][:], nl["sd"][:])
    dve.drain()
    return vec.tensor_scalar(out, x, nl["mv"][:, 0:1], nl["rsd"][:, 0:1], ALU.subtract, ALU.mult)


def projection_buffers(mem, blocks, width, heads):
    outs = width // 128
    return dict(blocks=blocks, width=width, heads=heads, outs=outs,
                w=mem.sb("w", [128, blocks, 2, width]), wt=mem.sb("wt", [128, outs, 2, blocks * 128]),
                qk=mem.sb("qk", [128, outs, 2, heads]), wk=mem.sb("wk", [128, blocks, 2, 2 * heads]),
                psx=[mem.ps(f"x{r}") for r in range(2)], psk=mem.ps("k"))


PROJECTION_LOADS, PROJECTION_STORES = 6, 6


def projection_load(nc, sp, pr, w, wt, k, q, sem):
    with nc.allow_non_contiguous_dma(reason="short rows of the key and query vectors"):
        sp.dma_start(pr["qk"][:, :, 0, :], k.rearrange("(o p) h -> p o h", p=128)).then_inc(sem, 16)
        sp.dma_start(pr["qk"][:, :, 1, :], q.rearrange("(o p) h -> p o h", p=128)).then_inc(sem, 16)
    for r in range(2):
        sp.dma_start(pr["w"][:, :, r, :], w[r].rearrange("(b p) o -> p b o", p=128)).then_inc(sem, 16)
        sp.dma_start(pr["wt"][:, :, r, :], wt[r].rearrange("(o p) b -> p o b", p=128)).then_inc(sem, 16)


def score_weights(nc, pr):
    heads, outs = pr["heads"], pr["outs"]
    for b in range(pr["blocks"]):
        for r in range(2):
            at = (b * 2 + r) * 2 * heads
            for o in range(outs):
                last = nc.tensor.matmul(pr["psk"][:, at:at + 2 * heads], pr["wt"][:, o, r, b * 128:b * 128 + 128],
                                        pr["qk"][:, o].rearrange("p s h -> p (s h)"), start=(o == 0),
                                        stop=(o == outs - 1))
    return last


def take_score_weights(nc, pr):
    n = pr["blocks"] * 2 * 2 * pr["heads"]
    return nc.vector.tensor_copy(pr["wk"][:].rearrange("p b r s -> p (b r s)"), pr["psk"][:, 0:n])


def project(nc, pr, blocks):
    mm, S = nc.tensor.matmul, 2 * pr["heads"]
    for r in range(2):
        for n, (x, b) in enumerate(blocks):
            mm(pr["psx"][r][0:P, 0:pr["width"]], x, pr["w"][:, b, r, :], start=(n == 0), stop=(n == len(blocks) - 1))
    for r in range(2):
        for n, (x, b) in enumerate(blocks):
            last = mm(pr["psk"][0:P, r * S:r * S + S], x, pr["wk"][:, b, r, :], start=(n == 0),
                      stop=(n == len(blocks) - 1))
    return last


def projection_store(sp, dr, pr, t, xsb, ksb, sem):
    H = pr["heads"]
    xw, kt, qt = (dr["xw"], dr["kt"], dr["qt"]) if H == 4 else (dr["xw1"], dr["kt1"], dr["qt1"])
    for r in range(2):
        sp.dma_start(rows(xw, t, r * N), xsb[:, r, :]).then_inc(sem, 16)
        sp.dma_start(rows(kt, t, r * N), ksb[:, r, 0:H]).then_inc(sem, 16)
        sp.dma_start(rows(qt, t, r * N), ksb[:, r, H:2 * H]).then_inc(sem, 16)


def nodes_gate(nc, mem, dr, mt):
    pr = projection_buffers(mem, 6, 512, 4)
    nl = norm_buffers(mem)
    xt, xn = mem.sb("xt", [128, 2, P]), mem.sb("xn", [P, NT, D])
    gw1, gw2 = mem.sb("gw1", [128, 4, D]), mem.sb("gw2", [128, 2, D])
    gb1, gb2, gc, qc = (mem.sb(n, [128, 2]) for n in ("gb1", "gb2", "gc", "qc"))
    qb, ones = mem.sb("qb", [128, 2, P]), mem.sb("ones", [128, P])
    xb, kb = mem.sb("xb", [P, 2, 512]), mem.sb("kb", [P, 2, 8])
    ident = mem.sb("ident", [128, 128])
    r1, x1, x0 = mem.sb("r1", [P, D]), mem.sb("x1", [P, D]), mem.sb("x0", [P, D])
    x1t, ght, gt, x0t = (mem.sb(n, [128, 2, P]) for n in ("x1t", "ght", "gt", "x0t"))
    xsb, ksb = mem.sb("xsb", [P, 2, 512]), mem.sb("ksb", [P, 2, 8])
    psy, pst, psg, psh, ps0 = (mem.ps(n) for n in ("y", "t", "g", "h", "0"))
    (landed, ones_made, spread, gate_c, scaled, bias_made, ready, y_made, x1_made, x1_stored, t_made, x1t_made, gh_made,
     ght_made, g_made, gt_made, x0t_made, x0_turned, x0_made, projected, table_made, done1, done2, table_stored) = (
        mem.sem(n) for n in (
            "landed", "ones_made", "spread", "gate_c", "scaled", "bias_made", "ready", "y_made", "x1_made", "x1_stored",
            "t_made", "x1t_made", "gh_made", "ght_made", "g_made", "gt_made", "x0t_made", "x0_turned", "x0_made",
            "projected", "table_made", "done1", "done2", "table_stored"))
    xt_in = mem.sem("xt_in")
    vec, mm = nc.vector, nc.tensor.matmul
    LOADS = PROJECTION_LOADS + 7

    with nc.Block() as block:
        @block.sync
        def _(sp):
            with nc.allow_non_contiguous_dma(reason="short vectors"):
                sp.dma_start(qc[:], dr["L1_gnn_query"][0].rearrange("(b p) -> p b", p=128)).then_inc(landed, 16)
                sp.dma_start(gb1[:], dr["L1_gnn_gate_b1"].rearrange("(b p) -> p b", p=128)).then_inc(landed, 16)
                sp.dma_start(gb2[:], dr["L1_gnn_gate_b2"].rearrange("(b p) -> p b", p=128)).then_inc(landed, 16)
            sp.dma_start(gw1[:], dr["L1_gnn_gate_w1"].rearrange("(b p) o -> p b o", p=128)).then_inc(landed, 16)
            sp.dma_start(gw2[:], dr["L1_gnn_gate_w2"].rearrange("(b p) o -> p b o", p=128)).then_inc(landed, 16)
            sp.dma_start(ident[:], dr["c_ident"]).then_inc(landed, 16)
            projection_load(nc, sp, pr, dr["L1_gnn_W1"], dr["W1_t"], dr["L1_gnn_k1"], dr["L1_gnn_q1"], landed)
            sp.dma_start(xn[:], dr["x"].rearrange("(t p) c -> p t c", p=P)).then_inc(landed, 16)
            sp.nop().then_inc(x1_stored, 1)
            sp.nop().then_inc(table_stored, 1)
            sp.dma_start(xt[:], dr["x_t2"][:, 0:P].rearrange("(b p) n -> p b n", p=128)).then_inc(xt_in, 16)
            with sp.Fori(0, NT) as t:
                sp.wait_ge(x1_made, t + 1)
                sp.dma_start(xt[:], dr["x_t2"][:, bass.ds(t * P + P, P)].rearrange("(b p) n -> p b n", p=128)).then_inc(xt_in, 16)
                sp.dma_start(rows(dr["x1"], t), x1[:]).then_inc(done1, 16)
                sp.wait_ge(done1, t * 16 + 16)
                sp.nop().then_inc(x1_stored, 1)
                sp.wait_ge(x0_made, t + 1)
                sp.wait_ge(table_made, 2 * t + 2)
                sp.dma_start(rows(dr["x0"], t), x0[:]).then_inc(done2, 16)
                projection_store(sp, dr, pr, t, xsb, ksb, done2)
                sp.wait_ge(done2, t * (16 * 7) + 16 * 7)
                sp.nop().then_inc(table_stored, 1)
            sp.wait_ge(xt_in, 16 * (NT + 1))

        @block.tensor
        def _(pe):
            pe.wait_ge(landed, 16 * LOADS)
            for o in range(2):
                for b in range(2):
                    last = mm(psg[:, o:o + 1], gw1[:, 2 + b, 128 * o:128 * o + 128], qc[:, b:b + 1], start=(b == 0), stop=(b == 1))
            last.then_inc(gate_c, 1)
            score_weights(nc, pr).then_inc(gate_c, 1)
            pe.wait_ge(spread, 1)
            pe.wait_ge(scaled, 1)
            for r in range(2):
                for b in range(2):
                    mm(pr["psx"][r][0:P, :], qb[:, b, :], pr["w"][:, 2 + b, r, :], start=(b == 0), stop=(b == 1))
            for r in range(2):
                for b in range(2):
                    last = mm(psh[0:P, 8 * r:8 * r + 8], qb[:, b, :], pr["wk"][:, 2 + b, r, :], start=(b == 0), stop=(b == 1))
            last.then_inc(bias_made, 1)
            pe.wait_ge(ready, 1)
            with pe.Fori(0, NT) as t:
                pe.wait_ge(xt_in, t * 16 + 16)
                for b in range(2):
                    last = mm(psy[0:P, 0:D], xt[:, b, :], mt[:, b, :], start=(b == 0), stop=(b == 1))
                last.then_inc(y_made, 1)
                pe.wait_ge(x1_made, t + 1)
                for b in range(2):
                    last = nc.tensor.transpose(pst[:, b * P:b * P + P], x1[:, 128 * b:128 * b + 128], ident[0:P, 0:P])
                last.then_inc(t_made, 1)
                pe.wait_ge(x1t_made, t + 1)
                for o in range(2):
                    for b in range(2):
                        last = mm(psg[:, o * P:o * P + P], gw1[:, b, 128 * o:128 * o + 128], x1t[:, b, :], start=(b == 0), stop=(b == 1))
                last.then_inc(gh_made, 1)
                pe.wait_ge(ght_made, t + 1)
                for o in range(2):
                    for b in range(2):
                        last = mm(psh[:, o * P:o * P + P], gw2[:, b, 128 * o:128 * o + 128], ght[:, b, :], start=(b == 0), stop=(b == 1))
                last.then_inc(g_made, 1)
                pe.wait_ge(x0t_made, t + 1)
                for b in range(2):
                    last = nc.tensor.transpose(ps0[0:P, 128 * b:128 * b + 128], x0t[:, b, :], ident[:])
                last.then_inc(x0_turned, 1)
                pe.wait_ge(table_made, 2 * t + 1)
                project(nc, pr, [(x0t[:, 0, :], 0), (x0t[:, 1, :], 1), (x1t[:, 0, :], 4), (x1t[:, 1, :], 5)]).then_inc(projected, 1)

        @block.scalar
        def _(act):
            with act.Fori(0, NT) as t:
                norm_root(nc, act, nl, t)
                act.wait_ge(gh_made, t + 1)
                for o in range(2):
                    last = nc.scalar.activation(ght[:, o, :], psg[:, o * P:o * P + P], ACT.Relu, bias=gc[:, o:o + 1])
                last.then_inc(ght_made, 1)
                act.wait_ge(g_made, t + 1)
                for o in range(2):
                    last = nc.scalar.activation(gt[:, o, :], psh[:, o * P:o * P + P], ACT.Sigmoid, bias=gb2[:, o:o + 1])
                last.then_inc(gt_made, 1)
                act.wait_ge(table_stored, t + 1)
                act.wait_ge(x0_turned, t + 1)
                nc.scalar.copy(x0[:], ps0[0:P, 0:D]).then_inc(x0_made, 1)

        @block.vector
        def _(dve):
            vec.memset(ones[:], 1.0)
            dve.wait_ge(landed, 16 * LOADS)
            dve.drain()
            for b in range(2):
                vec.tensor_scalar(qb[:, b, :], ones[:], qc[:, b:b + 1], None, ALU.mult)
            dve.drain()
            dve.nop().then_inc(spread, 1)
            dve.wait_ge(gate_c, 1)
            vec.tensor_tensor(gc[:], psg[:, 0:2], gb1[:], ALU.add)
            dve.wait_ge(gate_c, 2)
            take_score_weights(nc, pr)
            dve.drain()
            for b in range(2):
                vec.tensor_scalar(pr["w"][:, 4 + b], pr["w"][:, 4 + b], qc[:, b:b + 1], None, ALU.mult)
                vec.tensor_scalar(pr["wk"][:, 4 + b], pr["wk"][:, 4 + b], qc[:, b:b + 1], None, ALU.mult)
            dve.drain()
            dve.nop().then_inc(scaled, 1)
            dve.wait_ge(bias_made, 1)
            for r in range(2):
                vec.tensor_copy(xb[:, r, :], pr["psx"][r][0:P, :])
            vec.tensor_copy(kb[:].rearrange("p r s -> p (r s)"), psh[0:P, 0:16])
            dve.drain()
            dve.nop().then_inc(ready, 1)
            dve.nop().then_inc(table_made, 1)
            with dve.Fori(0, NT) as t:
                dve.wait_ge(y_made, t + 1)
                dve.nop().then_inc(ready, 1)
                vec.tensor_tensor(r1[:], psy[0:P, 0:D], xn[:, bass.ds(t, 1), :].rearrange("p o c -> p (o c)"), ALU.add)
                norm_statistics(nc, dve, nl, r1[:])
                dve.wait_ge(x1_stored, t + 1)
                norm_scale(nc, dve, nl, t, x1[:], r1[:]).then_inc(x1_made, 1)
                dve.wait_ge(t_made, t + 1)
                vec.tensor_copy(x1t[:].rearrange("p b n -> p (b n)"), pst[:, 0:2 * P]).then_inc(x1t_made, 1)
                dve.drain()
                dve.wait_ge(gt_made, t + 1)
                vec.tensor_tensor(x0t[:], x1t[:], gt[:], ALU.mult).then_inc(x0t_made, 1)
                dve.wait_ge(projected, t + 1)
                dve.wait_ge(table_stored, t + 1)
                for r in range(2):
                    vec.tensor_tensor(xsb[:, r, :], pr["psx"][r][0:P, :], xb[:, r, :], ALU.add)
                vec.tensor_tensor(ksb[:].rearrange("p r s -> p (r s)"), pr["psk"][0:P, 0:16], kb[:].rearrange("p r s -> p (r s)"),
                                  ALU.add)
                dve.drain()
                dve.nop().then_inc(table_made, 1)
                dve.nop().then_inc(table_made, 1)


def normalized_heads(nc, dve, out, agg, t, bias, den, width, heads):
    vec, w = nc.vector, width // heads
    vec.tensor_scalar(den[:, 0:heads], agg[:, bass.ds(t, 1), width:width + heads].rearrange("p o h -> p (o h)"), 1e-16,
                      None, ALU.add)
    dve.drain()
    vec.reciprocal(den[:, heads:2 * heads], den[:, 0:heads])
    dve.drain()
    for h in range(heads):
        vec.scalar_tensor_tensor(out[:, h * w:h * w + w], agg[:, bass.ds(t, 1), h * w:h * w + w].rearrange("p o c -> p (o c)"),
                                 den[:, heads + h:heads + h + 1], bias[:, h * w:h * w + w], ALU.mult, ALU.add)
    dve.drain()


def nodes_attend(nc, mem, dr, agg, kept, bias, names, width, heads, first):
    F, H = width, heads
    pr = projection_buffers(mem, 4, F, H)
    den, raw, hc = mem.sb("den", [P, 8]), mem.sb("raw", [P, 512]), mem.sb("hc", [P, 512])
    ht = mem.sb("ht", [128, 4, P])
    bb = mem.sb("bb", [P, 512])
    ident = mem.sb("ident", [128, 128])
    xsb, ksb = mem.sb("xsb", [P, 2, F]), mem.sb("ksb", [P, 2, 2 * H])
    pst = mem.ps("t")
    landed, wk_made, ready, h_made, turned, ht_made, projected, table_made, done, stored = (
        mem.sem(n) for n in ("landed", "wk_made", "ready", "h_made", "turned", "ht_made", "projected", "table_made",
                             "done", "stored"))
    vec = nc.vector
    LOADS = PROJECTION_LOADS + 2

    with nc.Block() as block:
        @block.sync
        def _(sp):
            sp.dma_start(bb[:], dr[bias].partition_broadcast(P)).then_inc(landed, 16)
            sp.dma_start(ident[:], dr["c_ident"]).then_inc(landed, 16)
            projection_load(nc, sp, pr, *(dr[n] for n in names), landed)
            sp.nop().then_inc(stored, 1)
            with sp.Fori(0, NT) as t:
                sp.wait_ge(table_made, 2 * t + 3)
                projection_store(sp, dr, pr, t, xsb, ksb, done)
                sp.wait_ge(done, t * (16 * PROJECTION_STORES) + 16 * PROJECTION_STORES)
                sp.nop().then_inc(stored, 1)

        @block.tensor
        def _(pe):
            pe.wait_ge(landed, 16 * LOADS)
            score_weights(nc, pr).then_inc(wk_made, 1)
            pe.wait_ge(ready, 1)
            with pe.Fori(0, NT) as t:
                pe.wait_ge(h_made, t + 1)
                for b in range(4):
                    last = nc.tensor.transpose(pst[:, b * P:b * P + P], hc[:, 128 * b:128 * b + 128], ident[0:P, 0:P])
                last.then_inc(turned, 1)
                pe.wait_ge(ht_made, t + 1)
                pe.wait_ge(table_made, 2 * t + 1)
                project(nc, pr, [(ht[:, b, :], b) for b in range(4)]).then_inc(projected, 1)

        @block.scalar
        def _(act):
            with act.Fori(0, NT) as t:
                act.wait_ge(turned, t + 1)
                nc.scalar.copy(ht[:].rearrange("p b n -> p (b n)"), pst[:, 0:4 * P]).then_inc(ht_made, 1)
                act.wait_ge(projected, t + 1)
                act.wait_ge(stored, t + 1)
                act.wait_ge(ready, 1)
                nc.scalar.copy(xsb[:, 1, :], pr["psx"][1][0:P, 0:F]).then_inc(table_made, 1)

        @block.vector
        def _(dve):
            dve.wait_ge(wk_made, 1)
            dve.wait_ge(landed, 16 * LOADS)
            take_score_weights(nc, pr)
            dve.drain()
            dve.nop().then_inc(ready, 1)
            dve.nop().then_inc(table_made, 1)
            with dve.Fori(0, NT) as t:
                normalized_heads(nc, dve, raw, agg, t, bb, den, 512, 4)
                dve.wait_ge(table_made, 2 * t + 1)
                here = kept[:, bass.ds(t, 1), :].rearrange("p o c -> p (o c)")
                if first:
                    vec.tensor_scalar(hc[:], raw[:], 0.0, None, ALU.max).then_inc(h_made, 1)
                    dve.drain()
                    vec.tensor_copy(here, hc[:])
                else:
                    vec.scalar_tensor_tensor(hc[:], raw[:], 0.0, here, ALU.max, ALU.add).then_inc(h_made, 1)
                dve.wait_ge(projected, t + 1)
                dve.wait_ge(stored, t + 1)
                vec.tensor_copy(xsb[:, 0, :], pr["psx"][0][0:P, 0:F])
                vec.tensor_copy(ksb[:].rearrange("p r s -> p (r s)"), pr["psk"][0:P, 0:4 * H])
                dve.drain()
                dve.nop().then_inc(table_made, 1)


def nodes_mix(nc, mem, dr, agg):
    nl = norm_buffers(mem)
    den, raw, hc, ht = mem.sb("den", [P, 8]), mem.sb("raw", [P, 128]), mem.sb("hc", [P, 128]), mem.sb("ht", [128, P])
    b3, pb, ab = mem.sb("b3", [P, 128]), mem.sb("pb", [P, D]), mem.sb("ab", [P, D])
    pw, aw = mem.sb("pw", [128, D]), mem.sb("aw", [128, 2, D])
    ident = mem.sb("ident", [128, 128])
    x0, x1 = mem.sb("x0", [P, D]), mem.sb("x1", [P, D])
    o1, o2, sq = mem.sb("o1", [P, D]), mem.sb("o2", [P, D]), mem.sb("sq", [P, D])
    ss, nrm, inv = mem.sb("ss", [P, 1]), mem.sb("nrm", [P, 1]), mem.sb("inv", [P, 2])
    r1, x2, x2t, hsb = mem.sb("r1", [P, D]), mem.sb("x2", [P, D]), mem.sb("x2t", [128, 2, P]), mem.sb("hsb", [P, D])
    pst, pso, psu, psh = (mem.ps(n) for n in ("t", "o", "u", "h"))
    (landed, x_in, used, h_made, turned, ht_made, o_made, ss_made, nrm_made, x2_made, x2_turned, x2t_made, table, made,
     done, stored) = (mem.sem(n) for n in (
         "landed", "x_in", "used", "h_made", "turned", "ht_made", "o_made", "ss_made", "nrm_made", "x2_made",
         "x2_turned", "x2t_made", "table", "made", "done", "stored"))
    vec, mm = nc.vector, nc.tensor.matmul

    with nc.Block() as block:
        @block.sync
        def _(sp):
            for t, name in ((b3, "L1_gnn_b3"), (pb, "L1_gnn_proj_b"), (ab, "L2_gnn_aw_b")):
                sp.dma_start(t[:], dr[name].partition_broadcast(P)).then_inc(landed, 16)
            sp.dma_start(pw[:], dr["L1_gnn_proj_w"]).then_inc(landed, 16)
            sp.dma_start(aw[:], dr["L2_gnn_aw_W"].rearrange("(b p) o -> p b o", p=128)).then_inc(landed, 16)
            sp.dma_start(ident[:], dr["c_ident"]).then_inc(landed, 16)
            sp.nop().then_inc(stored, 1)
            with sp.Fori(0, NT) as t:
                sp.wait_ge(used, t + 1)
                sp.dma_start(x0[:], rows(dr["x0"], t)).then_inc(x_in, 16)
                sp.dma_start(x1[:], rows(dr["x1"], t)).then_inc(x_in, 16)
                sp.wait_ge(made, t + 1)
                sp.dma_start(rows(dr["x2"], t), x2[:]).then_inc(done, 16)
                sp.dma_start(rows(dr["h2"], t), hsb[:]).then_inc(done, 16)
                sp.wait_ge(done, t * 32 + 32)
                sp.nop().then_inc(stored, 1)

        @block.tensor
        def _(pe):
            pe.wait_ge(landed, 16 * 6)
            with pe.Fori(0, NT) as t:
                pe.wait_ge(h_made, t + 1)
                nc.tensor.transpose(pst[:, 0:P], hc[:], ident[0:P, 0:P]).then_inc(turned, 1)
                pe.wait_ge(ht_made, t + 1)
                mm(pso[0:P, 0:D], ht[:], pw[:], start=True, stop=True).then_inc(o_made, 1)
                pe.wait_ge(x2_made, t + 1)
                for b in range(2):
                    last = nc.tensor.transpose(psu[:, b * P:b * P + P], x2[:, 128 * b:128 * b + 128], ident[0:P, 0:P])
                last.then_inc(x2_turned, 1)
                pe.wait_ge(x2t_made, t + 1)
                for b in range(2):
                    last = mm(psh[0:P, 0:D], x2t[:, b, :], aw[:, b, :], start=(b == 0), stop=(b == 1))
                last.then_inc(table, 1)

        @block.scalar
        def _(act):
            with act.Fori(0, NT) as t:
                act.wait_ge(turned, t + 1)
                nc.scalar.copy(ht[:], pst[:, 0:P]).then_inc(ht_made, 1)
                act.wait_ge(ss_made, t + 1)
                nc.scalar.activation(nrm[:], ss[:], ACT.Sqrt).then_inc(nrm_made, 1)
                norm_root(nc, act, nl, t)
                act.wait_ge(x2_turned, t + 1)
                nc.scalar.copy(x2t[:].rearrange("p b n -> p (b n)"), psu[:, 0:2 * P]).then_inc(x2t_made, 1)

        @block.vector
        def _(dve):
            dve.nop().then_inc(used, 1)
            dve.wait_ge(landed, 16 * 6)
            with dve.Fori(0, NT) as t:
                normalized_heads(nc, dve, raw, agg, t, b3, den, 128, 1)
                vec.tensor_scalar(hc[:], raw[:], 0.0, None, ALU.max).then_inc(h_made, 1)
                dve.wait_ge(o_made, t + 1)
                vec.tensor_tensor(o1[:], pso[0:P, 0:D], pb[:], ALU.add)
                dve.drain()
                dve.wait_ge(x_in, t * 32 + 32)
                vec.tensor_tensor(o2[:], o1[:], x0[:], ALU.add)
                dve.drain()
                vec.tensor_tensor_reduce(out=sq[:], in0=o2[:], in1=o2[:], scale=1.0, scalar=0.0, op0=ALU.mult,
                                         op1=ALU.add, accum_out=ss[:]).then_inc(ss_made, 1)
                dve.wait_ge(nrm_made, t + 1)
                vec.tensor_scalar(inv[:, 0:1], nrm[:], 1e-12, None, ALU.max)
                dve.drain()
                vec.reciprocal(inv[:, 1:2], inv[:, 0:1])
                dve.drain()
                vec.scalar_tensor_tensor(r1[:], o2[:], inv[:, 1:2], x1[:], ALU.mult, ALU.add).then_inc(used, 1)
                norm_statistics(nc, dve, nl, r1[:])
                dve.wait_ge(stored, t + 1)
                norm_scale(nc, dve, nl, t, x2[:], r1[:]).then_inc(x2_made, 1)
                dve.wait_ge(table, t + 1)
                vec.tensor_tensor(hsb[:], psh[0:P, 0:D], ab[:], ALU.add).then_inc(made, 1)


def soft(nc, dve, t_in, neg):
    return nc.vector.scalar_tensor_tensor(neg, t_in, -1.0, t_in, ALU.mult, ALU.min)


def filter_sum(nc, mem, dr, keep, agg):
    C4 = HF * P
    idx, gx = mem.sb("idx", [P, U], I32), mem.sb("gx", [P, 2, HF, D])
    ea = mem.sb("ea", [64, 2, HF, P])
    m1, m2, mb = mem.sb("m1", [64, D]), mem.sb("m2", [128, 2, D]), mem.sb("mb", [P, D])
    iota, half = mem.sb("iota", [128, 512]), mem.sb("half", [128, 1])
    neg1, h1 = mem.sb("neg1", [128, 2, C4]), mem.sb("h1", [128, 2, C4])
    f2, neg2, sp2, ms = (mem.sb(n, [P, HF, D]) for n in ("f2", "neg2", "sp2", "ms"))
    cl, dl, sel = mem.sb("cl", [P, HF]), mem.sb("dl", [P, HF]), mem.sb("sel", [P, HF, P])
    ps1, ps2, ps3 = mem.ps("1", [128, 2, 512]), mem.ps("2", [128, HF, D]), mem.ps("3", [128, HF, D])
    (landed, listed, nopped, used, ea_free, hid, neg1_made, log1_made, h1_made, filt, neg2_made, log2_made, ms_made,
     summed, added) = (mem.sem(n) for n in (
         "landed", "listed", "nopped", "used", "ea_free", "hid", "neg1_made", "log1_made", "h1_made", "filt",
         "neg2_made", "log2_made", "ms_made", "summed", "added"))
    x_in, e_in = [mem.sem(f"x{q}") for q in range(2)], [mem.sem(f"e{q}") for q in range(2)]
    vec, mm = nc.vector, nc.tensor.matmul
    TURNS = KS // U

    with nc.Block() as block:
        @block.gpsimd
        def _(pool):
            pool.wait_ge(landed, 16 * 5)
            with pool.Fori(0, TURNS) as i:
                for q in range(2):
                    pool.wait_ge(used, 2 * i + q + 1)
                    pool.nop().then_inc(nopped, 1)
                    nc.gpsimd.tensor_copy(idx[:, HF * q:HF * q + HF],
                                          keep["src_step"][:, bass.ds(i * U + HF * q, HF)]).then_inc(listed, 1)
                    pool.wait_ge(listed, 2 * i + q + 1)
                    pool.nop().then_inc(nopped, 1)
                    for j in range(HF):
                        n = HF * q + j
                        nc.gpsimd.indirect_dma_start(
                            out=gx[:, q, j, :], out_offset=None, in_=dr["h2"],
                            in_offset=bass.IndirectOffsetOnAxis(ap=idx[:, n:n + 1], axis=0)).then_inc(x_in[q], 16)

        @block.sync
        def _(sp):
            sp.dma_start(m1[0:50, :], dr["L2_gnn_m1_W"]).then_inc(landed, 16)
            sp.dma_start(m1[50:51, :], dr["L2_gnn_m1_b"].rearrange("(o c) -> o c", o=1)).then_inc(landed, 16)
            sp.dma_start(m2[:], dr["L2_gnn_m2_W"].rearrange("(b p) o -> p b o", p=128)).then_inc(landed, 16)
            sp.dma_start(iota[:], dr["c_iota"]).then_inc(landed, 16)
            sp.dma_start(mb[:], dr["L2_gnn_m2_b"].partition_broadcast(P)).then_inc(landed, 16)

            def load(first, q):
                for j in range(HF):
                    tile = sp.value_load(keep["etile"][0:1, bass.ds(first + j, 1)], min_val=0, max_val=ET - 1)
                    sp.dma_start(ea[0:50, q, j, :], dr["ea_t"][:, bass.ds(tile * P, P)]).then_inc(e_in[q], 16)
            sp.wait_ge(ea_free, 2)
            load(0, 0)
            load(HF, 1)
            with sp.Fori(0, TURNS) as i:
                for q in range(2):
                    sp.wait_ge(ea_free, 2 * i + q + 3)
                    load(i * U + U + q * HF, q)
            sp.wait_ge(e_in[0], 16 * HF * (TURNS + 1))
            sp.wait_ge(e_in[1], 16 * HF * (TURNS + 1))

        @block.tensor
        def _(pe):
            def front(q, n, landings):
                pe.wait_ge(e_in[q], landings)
                pe.wait_ge(h1_made, n + 1)
                for o in range(2):
                    last = mm(ps1[:, o, 0:C4], m1[0:51, 128 * o:128 * o + 128],
                              ea[0:51, q].rearrange("p j e -> p (j e)"), start=True, stop=True)
                last.then_inc(hid, 1)

            pe.wait_ge(landed, 16 * 5)
            pe.wait_ge(added, 1)
            front(0, 0, 16 * HF)
            with pe.Fori(0, TURNS) as i:
                for q in range(2):
                    n = 2 * i + q
                    pe.wait_ge(h1_made, n + 2)
                    pe.wait_ge(added, n + 1)
                    for j in range(HF):
                        for b in range(2):
                            last = mm(ps2[0:P, j, :], h1[:, b, j * P:j * P + P], m2[:, b, :], start=(b == 0), stop=(b == 1))
                    last.then_inc(filt, 1)
                    front(1 - q, n + 1, (i + 1 + q) * (16 * HF))
                    pe.wait_ge(ms_made, n + 1)
                    for j in range(HF):
                        last = mm(ps3[0:P, j, :], sel[:, j, :], ms[:, j, :], start=True, stop=True)
                    last.then_inc(summed, 1)

        @block.scalar
        def _(act):
            def log(neg, made, n, out):
                act.wait_ge(made, n + 1)
                nc.scalar.activation(neg[:], neg[:], ACT.Exp)
                act.drain()
                nc.scalar.activation(neg[:], neg[:], ACT.Ln, scale=0.5, bias=half[0:neg.shape[0], :]).then_inc(out, 1)
            act.wait_ge(added, 1)
            log(neg1, neg1_made, 0, log1_made)
            with act.Fori(0, TURNS) as i:
                for q in range(2):
                    log(neg2, neg2_made, 2 * i + q, log2_made)
                    log(neg1, neg1_made, 2 * i + q + 1, log1_made)

        @block.vector
        def _(dve):
            def front_neg(n):
                dve.wait_ge(hid, n + 1)
                vec.tensor_copy(h1[:], ps1[:, :, 0:C4])
                dve.drain()
                soft(nc, dve, h1[:], neg1[:]).then_inc(neg1_made, 1)
                dve.nop().then_inc(ea_free, 1)

            def front_sum(n):
                dve.wait_ge(log1_made, n + 1)
                vec.scalar_tensor_tensor(h1[:], h1[:], 0.0, neg1[:], ALU.max, ALU.add).then_inc(h1_made, 1)

            for q in range(2):
                vec.memset(ea[:, q], 1.0)
            vec.memset(half[:], 0.5)
            for t in range(0, NT + 1, 13):
                vec.memset(agg[:, t:t + 13, 0:D], 0.0)
            dve.drain()
            for sem in (ea_free, ea_free, added, h1_made, used, used):
                dve.nop().then_inc(sem, 1)
            dve.wait_ge(landed, 16 * 5)
            front_neg(0)
            front_sum(0)
            with dve.Fori(0, TURNS) as i:
                for q in range(2):
                    n = 2 * i + q
                    vec.tensor_copy(cl[:], keep["cut"][:, bass.ds(i * U + q * HF, HF)])
                    vec.tensor_copy(dl[:], keep["dloc"][:, bass.ds(i * U + q * HF, HF)])
                    dve.drain()
                    for j in range(HF):
                        vec.tensor_scalar(sel[:, j, :], iota[0:P, 0:P], dl[:, j:j + 1], None, ALU.is_equal)
                    dve.wait_ge(filt, n + 1)
                    for j in range(HF):
                        last = vec.tensor_tensor(f2[:, j, :], ps2[0:P, j, :], mb[:], ALU.add)
                    dve.drain()
                    soft(nc, dve, f2[:], neg2[:]).then_inc(neg2_made, 1)
                    front_neg(n + 1)
                    dve.wait_ge(log2_made, n + 1)
                    vec.scalar_tensor_tensor(sp2[:], f2[:], 0.0, neg2[:], ALU.max, ALU.add)
                    dve.drain()
                    dve.wait_ge(x_in[q], (i + 1) * (16 * HF))
                    for j in range(HF):
                        vec.scalar_tensor_tensor(ms[:, j, :], sp2[:, j, :], cl[:, j:j + 1], gx[:, q, j, :], ALU.mult, ALU.mult)
                    dve.drain()
                    dve.nop().then_inc(ms_made, 1)
                    dve.nop().then_inc(used, 1)
                    front_sum(n + 1)
                    dve.wait_ge(summed, n + 1)
                    for j in range(HF):
                        tile = vec.value_load(keep["nk"][0:1, bass.ds(i * U + q * HF + j, 1)], min_val=0, max_val=NT - 1)
                        here = agg[:, bass.ds(tile, 1), 0:D].rearrange("p o f -> p (o f)")
                        vec.tensor_tensor(here, ps3[0:P, j, :], here, ALU.add)
                        dve.drain()
                    dve.nop().then_inc(added, 1)


def nodes_filter(nc, mem, dr, agg):
    nl = norm_buffers(mem)
    w1, w2, w3 = (mem.sb(n, [128, 2, D]) for n in ("w1", "w2", "w3"))
    b1, half = mem.sb("b1", [128, 2]), mem.sb("half", [128, 1])
    b2, b3 = mem.sb("b2", [P, D]), mem.sb("b3", [P, D])
    ident = mem.sb("ident", [128, 128])
    at, f1, neg, h1, x3t = (mem.sb(n, [128, 2, P]) for n in ("at", "f1", "neg", "h1", "x3t"))
    x2, o1, r1, x3, hsb = (mem.sb(n, [P, D]) for n in ("x2", "o1", "r1", "x3", "hsb1"))
    hs = mem.sb("hs", [P, D + 1])
    zero = mem.sb("zero", [P, D + 1])
    ag, ag_made = mem.sb("ag", [P, D]), mem.sem("ag_made")
    psa, psf, pso, psu, psh = (mem.ps(n) for n in ("a", "f", "o", "u", "h"))
    (landed, zeroed, x_in, used, turned, at_made, hid, neg_made, log_made, h1_made, o_made, x3_made, x3_turned,
     x3t_made, table, made, done, stored, cleared) = (mem.sem(n) for n in (
         "landed", "zeroed", "x_in", "used", "turned", "at_made", "hid", "neg_made", "log_made", "h1_made", "o_made",
         "x3_made", "x3_turned", "x3t_made", "table", "made", "done", "stored", "cleared"))
    vec, mm = nc.vector, nc.tensor.matmul

    with nc.Block() as block:
        @block.sync
        def _(sp):
            with nc.allow_non_contiguous_dma(reason="a short vector"):
                sp.dma_start(b1[:], dr["L2_gnn_o1_b"].rearrange("(b p) -> p b", p=128)).then_inc(landed, 16)
            for t, name in ((w1, "L2_gnn_o1_W"), (w2, "L2_gnn_o2_W"), (w3, "L3_gnn_W")):
                sp.dma_start(t[:], dr[name].rearrange("(b p) o -> p b o", p=128)).then_inc(landed, 16)
            for t, name in ((b2, "L2_gnn_o2_b"), (b3, "L3_gnn_b")):
                sp.dma_start(t[:], dr[name].partition_broadcast(P)).then_inc(landed, 16)
            sp.dma_start(ident[:], dr["c_ident"]).then_inc(landed, 16)
            sp.nop().then_inc(stored, 1)
            sp.wait_ge(zeroed, 1)
            for j in range(HF):
                for t in range(NT + 1):
                    sp.dma_start(dr["sum"][j][P * t:P * t + P, :], zero[:]).then_inc(cleared, 16)
            with sp.Fori(0, NT) as t:
                sp.wait_ge(used, t + 1)
                sp.dma_start(x2[:], rows(dr["x2"], t)).then_inc(x_in, 16)
                sp.wait_ge(made, t + 1)
                sp.dma_start(rows(dr["x3"], t), x3[:]).then_inc(done, 16)
                sp.dma_start(rows(dr["h3"], t), hs[:]).then_inc(done, 16)
                sp.wait_ge(done, t * 32 + 32)
                sp.nop().then_inc(stored, 1)
            sp.wait_ge(cleared, 16 * HF * (NT + 1))

        @block.tensor
        def _(pe):
            pe.wait_ge(landed, 16 * 7)
            with pe.Fori(0, NT) as t:
                pe.wait_ge(ag_made, t + 1)
                for b in range(2):
                    last = nc.tensor.transpose(psa[:, b * P:b * P + P], ag[:, 128 * b:128 * b + 128], ident[0:P, 0:P])
                last.then_inc(turned, 1)
                pe.wait_ge(at_made, t + 1)
                for o in range(2):
                    for b in range(2):
                        last = mm(psf[:, o * P:o * P + P], w1[:, b, 128 * o:128 * o + 128], at[:, b, :], start=(b == 0), stop=(b == 1))
                last.then_inc(hid, 1)
                pe.wait_ge(h1_made, t + 1)
                for b in range(2):
                    last = mm(pso[0:P, 0:D], h1[:, b, :], w2[:, b, :], start=(b == 0), stop=(b == 1))
                last.then_inc(o_made, 1)
                pe.wait_ge(x3_made, t + 1)
                for b in range(2):
                    last = nc.tensor.transpose(psu[:, b * P:b * P + P], x3[:, 128 * b:128 * b + 128], ident[0:P, 0:P])
                last.then_inc(x3_turned, 1)
                pe.wait_ge(x3t_made, t + 1)
                for b in range(2):
                    last = mm(psh[0:P, 0:D], x3t[:, b, :], w3[:, b, :], start=(b == 0), stop=(b == 1))
                last.then_inc(table, 1)

        @block.scalar
        def _(act):
            act.wait_ge(zeroed, 1)
            nc.scalar.copy(ag[:], agg[:, 0, 0:D]).then_inc(ag_made, 1)
            with act.Fori(0, NT) as t:
                act.wait_ge(turned, t + 1)
                nc.scalar.copy(at[:].rearrange("p b n -> p (b n)"), psa[:, 0:2 * P]).then_inc(at_made, 1)
                nc.scalar.copy(ag[:], agg[:, bass.ds(t + 1, 1), 0:D].rearrange("p o c -> p (o c)")).then_inc(ag_made, 1)
                act.wait_ge(neg_made, t + 1)
                nc.scalar.activation(neg[:], neg[:], ACT.Exp)
                act.drain()
                nc.scalar.activation(neg[:], neg[:], ACT.Ln, scale=0.5, bias=half[:]).then_inc(log_made, 1)
                norm_root(nc, act, nl, t)
                act.wait_ge(x3_turned, t + 1)
                nc.scalar.copy(x3t[:].rearrange("p b n -> p (b n)"), psu[:, 0:2 * P]).then_inc(x3t_made, 1)

        @block.vector
        def _(dve):
            vec.memset(half[:], 0.5)
            vec.memset(hs[:], 1.0)
            vec.memset(zero[:], 0.0)
            dve.drain()
            dve.nop().then_inc(zeroed, 1)
            dve.nop().then_inc(used, 1)
            dve.wait_ge(landed, 16 * 7)
            with dve.Fori(0, NT) as t:
                dve.wait_ge(hid, t + 1)
                for o in range(2):
                    vec.tensor_scalar(f1[:, o, :], psf[:, o * P:o * P + P], b1[:, o:o + 1], None, ALU.add)
                dve.drain()
                soft(nc, dve, f1[:], neg[:]).then_inc(neg_made, 1)
                dve.wait_ge(log_made, t + 1)
                vec.scalar_tensor_tensor(h1[:], f1[:], 0.0, neg[:], ALU.max, ALU.add).then_inc(h1_made, 1)
                dve.wait_ge(o_made, t + 1)
                vec.tensor_tensor(o1[:], pso[0:P, 0:D], b2[:], ALU.add)
                dve.drain()
                dve.wait_ge(x_in, t * 16 + 16)
                vec.tensor_tensor(r1[:], o1[:], x2[:], ALU.add).then_inc(used, 1)
                norm_statistics(nc, dve, nl, r1[:])
                dve.wait_ge(stored, t + 1)
                norm_scale(nc, dve, nl, t, x3[:], r1[:]).then_inc(x3_made, 1)
                dve.wait_ge(table, t + 1)
                vec.tensor_tensor(hs[:, 0:D], psh[0:P, 0:D], b3[:], ALU.add).then_inc(made, 1)


def source_sum(nc, mem, dr, keep):
    W = D + 1
    idx, gx = mem.sb("idx", [P, U], I32), mem.sb("gx", [P, U, W])
    si = mem.sb("si", [P, 2, HF, P], I32)
    col = mem.sb("col", [P, U], I32)
    sf, eq, hit = mem.sb("sf", [P, HF]), mem.sb("eq", [P, U, P]), mem.sb("hit", [P, HF, P])
    low, column = mem.sb("low", [128, 128]), mem.sb("column", [128, 3])
    before, off, tgt = mem.sb("before", [P, HF]), mem.sb("off", [P, HF]), mem.sb("tgt", [P, U], I32)
    ms = mem.sb("ms", [P, U, W])
    pss = [mem.ps(f"s{j}") for j in range(HF)]
    (landed, listed, nopped, summed, taken, eq_made, sums_made) = (mem.sem(n) for n in (
        "landed", "listed", "nopped", "summed", "taken", "eq_made", "sums_made"))
    x_in, s_in, free, done = ([mem.sem(f"{n}{q}") for q in range(2)] for n in ("x", "s", "f", "d"))
    vec = nc.vector
    TURNS = ET // U

    with nc.Block() as block:
        @block.sync
        def _(sp):
            sp.dma_start(low[:], dr["c_low"]).then_inc(landed, 16)
            sp.dma_start(column[:], dr["c_column"]).then_inc(landed, 16)
            with sp.Fori(0, TURNS) as i:
                for q in range(2):
                    sp.wait_ge(free[q], i + 1)
                    sp.dma_start(si[:, q].rearrange("p j e -> p (j e)"),
                                 dr["src"][bass.ds(i * (U * P) + q * HF * P, HF * P)].partition_broadcast(P)).then_inc(s_in[q], 16)

        @block.gpsimd
        def _(pool):
            def gather(i, q):
                pool.wait_ge(sums_made, 2 * i + q + 1)
                pool.nop().then_inc(nopped, 1)
                nc.gpsimd.tensor_copy(idx[:, HF * q:HF * q + HF],
                                      keep["dst_tile"][:, bass.ds(i * U + HF * q, HF)]).then_inc(listed, 1)
                pool.wait_ge(listed, 2 * i + q + 1)
                pool.nop().then_inc(nopped, 1)
                for j in range(HF * q, HF * q + HF):
                    nc.gpsimd.indirect_dma_start(
                        out=gx[:, j, :], out_offset=None, in_=dr["h3"],
                        in_offset=bass.IndirectOffsetOnAxis(ap=idx[:, j:j + 1], axis=0)).then_inc(x_in[q], 16)

            def scatter(i, q):
                pool.wait_ge(sums_made, 2 * i + q + 3)
                if not (isinstance(i, int) and i + q == 0):
                    pool.wait_ge(done[1 - q], (i + q) * (16 * HF))
                    pool.nop().then_inc(nopped, 1)
                for j in range(HF):
                    n = HF * q + j
                    nc.gpsimd.indirect_dma_start(
                        out=dr["sum"][j], out_offset=bass.IndirectOffsetOnAxis(ap=tgt[:, n:n + 1], axis=0),
                        in_=ms[:, n, :], in_offset=None, compute_op=ALU.add).then_inc(done[q], 16)

            pool.wait_ge(landed, 32)
            gather(0, 0)
            gather(0, 1)
            scatter(0, 0)
            with pool.Fori(1, TURNS) as i:
                gather(i, 0)
                scatter(i - 1, 1)
                gather(i, 1)
                scatter(i, 0)
            scatter(TURNS - 1, 1)
            for q in range(2):
                pool.wait_ge(done[q], TURNS * 16 * HF)

        @block.tensor
        def _(pe):
            for j in range(HF):
                pe.nop().then_inc(taken, 1)
            with pe.Fori(0, TURNS) as i:
                for q in range(2):
                    pe.wait_ge(eq_made, 2 * i + q + 1)
                    pe.wait_ge(x_in[q], i * (16 * HF) + 16 * HF)
                    for j in range(HF):
                        pe.wait_ge(taken, i * U + q * HF + j + 1)
                        nc.tensor.matmul(pss[j][0:P, 0:W], eq[:, HF * q + j, :], gx[:, HF * q + j, :], start=True,
                                         stop=True).then_inc(summed, 1)

        @block.vector
        def _(dve):
            for q in range(2):
                dve.nop().then_inc(sums_made, 1)
                dve.nop().then_inc(free[q], 1)
            dve.wait_ge(landed, 32)
            def tiles(i, first):
                for q in range(2):
                    half = slice(HF * q, HF * q + HF)
                    vec.tensor_copy(sf[:], keep["src_tile"][:, bass.ds(i * U + HF * q, HF)])
                    dve.drain()
                    dve.wait_ge(s_in[q], i * 16 + 16)
                    for j in range(HF):
                        vec.tensor_scalar(eq[:, HF * q + j, :], si[:, q, j, :], sf[:, j:j + 1], None, ALU.is_equal)
                    dve.drain()
                    dve.nop().then_inc(eq_made, 1)
                    dve.nop().then_inc(free[q], 1)
                    for j in range(HF):
                        vec.tensor_tensor_reduce(out=hit[:, j, :], in0=eq[:, HF * q + j, :], in1=low[0:P, 0:P], scale=1.0,
                                                 scalar=0.0, op0=ALU.mult, op1=ALU.add, accum_out=before[:, j:j + 1])
                    dve.drain()
                    vec.tensor_scalar(before[:], before[:], 1.0, None, ALU.min)
                    vec.tensor_scalar(off[:], sf[:], column[0:P, 2:3], -1.0, ALU.subtract, ALU.mult)
                    dve.drain()
                    vec.tensor_tensor(off[:], off[:], before[:], ALU.mult)
                    dve.drain()
                    if not first:
                        dve.wait_ge(done[q], i * (16 * HF))
                    vec.tensor_tensor(tgt[:, half], off[:], sf[:], ALU.add)
                    for j in range(HF):
                        dve.wait_ge(summed, i * U + q * HF + j + 1)
                        vec.tensor_copy(ms[:, HF * q + j, :], pss[j][0:P, 0:W]).then_inc(taken, 1)
                    dve.drain()
                    dve.nop().then_inc(sums_made, 1)

            tiles(0, True)
            with dve.Fori(1, TURNS) as i:
                tiles(i, False)


def nodes_mean(nc, mem, dr):
    nl = norm_buffers(mem)
    W = D + 1
    sm, x3 = mem.sb("sm", [P, 2, HF, W]), mem.sb("x3", [P, 2, D])
    s1, s2 = mem.sb("s1", [P, 2, W]), mem.sb("s2", [P, W])
    cnt, r1, res = mem.sb("cnt", [P, 2]), mem.sb("r1", [P, D]), mem.sb("res", [P, D])
    used, made, done, stored = (mem.sem(n) for n in ("used", "made", "done", "stored"))
    x_in = [mem.sem(f"x_in{q}") for q in range(2)]
    vec = nc.vector

    with nc.Block() as block:
        @block.sync
        def _(sp):
            def load(t, q):
                for j in range(HF):
                    sp.dma_start(sm[:, q, j, :], rows(dr["sum"][j], t)).then_inc(x_in[q], 16)
                sp.dma_start(x3[:, q, :], rows(dr["x3"], t)).then_inc(x_in[q], 16)

            load(0, 0)
            with sp.Fori(0, (NT - 1) // 2) as i:
                for q in range(2):
                    sp.wait_ge(used, 2 * i + q + 1)
                    load(2 * i + q + 1, 1 - q)
            sp.wait_ge(used, NT + 1)

        @block.scalar
        def _(act):
            with act.Fori(0, NT) as t:
                norm_root(nc, act, nl, t)
                act.wait_ge(made, t + 1)
                act.dma_start(rows(dr["out"], t), res[:]).then_inc(done, 16)
                act.wait_ge(done, t * 16 + 16)
                act.nop().then_inc(stored, 1)

        @block.vector
        def _(dve):
            dve.nop().then_inc(used, 1)
            dve.nop().then_inc(stored, 1)

            def tile(t, q, landings):
                dve.wait_ge(x_in[q], landings)
                vec.tensor_tensor(s1[:], sm[:, q, 0:2, :], sm[:, q, 2:4, :], ALU.add)
                dve.drain()
                vec.tensor_tensor(s2[:], s1[:, 0, :], s1[:, 1, :], ALU.add)
                dve.drain()
                vec.tensor_scalar(cnt[:, 0:1], s2[:, D:W], 1.0, None, ALU.max)
                dve.drain()
                vec.reciprocal(cnt[:, 1:2], cnt[:, 0:1])
                dve.drain()
                vec.scalar_tensor_tensor(r1[:], s2[:, 0:D], cnt[:, 1:2], x3[:, q, :], ALU.mult, ALU.add).then_inc(used, 1)
                norm_statistics(nc, dve, nl, r1[:])
                dve.wait_ge(stored, t + 1)
                norm_scale(nc, dve, nl, t, res[:], r1[:]).then_inc(made, 1)
                dve.drain()

            with dve.Fori(0, (NT - 1) // 2) as i:
                for q in range(2):
                    tile(2 * i + q, q, i * 80 + 80)
            tile(NT - 1, 0, 80 * ((NT + 1) // 2))


def build(nc, dr):
    for name, shape in (("rho", (NCOL, R)), ("ends", (2, ET)), ("carry", (4, 4, ET)), ("x0", (N, D)), ("x1", (N, D)),
                        ("x2", (N, D)), ("x3", (N, D)), ("xw", (2 * N, 512)), ("xw1", (2 * N, 128)), ("kt", (2 * N, 4)),
                        ("qt", (2 * N, 4)), ("kt1", (2 * N, 1)), ("qt1", (2 * N, 1)), ("h2", (N, D)), ("h3", (N, D + 1))):
        dr[name] = nc.dram_tensor("scratch_" + name, shape, F32, kind="Internal").ap()
    dr["sum"] = [nc.dram_tensor(f"scratch_sum{j}", (N + P, D + 1), F32, kind="Internal").ap() for j in range(HF)]

    def phase(name):
        return Mem(nc, name)

    with phase("turned") as outer:
        mt = outer.sb("mt", [128, 2, D])
        with phase("steps") as columns:
            col = columns.sb("col", [128, 4, NCOL])
            with phase("prepare") as mem:
                layer0_prepare(nc, mem, dr, col)
            with phase("turn") as mem:
                layer0_turn(nc, mem, dr, col, mt)
        with phase("gate") as mem:
            nodes_gate(nc, mem, dr, mt)
    with phase("keep") as keeper:
        keep = edge_lists(keeper)
        agg = keeper.sb("agg", [P, NT + 1, 516])
        with phase("order") as mem:
            edge_order(nc, mem, dr, keep)
        with phase("kept") as outer:
            kept = outer.sb("h", [P, NT, 512])
            with phase("weights1") as mem:
                attention_weights(nc, mem, dr, keep, 4, 1)
            with phase("sum1") as mem:
                attention_sum(nc, mem, dr, keep, agg, dr["xw"], 4, 512, 1)
            with phase("attend1") as mem:
                nodes_attend(nc, mem, dr, agg, kept, "L1_gnn_b1", ("L1_gnn_W2", "W2_t", "L1_gnn_k2", "L1_gnn_q2"),
                             512, 4, True)
            with phase("weights2") as mem:
                attention_weights(nc, mem, dr, keep, 4, 2)
            with phase("sum2") as mem:
                attention_sum(nc, mem, dr, keep, agg, dr["xw"], 4, 512, 2)
            with phase("attend2") as mem:
                nodes_attend(nc, mem, dr, agg, kept, "L1_gnn_b2", ("L1_gnn_W3", "W3_t", "L1_gnn_k3", "L1_gnn_q3"),
                             128, 1, False)
        with phase("weights3") as mem:
            attention_weights(nc, mem, dr, keep, 1, 3)
        with phase("sum3") as mem:
            attention_sum(nc, mem, dr, keep, agg, dr["xw1"], 1, 128, 3)
        with phase("mix") as mem:
            nodes_mix(nc, mem, dr, agg)
        with phase("filter") as mem:
            filter_sum(nc, mem, dr, keep, agg)
        with phase("filtered") as mem:
            nodes_filter(nc, mem, dr, agg)
        with phase("source") as mem:
            source_sum(nc, mem, dr, keep)
        with phase("mean") as mem:
            nodes_mean(nc, mem, dr)


_INS = [
    "x", "src", "dst", "edge_type_2", "edge_weight", "L1_gnn_query", "L1_gnn_gate_w1", "L1_gnn_gate_b1",
    "L1_gnn_gate_w2", "L1_gnn_gate_b2", "L1_gnn_W1", "L1_gnn_q1", "L1_gnn_k1", "L1_gnn_b1", "L1_gnn_W2", "L1_gnn_q2",
    "L1_gnn_k2", "L1_gnn_b2", "L1_gnn_W3", "L1_gnn_q3", "L1_gnn_k3", "L1_gnn_b3", "L1_gnn_proj_w", "L1_gnn_proj_b",
    "L2_gnn_aw_W", "L2_gnn_aw_b", "L2_gnn_m1_W", "L2_gnn_m1_b", "L2_gnn_m2_W", "L2_gnn_m2_b", "L2_gnn_o1_W",
    "L2_gnn_o1_b", "L2_gnn_o2_W", "L2_gnn_o2_b", "L3_gnn_W", "L3_gnn_b"]


def kernel(**inputs):
    import concourse.bacc as bacc
    from concourse.bass_utils import run_bass_kernel_spmd

    arrays = {name: np.ascontiguousarray(inputs[name]) for name in _INS}
    arrays["x_t2"] = np.ascontiguousarray(np.pad(np.asarray(inputs["x"]).T, ((0, 0), (0, P))))
    arrays["ea_t"] = np.ascontiguousarray(np.asarray(inputs["edge_attr_50"]).T)
    for n in (1, 2, 3):
        arrays[f"W{n}_t"] = np.ascontiguousarray(np.asarray(inputs[f"L1_gnn_W{n}"]).transpose(0, 2, 1))
    arrays.update(host_constants())
    nc = bacc.Bacc("TRN2", target_bir_lowering=False, num_devices=1)
    dr = {n: nc.dram_tensor("in_" + n, a.shape, mybir.dt.from_np(a.dtype), kind="ExternalInput").ap()
          for n, a in arrays.items()}
    dr["out"] = nc.dram_tensor("out_x", (N, D), F32, kind="ExternalOutput").ap()
    build(nc, dr)
    r = run_bass_kernel_spmd(nc, [{"in_" + n: a for n, a in arrays.items()}], core_ids=[0])
    return r.results[0]["out_x"]
```

```python
from contextlib import ExitStack

import numpy as np

import concourse.bass as bass
from concourse import mybir

F32 = mybir.dt.float32
I32 = mybir.dt.int32
ALU = mybir.AluOpType
ACT = mybir.ActivationFunctionType
AX = mybir.AxisListType

N, E, D = 3125, 50000, 256
P = 125
NT, ET = N // P, E // P
EC = 100
NEC = ET // EC

K = 64
R = 2 * K
CP, CA = 112, 7
NCH = CP * CA
G = 4
NG = NCH // G
STAGES = NG + 2
NCOL = (STAGES + 2) * G
LV = 6
TWO_PI_HI, TWO_PI_LO = 6.28125, 0.0019353071795864769
ROUND = 12582912.0
PI_SAFE = 3.1415925
BIG = 1.0e30


def host_constants():
    t = np.arange(R) % K
    masks = np.zeros((128, LV + 1, G, 128), np.float32)
    for lv in range(LV):
        b = t // (1 << lv)
        masks[:, lv] = ((b[:, None] + 1 == b[None, :]) & (b[None, :] % 2 == 1))[:, None, :]
    ident = np.eye(128, dtype=np.float32)
    masks[:, LV] = ident[:, None, :]
    iota = np.broadcast_to(np.arange(512, dtype=np.float32), (128, 512))
    column = np.stack([np.arange(128), np.arange(128) + 128, np.arange(128) + N], 1).astype(np.float32)
    tri = (np.arange(128)[:, None] < np.arange(128)[None, :]).astype(np.float32)
    return dict(c_masks=masks, c_ident=ident, c_iota=np.ascontiguousarray(iota), c_column=column, c_tri=tri,
                c_low=np.ascontiguousarray(tri.T))


class Mem:

    def __init__(self, nc, phase):
        self.nc, self.phase, self.ctx, self.sems = nc, phase, ExitStack(), []

    def __enter__(self):
        return self

    def __exit__(self, *a):
        if self.sems:
            self.nc.clear_and_free_semaphores(self.sems)
            self.nc.all_engine_barrier()
        self.ctx.close()

    def sb(self, name, shape, dt=F32):
        return self.ctx.enter_context(self.nc.sbuf_tensor(f"{self.phase}_{name}_sb", shape, dt))

    def ps(self, name, shape=(128, 512)):
        return self.ctx.enter_context(self.nc.psum_tensor(f"{self.phase}_{name}_ps", list(shape), F32))

    def sem(self, name):
        self.sems.append(self.nc.alloc_semaphore(f"{self.phase}_{name}"))
        return self.sems[-1]


def layer0_order(nc, mem, dr, turns):
    raw = {n: mem.sb("r_" + n, [EC, NEC, P], I32) for n in ("src", "dst")}
    f = {n: mem.sb("f_" + n, [EC, NEC, P]) for n in ("src", "dst")}
    th = mem.sb("th", [EC, NEC, P])
    ident, tri, ones = mem.sb("ident", [128, 128]), mem.sb("tri", [128, 128]), mem.sb("ones", [128, 128])
    column, iota = mem.sb("column", [128, 3]), mem.sb("iota", [128, 512])
    rec = mem.sb("rec", [P, ET, 3])
    touch, place, others, number = (mem.sb(n, [P, ET]) for n in ("touch", "place", "others", "number"))
    one, through, row = mem.sb("one", [P, ET]), mem.sb("through", [P, ET]), mem.sb("row", [P, ET], I32)
    need = mem.sb("need", [1, 1])
    S8 = 8
    at, out = mem.sb("at", [P, 2, S8], I32), mem.sb("out", [P, 2, S8, 3])
    pst = [mem.ps(f"t{q}") for q in range(2)]
    before, tiles_sum = mem.ps("before"), mem.ps("tiles")
    landed, floats, turned, copied, touched, counted, placed, listed, nopped = (mem.sem(n) for n in (
        "landed", "floats", "turned", "copied", "touched", "counted", "placed", "listed", "nopped"))
    moved = [mem.sem(f"moved{q}") for q in range(2)]
    vec = nc.vector

    def tiles(name):
        return dr[name].rearrange("(c p l) -> p c l", p=EC, l=P)

    with nc.Block() as block:
        @block.sync
        def _(sp):
            for t, name in ((raw["src"], "src"), (raw["dst"], "dst"), (th, "edge_weight")):
                sp.dma_start(t[:], tiles(name)).then_inc(landed, 16)
            for t, name in ((ident, "c_ident"), (tri, "c_tri"), (column, "c_column"), (iota, "c_iota")):
                sp.dma_start(t[:], dr[name]).then_inc(landed, 16)

        @block.tensor
        def _(pe):
            pe.wait_ge(landed, 16 * 7)
            pe.wait_ge(floats, 1)
            for n in range(3 * NEC):
                field = (f["src"], f["dst"], th)[n // NEC]
                if n >= 2:
                    pe.wait_ge(copied, n - 1)
                nc.tensor.transpose(pst[n % 2][0:P, 0:EC], field[:, n % NEC, :], ident[0:EC, 0:EC]).then_inc(turned, 1)
            pe.wait_ge(touched, 1)
            nc.tensor.matmul(before[0:P, 0:ET], tri[0:P, 0:P], touch[:], start=True, stop=True)
            nc.tensor.matmul(tiles_sum[0:P, 0:ET], ones[0:P, 0:P], touch[:], start=True, stop=True).then_inc(counted, 1)

        @block.vector
        def _(dve):
            vec.memset(ones[:], 1.0)
            vec.memset(one[:], 1.0)
            dve.wait_ge(landed, 16 * 7)
            for n in ("src", "dst"):
                vec.tensor_copy(f[n][:], raw[n][:])
            dve.drain()
            dve.nop().then_inc(floats, 1)
            for n in range(3 * NEC):
                dve.wait_ge(turned, n + 1)
                c = n % NEC
                vec.tensor_copy(rec[:, c * EC:c * EC + EC, n // NEC], pst[n % 2][0:P, 0:EC]).then_inc(copied, 1)
            dve.drain()
            vec.tensor_tensor(touch[:], rec[:, :, 0], rec[:, :, 1], ALU.min)
            vec.tensor_scalar(number[:], iota[0:P, 0:ET], float(P), column[0:P, 0:1], ALU.mult, ALU.add)
            dve.drain()
            vec.tensor_scalar(touch[:], touch[:], float(D), None, ALU.is_lt)
            dve.drain()
            dve.nop().then_inc(touched, 1)
            dve.wait_ge(counted, 1)
            vec.tensor_tensor_scan(through[:], one[:], tiles_sum[0:P, 0:ET], 0.0, ALU.mult, ALU.add)
            dve.drain()
            vec.tensor_tensor(place[:], through[:], tiles_sum[0:P, 0:ET], ALU.subtract)
            dve.drain()
            vec.tensor_tensor(place[:], place[:], before[0:P, 0:ET], ALU.add)
            vec.tensor_scalar(need[:], through[0:1, ET - 1:ET], 1.0 / (2 * G * K),
                              (3 * G * K - 1) / (2 * G * K) - 0.5 + 1 / 1024, ALU.mult, ALU.add)
            dve.drain()
            vec.tensor_tensor(others[:], number[:], place[:], ALU.subtract)
            vec.tensor_scalar(need[:], need[:], ROUND, None, ALU.add)
            dve.drain()
            vec.tensor_scalar(others[:], others[:], through[:, ET - 1:ET], None, ALU.add)
            vec.tensor_scalar(need[:], need[:], -ROUND, None, ALU.add)
            dve.drain()
            vec.tensor_copy(turns[:], need[:])
            vec.tensor_tensor(place[:], place[:], others[:], ALU.subtract)
            dve.drain()
            vec.tensor_tensor(place[:], place[:], touch[:], ALU.mult)
            dve.drain()
            vec.tensor_tensor(place[:], place[:], others[:], ALU.add)
            dve.drain()
            vec.tensor_copy(row[:], place[:])
            dve.drain()
            dve.nop().then_inc(placed, 1)

        @block.gpsimd
        def _(pool):
            pool.wait_ge(placed, 1)
            pool.nop().then_inc(nopped, 1)

            def scatter(first, q, parts):
                nc.gpsimd.tensor_copy(at[:, q], row[:, bass.ds(first, S8)])
                nc.gpsimd.tensor_copy(out[:, q], rec[:, bass.ds(first, S8), :]).then_inc(listed, 1)
                pool.wait_ge(listed, parts)
                pool.nop().then_inc(nopped, 1)
                for j in range(S8):
                    nc.gpsimd.indirect_dma_start(
                        out=dr["ordered"], out_offset=bass.IndirectOffsetOnAxis(ap=at[:, q, j:j + 1], axis=0),
                        in_=out[:, q, j, :], in_offset=None).then_inc(moved[q], 16)
            for q in range(2):
                scatter(q * S8, q, q + 1)
            with pool.Fori(0, ET // (2 * S8) - 1) as i:
                for q in range(2):
                    pool.wait_ge(moved[q], (i + 1) * (16 * S8))
                    pool.nop().then_inc(nopped, 1)
                    scatter((i + 1) * (2 * S8) + q * S8, q, 2 * i + q + 3)
            for q in range(2):
                pool.wait_ge(moved[q], 16 * ET // 2)


def layer0_prepare(nc, mem, dr, col):
    W = CA * K
    st, th = mem.sb("st", [CP, W, 3]), mem.sb("th", [CP, W])
    fi, fj = mem.sb("fi", [CP, W]), mem.sb("fj", [CP, W])
    k1, k2, y1, y2 = (mem.sb(n, [CP, W]) for n in ("k1", "k2", "y1", "y2"))
    sn, cs, v1, v2 = (mem.sb(n, [CP, W]) for n in ("sn", "cs", "v1", "v2"))
    pk = mem.sb("pk", [CP, 4, CA, R])
    rh = mem.sb("rh", [CP, CA, R])
    ident = mem.sb("ident0", [128, 128])
    pst = [mem.ps(f"t0{q}", [128, 4, 128]) for q in range(2)]
    blank, landed, angles, sines = mem.sem("blank"), mem.sem("landed"), mem.sem("angles"), mem.sem("sines")
    packed, stored, turned, copied = mem.sem("packed"), mem.sem("stored"), mem.sem("turned"), mem.sem("copied")
    full, rest = CP - 1, E - (CP - 1) * W
    vec = nc.vector

    def steps(t):
        return t[:].rearrange("p (a k) -> p a k", k=K)

    with nc.Block() as block:
        @block.sync
        def _(sp):
            sp.wait_ge(blank, 1)
            steps_in = dr["ordered"][0:full * W, :].rearrange("(p w) c -> p w c", w=W)
            sp.dma_start(st[0:full, :, :], steps_in).then_inc(landed, 16)
            steps_in = dr["ordered"][full * W:E, :].rearrange("(p w) c -> p w c", p=1)
            sp.dma_start(st[full:CP, 0:rest, :], steps_in).then_inc(landed, 16)
            sp.dma_start(ident[:], dr["c_ident"]).then_inc(landed, 16)
            sp.wait_ge(packed, 1)
            sp.dma_start(dr["rho"][0:NCH, :].rearrange("(p a) r -> p (a r)", a=CA),
                         rh[:].rearrange("p a r -> p (a r)")).then_inc(stored, 16)
            sp.wait_ge(packed, 2)
            sp.dma_start(dr["rho"][NCH:NCOL, :], fi[0:NCOL - NCH, 0:R]).then_inc(stored, 16)
            sp.wait_ge(stored, 32)

        @block.vector
        def _(dve):
            vec.memset(st[:], 9999.0).then_inc(blank, 1)
            dve.wait_ge(landed, 16 * 3)
            vec.tensor_copy(fi[:], st[:, :, 0])
            vec.tensor_copy(fj[:], st[:, :, 1])
            vec.tensor_copy(th[:], st[:, :, 2])
            dve.drain()
            vec.tensor_scalar(k1[:], th[:], 1 / (2 * np.pi), ROUND, ALU.mult, ALU.add)
            vec.tensor_scalar(k2[:], th[:], 1 / (2 * np.pi), 0.25, ALU.mult, ALU.add)
            dve.drain()
            vec.tensor_scalar(k2[:], k2[:], ROUND, None, ALU.add)
            vec.tensor_scalar(k1[:], k1[:], -ROUND, None, ALU.add)
            dve.drain()
            vec.tensor_scalar(k2[:], k2[:], -ROUND, None, ALU.add)
            vec.scalar_tensor_tensor(y1[:], k1[:], -TWO_PI_HI, th[:], ALU.mult, ALU.add)
            dve.drain()
            vec.scalar_tensor_tensor(y2[:], k2[:], -TWO_PI_HI, th[:], ALU.mult, ALU.add)
            vec.scalar_tensor_tensor(v1[:], k1[:], -TWO_PI_LO, y1[:], ALU.mult, ALU.add)
            dve.drain()
            vec.tensor_scalar(y2[:], y2[:], float(np.pi / 2), None, ALU.add)
            vec.tensor_scalar(y1[:], v1[:], PI_SAFE, -PI_SAFE, ALU.min, ALU.max)
            dve.drain()
            vec.scalar_tensor_tensor(v2[:], k2[:], -TWO_PI_LO, y2[:], ALU.mult, ALU.add)
            dve.drain()
            vec.tensor_scalar(y2[:], v2[:], PI_SAFE, -PI_SAFE, ALU.min, ALU.max).then_inc(angles, 1)
            vec.tensor_scalar(rh[:, :, 0:K], steps(fi), 255.0, None, ALU.min)
            vec.tensor_scalar(rh[:, :, K:R], steps(fj), 255.0, None, ALU.min).then_inc(packed, 1)
            dve.drain()
            vec.tensor_tensor(v1[:], fi[:], fj[:], ALU.not_equal)
            vec.tensor_scalar(v2[:], fj[:], 256.0, None, ALU.is_lt)
            dve.drain()
            vec.scalar_tensor_tensor(k1[:], fi[:], 256.0, v1[:], ALU.is_lt, ALU.mult)
            vec.scalar_tensor_tensor(k2[:], fj[:], 1.0, v2[:], ALU.add, ALU.mult)
            dve.drain()
            vec.scalar_tensor_tensor(v1[:], fi[:], 1.0, k1[:], ALU.add, ALU.mult)
            for side in range(2):
                vec.tensor_scalar(pk[:, 2, :, side * K:side * K + K], steps(k2), -1.0, None, ALU.add)
            dve.drain()
            for side in range(2):
                vec.tensor_scalar(pk[:, 0, :, side * K:side * K + K], steps(v1), -1.0, None, ALU.add)
            vec.memset(fi[:], 0.0)
            vec.memset(col[:, :, NCH:NCOL], -1.0)
            dve.drain()
            for kind in (1, 3):
                vec.memset(col[:, kind, NCH:NCOL], 0.0)
            dve.drain()
            dve.nop().then_inc(packed, 1)
            dve.wait_ge(sines, 2)
            vec.tensor_scalar(pk[:, 1, :, 0:K], steps(cs), -1.0, None, ALU.add)
            vec.tensor_scalar(pk[:, 1, :, K:R], steps(sn), -1.0, None, ALU.mult)
            vec.tensor_copy(pk[:, 3, :, 0:K], steps(sn))
            vec.tensor_scalar(pk[:, 3, :, K:R], steps(cs), -1.0, None, ALU.add)
            dve.drain()
            dve.nop().then_inc(packed, 1)
            for a in range(CA):
                dve.wait_ge(turned, a + 1)
                vec.tensor_copy(col[:, :, a:NCH:CA], pst[a % 2][:, :, 0:CP]).then_inc(copied, 1)

        @block.scalar
        def _(act):
            act.wait_ge(angles, 1)
            nc.scalar.activation(sn[:], y1[:], ACT.Sin).then_inc(sines, 1)
            nc.scalar.activation(cs[:], y2[:], ACT.Sin).then_inc(sines, 1)

        @block.tensor
        def _(pe):
            pe.wait_ge(packed, 3)
            pe.wait_ge(landed, 16 * 3)
            for a in range(CA):
                if a >= 2:
                    pe.wait_ge(copied, a - 1)
                for kind in range(4):
                    last = nc.tensor.transpose(pst[a % 2][:, kind, 0:CP], pk[:, kind, a, :], ident[0:CP, 0:CP])
                last.then_inc(turned, 1)


def layer0_turn(nc, mem, dr, col, turns, mt):
    masks = mem.sb("masks", [128, LV + 1, G, 128])
    ident = mem.sb("ident1", [128, 128])
    iota = mem.sb("iota1", [128, 512])
    column = mem.sb("column1", [128, 3])
    rb = [mem.sb(f"rb{q}", [128, G, R]) for q in range(2)]
    sc = mem.sb("sc", [128, 4, G])
    lta, ltb, lt = mem.sb("lta", [128, G, R]), mem.sb("ltb", [128, G, R]), mem.sb("lt", [128, G, R])
    wta, wtb = mem.sb("wta", [128, G, D]), mem.sb("wtb", [128, G, D])
    wt = [mem.sb(f"wt{q}", [128, G, D]) for q in range(2)]
    lm = [mem.sb(f"lm{q}", [128, LV, G, R]) for q in range(2)]
    st = [mem.sb(f"st{q}", [128, 2, G, R]) for q in range(2)]
    wx = [mem.sb(f"wx{q}", [128, G, D]) for q in range(2)]
    xt = [mem.sb(f"xt{q}", [128, G, R]) for q in range(2)]
    xx = [mem.sb(f"xx{q}", [128, G, R]) for q in range(2)]
    ysb = mem.sb("ysb", [128, G, R])
    rs = mem.sb("rs", [128, D])
    m = mem.sb("m", [128, 2, D])
    psy, psz = ([mem.ps(f"{n}{h}") for h in range(2)] for n in ("y", "z"))
    psr, psu = mem.ps("r"), mem.ps("u")
    psw = mem.ps("w", [128, G, D])
    sems = {n: mem.sem(n) for n in (
        "consts", "levels", "all_in", "rb_in0", "rb_in1", "rb_free", "lt_made", "lt_masked", "w_parts", "w_made", "st_made",
        "x_made", "y_made", "y_copied", "z_made", "x_grown", "wx_made", "wx_copied", "r_made", "r_copied", "u_made",
        "m_grown", "m_turned")}
    vec = nc.vector
    W2 = G // 2 * R

    def half(t, h):
        return t[:].rearrange("p g r -> p (g r)")[:, W2 * h:W2 * h + W2]

    def chunks(h):
        return range(G // 2 * h, G // 2 * h + G // 2)

    with nc.Block() as block:
        @block.sync
        def _(sp):
            sp.dma_start(masks[:], dr["c_masks"]).then_inc(sems["consts"], 16)
            sp.dma_start(ident[:], dr["c_ident"]).then_inc(sems["consts"], 16)
            sp.dma_start(iota[:], dr["c_iota"]).then_inc(sems["consts"], 16)
            sp.dma_start(column[:], dr["c_column"]).then_inc(sems["consts"], 16)

            def load(group, q):
                rows = dr["rho"].rearrange("c r -> (c r)")[bass.ds(group * (G * R), G * R)]
                sp.dma_start(rb[q][:].rearrange("p g r -> p (g r)"), rows.partition_broadcast(128)).then_inc(
                    (sems["rb_in0"], sems["rb_in1"])[q], 16)
            load(0, 0)
            load(1, 1)
            need = sp.value_load(turns[:], min_val=1, max_val=STAGES // 2)
            with sp.Fori(0, STAGES // 2) as i:
                with sp.If(i < need):
                    for u in range(2):
                        sp.wait_ge(sems["rb_free"], 2 * i + u + 1)
                        if u == 0:
                            load(2 * i + 2, 0)
                        else:
                            load(2 * i + 3, 1)
            sp.wait_ge(sems["rb_in0"], need * 16 + 16)
            sp.nop().then_inc(sems["all_in"], 1)
            sp.wait_ge(sems["rb_in1"], need * 16 + 16)
            sp.nop().then_inc(sems["all_in"], 1)

        @block.vector
        def _(dve):
            def build(group, q, landed, parts):
                if 0 in parts:
                    dve.wait_ge((sems["rb_in0"], sems["rb_in1"])[q], landed)
                    vec.tensor_copy(sc[:], col[:, :, bass.ds(group * G, G)])
                    dve.drain()
                    if not isinstance(group, int):
                        dve.wait_ge(sems["w_made"], group)
                for g in parts:
                    a = (sc[:, 0, g:g + 1], sc[:, 1, g:g + 1], ALU.is_equal, ALU.mult)
                    b = (sc[:, 2, g:g + 1], sc[:, 3, g:g + 1], ALU.is_equal, ALU.mult)
                    vec.tensor_scalar(lta[:, g, :], rb[q][:, g, :], *a)
                    vec.tensor_scalar(ltb[:, g, :], rb[q][:, g, :], *b)
                    vec.tensor_scalar(wta[:, g, :], iota[:, 0:D], *a)
                    last = vec.tensor_scalar(wtb[:, g, :], iota[:, 0:D], *b)
                if G - 1 in parts:
                    last.then_inc(sems["w_parts"], 1)
                    dve.drain()
                    if not isinstance(group, int):
                        dve.wait_ge(sems["lt_masked"], group)
                    vec.tensor_tensor(lt[:], lta[:], ltb[:], ALU.add).then_inc(sems["lt_made"], 1)

            def pick(q):
                vec.tensor_scalar(st[q][:, 0], rb[q][:], column[:, 0:1], None, ALU.is_equal)
                vec.tensor_scalar(st[q][:, 1], rb[q][:], column[:, 1:2], None, ALU.is_equal)
                dve.drain()
                dve.nop().then_inc(sems["st_made"], 1)
                dve.nop().then_inc(sems["rb_free"], 1)

            def grow_x(k, q, lv, h):
                dve.wait_ge(sems["z_made"], k * (2 * (LV - 1)) + 2 * lv - 1 + h)
                last = vec.tensor_tensor(half(xx[q], h), psz[h][:, 0:W2], half(xx[q], h), ALU.add)
                if lv < LV - 1:
                    last = vec.tensor_tensor(half(xt[q], h), psz[h][:, W2:2 * W2], half(xt[q], h), ALU.add)
                last.then_inc(sems["x_grown"], 1)
                dve.drain()

            def grow_m(k, c):
                dve.wait_ge(sems["u_made"], k * G + c + 1)
                vec.tensor_tensor(m[:].rearrange("p h c -> p (h c)"), psu[:], m[:].rearrange("p h c -> p (h c)"),
                                  ALU.add).then_inc(sems["m_grown"], 1)
                dve.drain()

            dve.wait_ge(sems["consts"], 64)
            vec.memset(m[:], 0.0)
            for q in range(2):
                vec.memset(st[q][:], 0.0)
                vec.memset(wx[q][:], 0.0)
            dve.drain()
            for h in range(2):
                vec.tensor_copy(m[:, h, 128 * h:128 * h + 128], ident[:])
            dve.drain()
            dve.nop().then_inc(sems["m_grown"], 1)
            dve.nop().then_inc(sems["st_made"], 1)
            for h in range(2):
                dve.nop().then_inc(sems["x_grown"], 1)
            build(0, 0, 16, range(G))
            need = dve.value_load(turns[:], min_val=1, max_val=STAGES // 2)
            with dve.Fori(0, STAGES // 2) as i:
                with dve.If(i < need):
                    for u in range(2):
                        k = 2 * i + u
                        landed = i * 16 + 16 + 16 * u
                        for lv in range(1, LV - 1):
                            if lv < LV - 2:
                                build(k + 1, 1 - u, landed, ((0, 1), (2,), (3,))[lv - 1])
                            for h in range(2):
                                grow_x(k, u, lv, h)
                            grow_m(k, lv - 1)
                        pick(u)
                        for h in range(2):
                            grow_x(k, u, 5, h)
            for kh in range(2):
                dve.wait_ge(sems["m_turned"], kh + 1)
                vec.tensor_copy(mt[:, kh, :], psy[kh][:, 0:D])

        @block.gpsimd
        def _(pool):
            tt = nc.gpsimd.tensor_tensor

            def mask(j, q):
                pool.wait_ge(sems["lt_made"], j + 1)
                pool.wait_ge(sems["wx_made"], j if not isinstance(j, int) else 1)
                tt(lm[q][:, 0], lt[:], masks[:, 0], ALU.mult).then_inc(sems["levels"], 1)
                for lv in range(1, LV):
                    last = tt(lm[q][:, lv], lt[:], masks[:, lv], ALU.mult)
                last.then_inc(sems["lt_masked"], 1)
                pool.wait_ge(sems["levels"], j + 1)
                tt(xt[q][:], lm[q][:, 0], masks[:, LV], ALU.add).then_inc(sems["x_made"], 1)
                pool.wait_ge(sems["w_parts"], j + 1)
                tt(wt[q][:], wta[:], wtb[:], ALU.add).then_inc(sems["w_made"], 1)

            pool.wait_ge(sems["consts"], 64)
            pool.nop().then_inc(sems["wx_made"], 1)
            mask(0, 0)
            need = pool.value_load(turns[:], min_val=1, max_val=STAGES // 2)
            with pool.Fori(0, STAGES // 2) as i:
                with pool.If(i < need):
                    for u in range(2):
                        mask(2 * i + u + 1, 1 - u)

        @block.scalar
        def _(act):
            for h in range(2):
                act.nop().then_inc(sems["y_copied"], 1)
            act.nop().then_inc(sems["wx_copied"], 1)

            def copy_y(k, n, q):
                for h in range(2):
                    act.wait_ge(sems["y_made"], k * (2 * LV) + 2 * n + h + 1)
                    nc.scalar.copy(half(xx[q] if n == 0 else ysb, h), psy[h][:, 0:W2]).then_inc(sems["y_copied"], 1)

            def copy_r(k, c):
                act.wait_ge(sems["r_made"], k * G + c + 1)
                nc.scalar.copy(rs[:], psr[:, 0:D]).then_inc(sems["r_copied"], 1)

            copy_y(0, 0, 0)
            need = act.value_load(turns[:], min_val=1, max_val=STAGES // 2)
            with act.Fori(0, STAGES // 2) as i:
                with act.If(i < need):
                    for u in range(2):
                        k = 2 * i + u
                        for lv in range(1, LV):
                            copy_y(k, lv, u)
                            if lv <= G:
                                copy_r(k, lv - 1)
                        copy_y(k + 1, 0, 1 - u)
                        act.wait_ge(sems["wx_made"], k + 2)
                        for h in range(2):
                            last = nc.scalar.copy(wx[u][:, 2 * h:2 * h + 2, :], psw[:, 2 * h:2 * h + 2, :])
                        last.then_inc(sems["wx_copied"], 1)

        @block.tensor
        def _(pe):
            mm = nc.tensor.matmul

            def start_x(k, q):
                pe.wait_ge(sems["x_made"], k + 1)
                for h in range(2):
                    pe.wait_ge(sems["y_copied"], k * (2 * LV) + h + 1)
                    for n, g in enumerate(chunks(h)):
                        last = nc.tensor.transpose(psy[h][:, n * R:n * R + R], xt[q][:, g, :], ident[:])
                    last.then_inc(sems["y_made"], 1)

            def make_y(k, q, lv):
                if lv == 1:
                    pe.wait_ge(sems["lt_masked"], k + 1)
                for h in range(2):
                    if lv > 1:
                        pe.wait_ge(sems["x_grown"], k * (2 * (LV - 1)) + 2 * lv - 1 + h)
                    pe.wait_ge(sems["y_copied"], k * (2 * LV) + 2 * lv + h + 1)
                    for n, g in enumerate(chunks(h)):
                        last = mm(psy[h][:, n * R:n * R + R], lm[q][:, lv, g, :], xx[q][:, g, :], start=True, stop=True)
                    last.then_inc(sems["y_made"], 1)

            def make_z(k, q, lv):
                for h in range(2):
                    pe.wait_ge(sems["y_copied"], k * (2 * LV) + 2 * lv + h + 3)
                    if lv == 1:
                        pe.wait_ge(sems["x_grown"], k * (2 * (LV - 1)) + 1 + h)
                    for n, g in enumerate(chunks(h)):
                        last = mm(psz[h][:, n * R:n * R + R], xt[q][:, g, :], ysb[:, g, :], start=True, stop=True)
                    if lv < LV - 1:
                        for n, g in enumerate(chunks(h)):
                            last = mm(psz[h][:, W2 + n * R:W2 + n * R + R], ysb[:, g, :], xt[q][:, g, :], start=True, stop=True)
                    last.then_inc(sems["z_made"], 1)

            def make_r(k, q, c):
                pe.wait_ge(sems["m_grown"], k * G + c + 1)
                if c == 0:
                    pe.wait_ge(sems["st_made"], k + 1)
                for h in range(2):
                    last = mm(psr[:, 0:D], st[q][:, h, c, :], m[:, h, :], start=(h == 0), stop=(h == 1))
                last.then_inc(sems["r_made"], 1)

            def make_u(k, q, c):
                pe.wait_ge(sems["r_copied"], k * G + c + 1)
                if c == 0:
                    pe.wait_ge(sems["wx_copied"], k + 1)
                for h in range(2):
                    last = mm(psu[:, h * D:h * D + D], wx[q][:, c, 128 * h:128 * h + 128], rs[:], start=True, stop=True)
                last.then_inc(sems["u_made"], 1)

            pe.wait_ge(sems["consts"], 64)
            start_x(0, 0)
            need = pe.value_load(turns[:], min_val=1, max_val=STAGES // 2)
            with pe.Fori(0, STAGES // 2) as i:
                with pe.If(i < need):
                    for u in range(2):
                        k = 2 * i + u
                        for lv in range(1, LV):
                            make_y(k, u, lv)
                            if lv <= G:
                                make_r(k, 1 - u, lv - 1)
                            make_z(k, u, lv)
                            if lv <= G:
                                make_u(k, 1 - u, lv - 1)
                        start_x(k + 1, 1 - u)
                        pe.wait_ge(sems["x_grown"], k * (2 * (LV - 1)) + 2 * LV)
                        pe.wait_ge(sems["w_made"], k + 1)
                        pe.wait_ge(sems["wx_copied"], k + 1)
                        for g in range(G):
                            last = mm(psw[:, g, :], xx[u][:, g, :], wt[u][:, g, :], start=True, stop=True)
                        last.then_inc(sems["wx_made"], 1)
            pe.wait_ge(sems["m_grown"], need * (2 * G) + 1)
            pe.wait_ge(sems["y_copied"], need * (4 * LV) + 4)
            for kh in range(2):
                for h in range(2):
                    last = nc.tensor.transpose(psy[kh][:, 128 * h:128 * h + 128],
                                               m[:, h, 128 * kh:128 * kh + 128], ident[:])
                last.then_inc(sems["m_turned"], 1)


U = 16
HF = 4
Q4 = U // HF
KS = -(-(ET + NT - 1) // U) * U
NODE_SHIFT = 0.5 / P - 0.5


def edge_lists(mem):
    shape = [EC, NEC, P]
    k = {n: mem.sb("k_" + n, shape) for n in ("nf", "nb", "nfirst", "nlast")}
    k["member"] = mem.sb("k_member", [EC, NEC, KS])
    k["nk"] = mem.sb("k_nk", [1, KS], I32)
    k["part"] = mem.sb("k_part", [1, KS // HF, 2], I32)
    k["etile"] = mem.sb("k_etile", [1, KS + U], I32)
    k["cut"] = mem.sb("k_cut", [P, KS])
    k["dloc"] = mem.sb("k_dloc", [P, KS + U])
    k["w"] = mem.sb("k_w", [P, KS + U, 4])
    for n in ("row_step", "src_step"):
        k[n] = mem.sb("k_" + n, [P, KS], I32)
    for n in ("row_tile", "src_tile", "dst_tile"):
        k[n] = mem.sb("k_" + n, [P, ET], I32)
    k["q_row"] = mem.sb("k_q_row", [P, NT], I32)
    k["first"] = mem.sb("k_first", [EC, NEC, 2], I32)
    k["type"] = mem.sb("k_type", shape)
    k["ncont"] = mem.sb("k_ncont", [4, ET + 1])
    k["ntile"] = mem.sb("k_ntile", [4, 2, ET])
    return k


def edge_order(nc, mem, dr, keep):
    shape = [EC, NEC, P]
    zeros = mem.sb("zeros", [P, E // P * 8])
    NB = 5
    lasts, less = mem.sb("lasts", [P, ET]), mem.sb("less", [P, NB, ET])
    near_i, near = mem.sb("near_i", [P, NT, P], I32), mem.sb("near", [P, NT, P])
    node, tile_of, clamped = (mem.sb(n, [P, NT]) for n in ("node", "tile_of", "clamped"))
    lower, equal, tile_i = mem.sb("lower", [P, NT]), mem.sb("equal", [P, NT]), mem.sb("tile_i", [P, NT], I32)
    blank, found, near_in = mem.sem("o_blank"), mem.sem("o_found"), mem.sem("o_near_in")
    ints = {n: mem.sb("i_" + n, shape, I32) for n in ("src", "dst", "edge_type_2")}
    f = {n: mem.sb("f_" + n, shape) for n in ints}
    ew, row, d1, tmp, tmp2 = (mem.sb(n, shape) for n in ("ew", "row", "d1", "tmp", "tmp2"))
    cut, one = mem.sb("cut", shape), mem.sb("one", shape)
    lo, hi, cnt, start, end, gap = (mem.sb(n, [EC, NEC]) for n in ("lo", "hi", "cnt", "start", "end", "gap"))
    gapb, eid = mem.sb("gapb", shape), mem.sb("eid", shape)
    column = mem.sb("column", [128, 3])
    ident, tri, ones = mem.sb("ident2", [128, 128]), mem.sb("tri", [128, 128]), mem.sb("ones2", [128, 128])
    iota = mem.sb("iota2", [128, 512])
    at_or_past = mem.sb("atp", [EC, NEC, KS])
    nk, valid, steps = mem.sb("nk", [P, KS]), mem.sb("valid", [P, KS]), mem.sb("stepf", [P, KS])
    edges = mem.sb("edges", [4, 2, ET])
    cont, single, both = mem.sb("cont", [4, ET + 1]), mem.sb("single", [4, ET]), mem.sb("both", [4, 2, ET])
    ps_start, pst, pss = mem.ps("start"), [mem.ps(f"t2{q}") for q in range(2)], [mem.ps(f"s2{q}") for q in range(2)]
    landed, floats, counted, placed = (mem.sem("o_" + n) for n in ("landed", "floats", "counted", "placed"))
    stored, back, turned, copied = (mem.sem("o_" + n) for n in ("stored", "back", "turned", "copied"))
    member, summed, taken, cosine = (mem.sem("o_" + n) for n in ("member", "summed", "taken", "cosine"))
    vec = nc.vector

    def tiles(name):
        return dr[name].rearrange("(c p l) -> p c l", p=EC, l=P)

    with nc.Block() as block:
        @block.sync
        def _(sp):
            for n, t in list(ints.items()) + [("edge_weight", ew)]:
                sp.dma_start(t[:], tiles(n)).then_inc(landed, 16)
            sp.dma_start(ident[:], dr["c_ident"]).then_inc(landed, 16)
            sp.dma_start(tri[:], dr["c_tri"]).then_inc(landed, 16)
            sp.dma_start(iota[:], dr["c_iota"]).then_inc(landed, 16)
            sp.dma_start(column[:], dr["c_column"]).then_inc(landed, 16)
            sp.wait_ge(floats, 1)
            with nc.allow_non_contiguous_dma(reason="one word per edge tile"):
                sp.dma_start(dr["ends"][0].rearrange("(c p) -> p c", p=EC), f["dst"][:, :, 0]).then_inc(stored, 16)
                sp.dma_start(dr["ends"][1].rearrange("(c p) -> p c", p=EC), f["dst"][:, :, P - 1]).then_inc(stored, 16)
            sp.wait_ge(stored, 32)
            sp.dma_start(edges[:].rearrange("h s e -> h (s e)"),
                         dr["ends"].rearrange("s e -> (s e)").partition_broadcast(4)).then_inc(back, 16)
            sp.dma_start(lasts[:], dr["ends"][1].partition_broadcast(P)).then_inc(back, 16)
            sp.wait_ge(blank, 1)
            for name, w in (("qe", 8), ("qe1", 2)):
                sp.dma_start(dr[name][0:E, :].rearrange("(p r) s -> p (r s)", p=P), zeros[:, 0:E // P * w]).then_inc(stored, 16)
            sp.wait_ge(stored, 64)

        @block.gpsimd
        def _(pool):
            pool.wait_ge(found, 1)
            for t in range(NT):
                nc.gpsimd.indirect_dma_start(
                    out=near_i[:, t, :], out_offset=None, in_=dr["dst"].rearrange("(e l) -> e l", l=P),
                    in_offset=bass.IndirectOffsetOnAxis(ap=tile_i[:, t:t + 1], axis=0)).then_inc(near_in, 16)

        @block.vector
        def _(dve):
            dve.wait_ge(landed, 16 * 8)
            vec.memset(keep["dloc"][:], -1.0)
            vec.memset(keep["w"][:], 0.0)
            for n in ints:
                vec.tensor_copy(f[n][:], ints[n][:])
            vec.memset(ones[:], 1.0)
            vec.memset(one[:], 1.0)
            vec.memset(keep["etile"][:], 0)
            vec.memset(zeros[:], 0.0).then_inc(blank, 1)
            vec.tensor_scalar(node[:], iota[0:P, 0:NT], float(P), column[0:P, 0:1], ALU.mult, ALU.add)
            dve.drain()
            dve.nop().then_inc(floats, 1)
            vec.tensor_copy(keep["type"][:], f["edge_type_2"][:])
            vec.tensor_copy(keep["first"][:, :, 0], f["dst"][:, :, 0])
            vec.tensor_scalar(keep["first"][:, :, 1], f["dst"][:, :, 0], float(N), None, ALU.add)
            dve.wait_ge(back, 32)
            for b in range(0, NT, NB):
                for t in range(NB):
                    vec.tensor_scalar(less[:, t], lasts[:], node[:, b + t:b + t + 1], None, ALU.is_lt)
                dve.drain()
                vec.tensor_reduce(tile_of[:, b:b + NB], less[:], AX.X, ALU.add)
                dve.drain()
            vec.tensor_scalar(clamped[:], tile_of[:], float(ET - 1), None, ALU.min)
            dve.drain()
            vec.tensor_copy(tile_i[:], clamped[:])
            dve.drain()
            dve.nop().then_inc(found, 1)
            fd = f["dst"]
            vec.scalar_tensor_tensor(row[:], f["edge_type_2"][:], float(N), f["src"][:], ALU.mult, ALU.add)
            vec.tensor_scalar(d1[:], fd[:], 1.0, None, ALU.add)
            vec.tensor_scalar(lo[:], fd[:, :, 0], 1.0 / P, NODE_SHIFT, ALU.mult, ALU.add)
            vec.tensor_scalar(hi[:], fd[:, :, P - 1], 1.0 / P, NODE_SHIFT, ALU.mult, ALU.add)
            dve.drain()
            vec.tensor_scalar(lo[:], lo[:], ROUND, -ROUND, ALU.add, ALU.add)
            vec.tensor_scalar(hi[:], hi[:], ROUND, -ROUND, ALU.add, ALU.add)
            dve.drain()
            vec.tensor_tensor(cnt[:], hi[:], lo[:], ALU.subtract)
            dve.drain()
            vec.tensor_scalar(cnt[:], cnt[:], 1.0, None, ALU.add)
            dve.drain()
            dve.nop().then_inc(counted, 1)
            nf, nb, nfirst, nlast = (keep[n] for n in ("nf", "nb", "nfirst", "nlast"))
            for t in (nf, nb):
                vec.memset(t[:], 0.0)
            dve.drain()
            vec.tensor_tensor(nf[:, :, 1:P], fd[:, :, 1:P], fd[:, :, 0:P - 1], ALU.not_equal)
            vec.tensor_tensor(nb[:, :, 0:P - 1], fd[:, :, 1:P], fd[:, :, 0:P - 1], ALU.not_equal)
            for c in range(NEC):
                vec.tensor_scalar(nfirst[:, c], fd[:, c], fd[:, c, 0:1], -BIG, ALU.not_equal, ALU.mult)
                vec.tensor_scalar(nlast[:, c], fd[:, c], fd[:, c, P - 1:P], -BIG, ALU.not_equal, ALU.mult)
            dve.drain()
            vec.tensor_scalar(nf[:], nf[:], -BIG, None, ALU.mult)
            vec.tensor_scalar(nb[:], nb[:], -BIG, None, ALU.mult)
            vec.tensor_scalar(tmp[:], ew[:], 0.05, 0.25, ALU.mult, ALU.add)
            dve.drain()
            vec.tensor_scalar(tmp[:], tmp[:], ROUND, None, ALU.add)
            dve.drain()
            vec.tensor_scalar(tmp[:], tmp[:], -ROUND, None, ALU.add)
            vec.tensor_scalar(ew[:], ew[:], float(np.float32(np.pi / 10.0)), float(np.pi / 2), ALU.mult, ALU.add)
            dve.drain()
            vec.scalar_tensor_tensor(tmp2[:], tmp[:], -TWO_PI_HI, ew[:], ALU.mult, ALU.add)
            dve.drain()
            vec.scalar_tensor_tensor(ew[:], tmp[:], -TWO_PI_LO, tmp2[:], ALU.mult, ALU.add)
            dve.drain()
            vec.tensor_scalar(ew[:], ew[:], PI_SAFE, -PI_SAFE, ALU.min, ALU.max)
            dve.drain()
            dve.nop().then_inc(cosine, 1)
            dve.wait_ge(placed, 1)
            vec.tensor_copy(start[:], ps_start[0:EC, 0:NEC])
            dve.drain()
            vec.tensor_tensor(end[:], start[:], cnt[:], ALU.add)
            vec.tensor_tensor(gap[:], lo[:], start[:], ALU.subtract)
            dve.drain()
            for c in range(NEC):
                vec.tensor_scalar(at_or_past[:, c], iota[0:EC, 0:KS], start[:, c:c + 1], None, ALU.is_ge)
                vec.tensor_scalar(gapb[:, c], one[:, c], gap[:, c:c + 1], None, ALU.mult)
                vec.tensor_scalar(eid[:, c], one[:, c], column[0:EC, 0:1], float(EC * c - 1), ALU.add, ALU.add)
            dve.drain()
            for c in range(NEC):
                vec.scalar_tensor_tensor(keep["member"][:, c], iota[0:EC, 0:KS], end[:, c:c + 1], at_or_past[:, c],
                                         ALU.is_lt, ALU.mult)
            dve.wait_ge(cosine, 2)
            vec.tensor_scalar(cut[:], cut[:], 1.0, 0.5, ALU.add, ALU.mult)
            dve.drain()
            dve.nop().then_inc(member, 1)
            for n, dst in enumerate((nk, valid, steps, None, None, keep["cut"], None)):
                dve.wait_ge(summed, n + 1)
                ps = pss[n % 2][0:P, 0:KS]
                if n == 0:
                    vec.tensor_tensor(nk[:], ps, iota[0:P, 0:KS], ALU.add).then_inc(taken, 1)
                elif n == 1:
                    vec.tensor_copy(valid[:], ps).then_inc(taken, 1)
                    dve.drain()
                    vec.tensor_tensor(nk[:], nk[:], valid[:], ALU.mult)
                    vec.tensor_scalar(valid[:], valid[:], float(1 - NT), float(NT - 1), ALU.mult, ALU.add)
                    dve.drain()
                    vec.tensor_tensor(nk[:], nk[:], valid[:], ALU.add)
                    dve.drain()
                    vec.tensor_copy(keep["nk"][:], nk[0:1, :])
                    vec.tensor_copy(keep["part"][:, :, 0], nk[0:1, 0:KS:HF])
                    vec.tensor_tensor(keep["part"][:, :, 1], nk[0:1, HF - 1:KS:HF], nk[0:1, 0:KS:HF], ALU.subtract)
                elif n == 2:
                    vec.scalar_tensor_tensor(steps[:], nk[:], -float(P), ps, ALU.mult, ALU.add).then_inc(taken, 1)
                    dve.drain()
                    vec.tensor_scalar(keep["dloc"][:, 0:KS], steps[:], -1.0, None, ALU.add)
                elif n == 6:
                    vec.tensor_copy(keep["etile"][0:1, 0:KS], ps[0:1, :]).then_inc(taken, 1)
                elif n in (3, 4):
                    vec.tensor_copy(keep[("row_step", "src_step")[n - 3]][:], ps).then_inc(taken, 1)
                else:
                    vec.tensor_copy(dst[:], ps).then_inc(taken, 1)
            for n in range(3 * NEC):
                dve.wait_ge(turned, n + 1)
                name = ("row_tile", "src_tile", "dst_tile")[n // NEC]
                c = n % NEC
                vec.tensor_copy(keep[name][:, c * EC:c * EC + EC], pst[n % 2][0:P, 0:EC]).then_inc(copied, 1)
            dve.wait_ge(near_in, 16 * NT)
            vec.tensor_copy(near[:], near_i[:])
            dve.drain()
            for sums, op in ((lower, ALU.is_lt), (equal, ALU.is_equal)):
                for b in range(0, NT, NB):
                    for t in range(NB):
                        vec.tensor_scalar(less[:, t, 0:P], near[:, b + t, :], node[:, b + t:b + t + 1], None, op)
                    dve.drain()
                    vec.tensor_reduce(sums[:, b:b + NB], less[:, :, 0:P], AX.X, ALU.add)
                    dve.drain()
            vec.scalar_tensor_tensor(lower[:], tile_of[:], float(P), lower[:], ALU.mult, ALU.add)
            vec.tensor_scalar(equal[:], equal[:], 0.0, None, ALU.is_gt)
            vec.tensor_scalar(node[:], node[:], float(E), None, ALU.add)
            dve.drain()
            vec.tensor_tensor(lower[:], lower[:], node[:], ALU.subtract)
            dve.drain()
            vec.tensor_tensor(lower[:], lower[:], equal[:], ALU.mult)
            dve.drain()
            vec.tensor_tensor(keep["q_row"][:], lower[:], node[:], ALU.add)
            vec.memset(cont[:], 0.0)
            vec.tensor_tensor(single[:], edges[:, 0, :], edges[:, 1, :], ALU.is_equal)
            dve.drain()
            vec.tensor_tensor(cont[:, 1:ET], edges[:, 1, 0:ET - 1], edges[:, 0, 1:ET], ALU.is_equal)
            dve.drain()
            for s in range(2):
                vec.tensor_tensor(both[:, s], single[:], cont[:, s:ET + s], ALU.mult)
            vec.tensor_scalar(keep["ncont"][:], cont[:], BIG, -BIG, ALU.mult, ALU.add)
            dve.drain()
            for s in range(2):
                vec.tensor_scalar(keep["ntile"][:, s], both[:, s], BIG, -BIG, ALU.mult, ALU.add)

        @block.scalar
        def _(act):
            act.wait_ge(cosine, 1)
            nc.scalar.activation(cut[:], ew[:], ACT.Sin).then_inc(cosine, 1)

        @block.tensor
        def _(pe):
            mm = nc.tensor.matmul
            pe.wait_ge(landed, 16 * 8)
            pe.wait_ge(counted, 1)
            for c in range(NEC):
                last = mm(ps_start[0:EC, c:c + 1], tri[0:EC, 0:EC], cnt[:, c:c + 1], start=True, stop=(c == 0))
                for b in range(c):
                    last = mm(ps_start[0:EC, c:c + 1], ones[0:EC, 0:EC], cnt[:, b:b + 1], start=False, stop=(b == c - 1))
            last.then_inc(placed, 1)
            pe.wait_ge(member, 1)
            for n, src in enumerate((gapb, one, d1, row, f["src"], cut, eid)):
                if n >= 2:
                    pe.wait_ge(taken, n - 1)
                for c in range(NEC):
                    last = mm(pss[n % 2][0:P, 0:KS], src[:, c, :], keep["member"][:, c, :], start=(c == 0), stop=(c == NEC - 1))
                last.then_inc(summed, 1)
            for n in range(3 * NEC):
                src = (row, f["src"], f["dst"])[n // NEC]
                if n >= 2:
                    pe.wait_ge(copied, n - 1)
                nc.tensor.transpose(pst[n % 2][0:P, 0:EC], src[:, n % NEC, :], ident[0:EC, 0:EC]).then_inc(turned, 1)


def attention_weights(nc, mem, dr, keep, heads, layer):
    H = heads
    kt, qt, qe = (dr[n if H == 4 else n + "1"] for n in ("kt", "qt", "qe"))
    idx, gk = mem.sb("idx", [P, U], I32), mem.sb("gk", [P, U, H])
    qn, first = mem.sb("qn", [P, NT, 2, H]), mem.sb("first", [EC, NEC, 2, H])
    qedge = mem.sb("qedge", [EC, 2, P, 2, H])
    same, other = mem.sb("same", [EC, NEC, P]), mem.sb("other", [EC, NEC, P])
    al = mem.sb("al", [P, ET, H])
    a, fw, amax, wt = (mem.sb(n, [EC, NEC, H, P]) for n in ("a", "fw", "amax", "wt"))
    ident = mem.sb("ident3", [128, 128])
    ends = mem.sb("ends", [4, 2, ET])
    state = mem.sb("state", [4, 2, ET])
    carry = mem.sb("carry", [4, 2, ET])
    carried = mem.sb("carried", [EC, 2, NEC, H])
    pst = [mem.ps(f"t3{q}") for q in range(2)]
    psw = [mem.ps(f"w3{q}") for q in range(2)]
    nm = lambda n: mem.sem(f"a{layer}_{n}")
    nopped = nm("nopped")
    listed, k_in, used = nm("listed"), *([nm(f"{n}{q}") for q in range(Q4)] for n in "ku")
    nodes_in, put, first_in, edge_in, spread = (nm(n) for n in ("nodes_in", "put", "first_in", "edge_in", "spread"))
    scored, turned, copied, landed = nm("scored"), nm("turned"), nm("copied"), nm("landed")
    summary, back, ready, exped, summed, taken = (nm(n) for n in ("summary", "back", "ready", "exped", "summed", "taken"))
    vec = nc.vector

    with nc.Block() as block:
        @block.gpsimd
        def _(pool):
            pool.wait_ge(landed, 16)
            pool.wait_ge(nodes_in, 32)
            for t in range(NT):
                nc.gpsimd.indirect_dma_start(
                    out=qe, out_offset=bass.IndirectOffsetOnAxis(ap=keep["q_row"][:, t:t + 1], axis=0),
                    in_=qn[:, t].rearrange("p s h -> p (s h)"), in_offset=None).then_inc(put, 16)
            for c in range(NEC):
                for s in range(2):
                    nc.gpsimd.indirect_dma_start(
                        out=first[:, c, s, :], out_offset=None, in_=qt,
                        in_offset=bass.IndirectOffsetOnAxis(ap=keep["first"][:, c, s:s + 1], axis=0)).then_inc(first_in, 16)
            with pool.Fori(0, ET // U) as i:
                for q in range(Q4):
                    half = slice(HF * q, HF * q + HF)
                    pool.wait_ge(used[q], i + 1)
                    nc.gpsimd.tensor_copy(idx[:, half], keep["row_tile"][:, bass.ds(i * U + HF * q, HF)]).then_inc(listed, 1)
                    pool.wait_ge(listed, Q4 * i + q + 1)
                    pool.nop().then_inc(nopped, 1)
                    for j in range(HF * q, HF * q + HF):
                        nc.gpsimd.indirect_dma_start(
                            out=gk[:, j, :], out_offset=None, in_=kt,
                            in_offset=bass.IndirectOffsetOnAxis(ap=idx[:, j:j + 1], axis=0)).then_inc(k_in[q], 16)

        @block.vector
        def _(dve):
            for q in range(Q4):
                dve.nop().then_inc(used[q], 1)
            vec.tensor_scalar(same[:], keep["nf"][:], 0.0, None, ALU.is_ge)
            vec.tensor_scalar(other[:], keep["type"][:], -1.0, 1.0, ALU.mult, ALU.add)
            dve.wait_ge(first_in, 16 * 2 * NEC)
            for c in range(NEC):
                if c % 2 == 0:
                    dve.wait_ge(edge_in, 32 * (c // 2 + 1))
                    vec.tensor_copy(qedge[:, :, 0], first[:, c:c + 2])
                    dve.drain()
                for s, out in ((0, fw), (1, amax)):
                    for h in range(H):
                        last = vec.tensor_tensor_scan(out[:, c, h], same[:, c], qedge[:, c % 2, :, s, h], 0.0,
                                                      ALU.mult, ALU.add)
                if c == 1:
                    last.then_inc(spread, 1)
            dve.drain()
            for h in range(H):
                vec.tensor_tensor(fw[:, :, h], fw[:, :, h], other[:], ALU.mult)
                vec.tensor_tensor(amax[:, :, h], amax[:, :, h], keep["type"][:], ALU.mult)
            dve.drain()
            vec.tensor_tensor(fw[:], fw[:], amax[:], ALU.add)
            with dve.Fori(0, ET // U) as i:
                for q in range(Q4):
                    dve.wait_ge(k_in[q], (i + 1) * (16 * HF))
                    vec.tensor_copy(al[:, bass.ds(i * U + HF * q, HF), :], gk[:, HF * q:HF * q + HF]).then_inc(used[q], 1)
            dve.drain()
            dve.nop().then_inc(scored, 1)
            for c in range(NEC):
                dve.wait_ge(turned, c + 1)
                vec.tensor_tensor(amax[:, c].rearrange("p h l -> p (h l)"), pst[c % 2][0:EC, 0:H * P],
                                  fw[:, c].rearrange("p h l -> p (h l)"), ALU.add).then_inc(copied, 1)
            dve.drain()
            vec.scalar_tensor_tensor(a[:], amax[:], 0.2, amax[:], ALU.mult, ALU.max)
            dve.drain()
            for c in range(NEC):
                for h in range(H):
                    vec.tensor_tensor_scan(fw[:, c, h], keep["nf"][:, c], a[:, c, h], -BIG, ALU.add, ALU.max)
            dve.drain()
            for c in range(NEC):
                for h in range(H):
                    vec.tensor_tensor_scan(amax[:, c, h, ::-1], keep["nb"][:, c, ::-1], fw[:, c, h, ::-1], -BIG,
                                           ALU.add, ALU.max)
            dve.drain()
            dve.nop().then_inc(summary, 1)
            dve.wait_ge(back, 16 * 2)
            vec.tensor_tensor_scan(state[0:H, 0], keep["ntile"][0:H, 0], ends[0:H, 1], -BIG, ALU.add, ALU.max)
            vec.tensor_tensor_scan(state[0:H, 1, ::-1], keep["ntile"][0:H, 1, ::-1], ends[0:H, 0, ::-1], -BIG,
                                   ALU.add, ALU.max)
            vec.memset(carry[:], -BIG)
            dve.drain()
            vec.tensor_tensor(carry[0:H, 0, 1:ET], state[0:H, 0, 0:ET - 1], keep["ncont"][0:H, 1:ET], ALU.add)
            vec.tensor_tensor(carry[0:H, 1, 0:ET - 1], state[0:H, 1, 1:ET], keep["ncont"][0:H, 1:ET], ALU.add)
            dve.drain()
            dve.nop().then_inc(summary, 1)
            dve.wait_ge(back, 16 * (2 + 2 * NEC))
            for s, mask in ((0, "nfirst"), (1, "nlast")):
                for c in range(NEC):
                    for h in range(H):
                        vec.scalar_tensor_tensor(amax[:, c, h], keep[mask][:, c], carried[:, s, c, h:h + 1],
                                                 amax[:, c, h], ALU.add, ALU.max)
                dve.drain()
            vec.tensor_tensor(fw[:], a[:], amax[:], ALU.subtract).then_inc(ready, 1)
            for h in range(H):
                dve.wait_ge(summed, h + 1)
                vec.tensor_copy(keep["w"][:, 0:KS, h], psw[h % 2][0:P, 0:KS]).then_inc(taken, 1)

        @block.sync
        def _(sp):
            sp.dma_start(ident[:], dr["c_ident"]).then_inc(landed, 16)
            with nc.allow_non_contiguous_dma(reason="one short row per node"):
                for s in range(2):
                    sp.dma_start(qn[:, :, s, :], qt[s * N:s * N + N, :].rearrange("(t p) h -> p t h", p=P)).then_inc(nodes_in, 16)
            sp.wait_ge(put, 16 * NT)
            edges = qe[0:E, :].rearrange("(c p l) s -> p c l s", p=EC, l=P)
            for c in range(0, NEC, 2):
                if c:
                    sp.wait_ge(spread, 1)
                for b in range(2):
                    sp.dma_start(qedge[:, b].rearrange("p l s h -> p (l s h)"),
                                 edges[:, c + b].rearrange("p l s -> p (l s)")).then_inc(edge_in, 16)
            sp.wait_ge(summary, 1)
            cd = dr["carry"]
            with nc.allow_non_contiguous_dma(reason="one word per edge tile and head"):
                for s, lane in ((0, 0), (1, P - 1)):
                    for c in range(NEC):
                        sp.dma_start(cd[s, 0:H, c * EC:c * EC + EC].rearrange("h p -> p h"), amax[:, c, :, lane]).then_inc(
                            landed, 16)
                sp.wait_ge(landed, 16 * (1 + 2 * NEC))
                for s in range(2):
                    sp.dma_start(ends[0:H, s], cd[s, 0:H]).then_inc(back, 16)
                sp.wait_ge(summary, 2)
                for s in range(2):
                    sp.dma_start(cd[2 + s, 0:H], carry[0:H, s]).then_inc(landed, 16)
                sp.wait_ge(landed, 16 * (3 + 2 * NEC))
                for s in range(2):
                    for c in range(NEC):
                        sp.dma_start(carried[:, s, c, :], cd[2 + s, 0:H, c * EC:c * EC + EC].rearrange("h p -> p h")).then_inc(
                            back, 16)

        @block.scalar
        def _(act):
            act.wait_ge(ready, 1)
            nc.scalar.activation(wt[:], fw[:], ACT.Exp).then_inc(exped, 1)

        @block.tensor
        def _(pe):
            pe.wait_ge(landed, 16)
            pe.wait_ge(scored, 1)
            for c in range(NEC):
                if c >= 2:
                    pe.wait_ge(copied, c - 1)
                for h in range(H):
                    last = nc.tensor.transpose(pst[c % 2][0:EC, h * P:h * P + P], al[:, c * EC:c * EC + EC, h],
                                               ident[0:P, 0:P])
                last.then_inc(turned, 1)
            pe.wait_ge(exped, 1)
            for h in range(H):
                if h >= 2:
                    pe.wait_ge(taken, h - 1)
                for c in range(NEC):
                    last = nc.tensor.matmul(psw[h % 2][0:P, 0:KS], wt[:, c, h, :], keep["member"][:, c, :],
                                            start=(c == 0), stop=(c == NEC - 1))
                last.then_inc(summed, 1)


def node_tiles(nc, keep, first, count):
    _, tiles = nc.values_load_multi_w_load_instructions(keep["nk"][0:1, bass.ds(first, count)], engines=(mybir.EngineType.DVE,),
                                                        min_val=0, max_val=NT - 1)
    return tiles


def part_tiles(nc, keep, i, engine):
    parts = keep["part"][:].rearrange("o k s -> o (k s)")
    _, values = nc.values_load_multi_w_load_instructions(parts[:, bass.ds(i * (2 * Q4), 2 * Q4)], engines=(engine,),
                                                         min_val=0, max_val=NT - 1)
    return values[0::2], values[1::2]


def attention_sum(nc, mem, dr, keep, agg, table, heads, width, layer):
    H, F = heads, width
    idx = mem.sb("idx", [P, U], I32)
    gx, ms = mem.sb("gx", [P, U, F]), mem.sb("ms", [P, HF, F])
    wl, dl = mem.sb("wl", [P, U, H]), mem.sb("dl", [P, U])
    sel = mem.sb("sel", [P, U, P])
    iota = mem.sb("iota4", [128, 128])
    psa = [mem.ps(f"a4{j}") for j in range(HF)]
    psd = [mem.ps(f"d4{j}") for j in range(HF)]
    nm = lambda n: mem.sem(f"b{layer}_{n}")
    listed, nopped, x_in, used = nm("listed"), nm("nopped"), *([nm(f"{n}{q}") for q in range(Q4)] for n in "xu")
    landed, picked, weighed, summed, added = (nm(n) for n in ("landed", "picked", "weighed", "summed", "added"))
    vec = nc.vector

    with nc.Block() as block:
        @block.sync
        def _(sp):
            sp.dma_start(iota[:], dr["c_iota"][:, 0:128]).then_inc(landed, 16)

        @block.gpsimd
        def _(pool):
            pool.wait_ge(landed, 16)
            with pool.Fori(0, KS // U) as i:
                for q in range(Q4):
                    pool.wait_ge(used[q], i + 1)
                    pool.nop().then_inc(nopped, 1)
                    nc.gpsimd.tensor_copy(idx[:, HF * q:HF * q + HF],
                                          keep["row_step"][:, bass.ds(i * U + HF * q, HF)]).then_inc(listed, 1)
                    pool.wait_ge(listed, Q4 * i + q + 1)
                    pool.nop().then_inc(nopped, 1)
                    for j in range(HF * q, HF * q + HF):
                        nc.gpsimd.indirect_dma_start(
                            out=gx[:, j, :], out_offset=None, in_=table,
                            in_offset=bass.IndirectOffsetOnAxis(ap=idx[:, j:j + 1], axis=0)).then_inc(x_in[q], 16)

        @block.scalar
        def _(act):
            for q in range(Q4):
                act.nop().then_inc(used[q], 1)
            with act.Fori(0, KS // U) as i:
                for q in range(Q4):
                    act.wait_ge(x_in[q], (i + 1) * (16 * HF))
                    act.wait_ge(picked, i * Q4 + q + 1)
                    for j in range(HF):
                        act.wait_ge(summed, i * U + q * HF + j + 1)
                        for h in range(H):
                            w = F // H
                            last = nc.scalar.activation(ms[:, j, h * w:h * w + w], gx[:, q * HF + j, h * w:h * w + w],
                                                        ACT.Copy, scale=wl[:, q * HF + j, h:h + 1])
                        last.then_inc(weighed, 1)
                    act.drain()
                    act.nop().then_inc(used[q], 1)

        @block.tensor
        def _(pe):
            for j in range(HF):
                pe.nop().then_inc(summed, 1)

            def sums(n, q, together):
                for j in range(HF):
                    if together:
                        b, flags = 2 * (q % 2), dict(start=(j == 0), stop=(j == HF - 1))
                        if j == 0:
                            pe.wait_ge(added, n + 1)
                    else:
                        b, flags = j, dict(start=True, stop=True)
                        pe.wait_ge(added, n + j + 2)
                    nc.tensor.matmul(psd[b][0:P, 0:H], sel[:, q * HF + j, :], wl[:, q * HF + j, :], **flags)
                    pe.wait_ge(weighed, n + j + 1)
                    nc.tensor.matmul(psa[b][0:P, 0:F], sel[:, q * HF + j, :], ms[:, j, :], **flags).then_inc(summed, 1)
                if not together:
                    pe.wait_ge(added, n + 2 * HF + 1)

            with pe.Fori(0, KS // U) as i:
                _, spans = part_tiles(nc, keep, i, mybir.EngineType.PE)
                for q in range(Q4):
                    pe.wait_ge(picked, i * Q4 + q + 1)
                    with pe.If(spans[q] < 1):
                        sums(i * U + q * HF, q, True)
                    with pe.If(spans[q] > 0):
                        sums(i * U + q * HF, q, False)

        @block.vector
        def _(dve):
            for t in range(0, NT + 1, 13):
                vec.memset(agg[:, t:t + 13, 0:F + H], 0.0)
            for j in range(HF + 1):
                dve.nop().then_inc(added, 1)
            dve.wait_ge(landed, 16)
            dve.drain()

            def pick(first, q):
                part = slice(q * HF, q * HF + HF)
                vec.tensor_copy(wl[:, part, :], keep["w"][:, bass.ds(first, HF), 0:H])
                vec.tensor_copy(dl[:, part], keep["dloc"][:, bass.ds(first, HF)])
                dve.drain()
                for j in range(HF):
                    vec.tensor_scalar(sel[:, q * HF + j, :], iota[0:P, 0:P], dl[:, q * HF + j:q * HF + j + 1], None,
                                      ALU.is_equal)
                dve.drain()
                dve.nop().then_inc(picked, 1)

            def add(n, b, tile, steps):
                dve.wait_ge(summed, n + HF + steps)
                here = agg[:, bass.ds(tile, 1), 0:F].rearrange("p o f -> p (o f)")
                vec.tensor_tensor(here, psa[b][0:P, 0:F], here, ALU.add)
                here = agg[:, bass.ds(tile, 1), F:F + H].rearrange("p o f -> p (o f)")
                vec.tensor_tensor(here, psd[b][0:P, 0:H], here, ALU.add).then_inc(added, steps)
                dve.drain()

            for q in range(Q4 - 1):
                pick(q * HF, q)
            with dve.Fori(0, KS // U) as i:
                firsts, spans = part_tiles(nc, keep, i, mybir.EngineType.DVE)
                for q in range(Q4):
                    pick(i * U + (q + Q4 - 1) * HF, (q + Q4 - 1) % Q4)
                    with dve.If(spans[q] < 1):
                        add(i * U + q * HF, 2 * (q % 2), firsts[q], HF)
                    with dve.If(spans[q] > 0):
                        tiles = node_tiles(nc, keep, i * U + q * HF, HF)
                        for j in range(HF):
                            add(i * U + q * HF + j, j, tiles[j], 1)


def rows(ap, t, base=0):
    return ap[bass.ds(t * P + base, P), :]


def norm_buffers(mem):
    return dict(stats=mem.sb("stats", [P, 6]), mv=mem.sb("mv", [P, 2]), var=mem.sb("var", [P, 1]),
                sd=mem.sb("sd", [P, 1]), rsd=mem.sb("rsd", [P, 1]), var_made=mem.sem("var_made"),
                sd_made=mem.sem("sd_made"))


def norm_statistics(nc, dve, nl, x):
    vec = nc.vector
    dve.drain()
    vec.bn_stats(nl["stats"][:], x)
    dve.drain()
    vec.bn_aggr(nl["mv"][:], nl["stats"][:])
    dve.drain()
    vec.tensor_scalar(nl["var"][:], nl["mv"][:, 1:2], 1e-5, None, ALU.add).then_inc(nl["var_made"], 1)


def norm_root(nc, act, nl, t):
    act.wait_ge(nl["var_made"], t + 1)
    nc.scalar.activation(nl["sd"][:], nl["var"][:], ACT.Sqrt).then_inc(nl["sd_made"], 1)


def norm_scale(nc, dve, nl, t, out, x):
    vec = nc.vector
    dve.wait_ge(nl["sd_made"], t + 1)
    vec.reciprocal(nl["rsd"][:], nl["sd"][:])
    dve.drain()
    return vec.tensor_scalar(out, x, nl["mv"][:, 0:1], nl["rsd"][:, 0:1], ALU.subtract, ALU.mult)


def projection_buffers(mem, blocks, width, heads):
    outs = width // 128
    return dict(blocks=blocks, width=width, heads=heads, outs=outs,
                w=mem.sb("w", [128, blocks, 2, width]), wt=mem.sb("wt", [128, outs, 2, blocks * 128]),
                qk=mem.sb("qk", [128, outs, 2, heads]), wk=mem.sb("wk", [128, blocks, 2, 2 * heads]),
                psx=[mem.ps(f"x{r}") for r in range(2)], psk=mem.ps("k"))


PROJECTION_LOADS, PROJECTION_STORES = 6, 6


def projection_load(nc, sp, pr, w, wt, k, q, sem):
    with nc.allow_non_contiguous_dma(reason="short rows of the key and query vectors"):
        sp.dma_start(pr["qk"][:, :, 0, :], k.rearrange("(o p) h -> p o h", p=128)).then_inc(sem, 16)
        sp.dma_start(pr["qk"][:, :, 1, :], q.rearrange("(o p) h -> p o h", p=128)).then_inc(sem, 16)
    for r in range(2):
        sp.dma_start(pr["w"][:, :, r, :], w[r].rearrange("(b p) o -> p b o", p=128)).then_inc(sem, 16)
        sp.dma_start(pr["wt"][:, :, r, :], wt[r].rearrange("(o p) b -> p o b", p=128)).then_inc(sem, 16)


def score_weights(nc, pr):
    heads, outs = pr["heads"], pr["outs"]
    for b in range(pr["blocks"]):
        for r in range(2):
            at = (b * 2 + r) * 2 * heads
            for o in range(outs):
                last = nc.tensor.matmul(pr["psk"][:, at:at + 2 * heads], pr["wt"][:, o, r, b * 128:b * 128 + 128],
                                        pr["qk"][:, o].rearrange("p s h -> p (s h)"), start=(o == 0),
                                        stop=(o == outs - 1))
    return last


def take_score_weights(nc, pr):
    n = pr["blocks"] * 2 * 2 * pr["heads"]
    return nc.vector.tensor_copy(pr["wk"][:].rearrange("p b r s -> p (b r s)"), pr["psk"][:, 0:n])


def project(nc, pr, blocks):
    mm, S = nc.tensor.matmul, 2 * pr["heads"]
    for r in range(2):
        for n, (x, b) in enumerate(blocks):
            mm(pr["psx"][r][0:P, 0:pr["width"]], x, pr["w"][:, b, r, :], start=(n == 0), stop=(n == len(blocks) - 1))
    for r in range(2):
        for n, (x, b) in enumerate(blocks):
            last = mm(pr["psk"][0:P, r * S:r * S + S], x, pr["wk"][:, b, r, :], start=(n == 0),
                      stop=(n == len(blocks) - 1))
    return last


def projection_store(sp, dr, pr, t, xsb, ksb, sem):
    H = pr["heads"]
    xw, kt, qt = (dr["xw"], dr["kt"], dr["qt"]) if H == 4 else (dr["xw1"], dr["kt1"], dr["qt1"])
    for r in range(2):
        sp.dma_start(rows(xw, t, r * N), xsb[:, r, :]).then_inc(sem, 16)
        sp.dma_start(rows(kt, t, r * N), ksb[:, r, 0:H]).then_inc(sem, 16)
        sp.dma_start(rows(qt, t, r * N), ksb[:, r, H:2 * H]).then_inc(sem, 16)


def nodes_gate(nc, mem, dr, mt):
    pr = projection_buffers(mem, 6, 512, 4)
    nl = norm_buffers(mem)
    xt, xn = mem.sb("xt", [128, 2, P]), mem.sb("xn", [P, NT, D])
    gw1, gw2 = mem.sb("gw1", [128, 4, D]), mem.sb("gw2", [128, 2, D])
    gb1, gb2, gc, qc = (mem.sb(n, [128, 2]) for n in ("gb1", "gb2", "gc", "qc"))
    qb, ones = mem.sb("qb", [128, 2, P]), mem.sb("ones", [128, P])
    xb, kb = mem.sb("xb", [P, 2, 512]), mem.sb("kb", [P, 2, 8])
    ident = mem.sb("ident", [128, 128])
    r1, x1, x0 = mem.sb("r1", [P, D]), mem.sb("x1", [P, D]), mem.sb("x0", [P, D])
    x1t, ght, gt, x0t = (mem.sb(n, [128, 2, P]) for n in ("x1t", "ght", "gt", "x0t"))
    xsb, ksb = mem.sb("xsb", [P, 2, 512]), mem.sb("ksb", [P, 2, 8])
    psy, pst, psg, psh, ps0 = (mem.ps(n) for n in ("y", "t", "g", "h", "0"))
    (landed, ones_made, spread, gate_c, scaled, bias_made, ready, y_made, x1_made, x1_stored, t_made, x1t_made, gh_made,
     ght_made, g_made, gt_made, x0t_made, x0_turned, x0_made, projected, table_made, done1, done2, table_stored) = (
        mem.sem(n) for n in (
            "landed", "ones_made", "spread", "gate_c", "scaled", "bias_made", "ready", "y_made", "x1_made", "x1_stored",
            "t_made", "x1t_made", "gh_made", "ght_made", "g_made", "gt_made", "x0t_made", "x0_turned", "x0_made",
            "projected", "table_made", "done1", "done2", "table_stored"))
    xt_in = mem.sem("xt_in")
    vec, mm = nc.vector, nc.tensor.matmul
    LOADS = PROJECTION_LOADS + 7

    with nc.Block() as block:
        @block.sync
        def _(sp):
            with nc.allow_non_contiguous_dma(reason="short vectors"):
                sp.dma_start(qc[:], dr["L1_gnn_query"][0].rearrange("(b p) -> p b", p=128)).then_inc(landed, 16)
                sp.dma_start(gb1[:], dr["L1_gnn_gate_b1"].rearrange("(b p) -> p b", p=128)).then_inc(landed, 16)
                sp.dma_start(gb2[:], dr["L1_gnn_gate_b2"].rearrange("(b p) -> p b", p=128)).then_inc(landed, 16)
            sp.dma_start(gw1[:], dr["L1_gnn_gate_w1"].rearrange("(b p) o -> p b o", p=128)).then_inc(landed, 16)
            sp.dma_start(gw2[:], dr["L1_gnn_gate_w2"].rearrange("(b p) o -> p b o", p=128)).then_inc(landed, 16)
            sp.dma_start(ident[:], dr["c_ident"]).then_inc(landed, 16)
            projection_load(nc, sp, pr, dr["L1_gnn_W1"], dr["W1_t"], dr["L1_gnn_k1"], dr["L1_gnn_q1"], landed)
            sp.dma_start(xn[:], dr["x"].rearrange("(t p) c -> p t c", p=P)).then_inc(landed, 16)
            sp.nop().then_inc(x1_stored, 1)
            sp.nop().then_inc(table_stored, 1)
            sp.dma_start(xt[:], dr["x_t2"][:, 0:P].rearrange("(b p) n -> p b n", p=128)).then_inc(xt_in, 16)
            with sp.Fori(0, NT) as t:
                sp.wait_ge(x1_made, t + 1)
                sp.dma_start(xt[:], dr["x_t2"][:, bass.ds(t * P + P, P)].rearrange("(b p) n -> p b n", p=128)).then_inc(xt_in, 16)
                sp.dma_start(rows(dr["x1"], t), x1[:]).then_inc(done1, 16)
                sp.wait_ge(done1, t * 16 + 16)
                sp.nop().then_inc(x1_stored, 1)
                sp.wait_ge(x0_made, t + 1)
                sp.wait_ge(table_made, 2 * t + 2)
                sp.dma_start(rows(dr["x0"], t), x0[:]).then_inc(done2, 16)
                projection_store(sp, dr, pr, t, xsb, ksb, done2)
                sp.wait_ge(done2, t * (16 * 7) + 16 * 7)
                sp.nop().then_inc(table_stored, 1)
            sp.wait_ge(xt_in, 16 * (NT + 1))

        @block.tensor
        def _(pe):
            pe.wait_ge(landed, 16 * LOADS)
            for o in range(2):
                for b in range(2):
                    last = mm(psg[:, o:o + 1], gw1[:, 2 + b, 128 * o:128 * o + 128], qc[:, b:b + 1], start=(b == 0), stop=(b == 1))
            last.then_inc(gate_c, 1)
            score_weights(nc, pr).then_inc(gate_c, 1)
            pe.wait_ge(spread, 1)
            pe.wait_ge(scaled, 1)
            for r in range(2):
                for b in range(2):
                    mm(pr["psx"][r][0:P, :], qb[:, b, :], pr["w"][:, 2 + b, r, :], start=(b == 0), stop=(b == 1))
            for r in range(2):
                for b in range(2):
                    last = mm(psh[0:P, 8 * r:8 * r + 8], qb[:, b, :], pr["wk"][:, 2 + b, r, :], start=(b == 0), stop=(b == 1))
            last.then_inc(bias_made, 1)
            pe.wait_ge(ready, 1)

            def turn(t):
                pe.wait_ge(xt_in, t * 16 + 16)
                for b in range(2):
                    last = mm(psy[0:P, 0:D], xt[:, b, :], mt[:, b, :], start=(b == 0), stop=(b == 1))
                last.then_inc(y_made, 1)

            def gate(t):
                pe.wait_ge(x1_made, t + 1)
                for b in range(2):
                    last = nc.tensor.transpose(pst[:, b * P:b * P + P], x1[:, 128 * b:128 * b + 128], ident[0:P, 0:P])
                last.then_inc(t_made, 1)
                pe.wait_ge(x1t_made, t + 1)
                for o in range(2):
                    for b in range(2):
                        last = mm(psg[:, o * P:o * P + P], gw1[:, b, 128 * o:128 * o + 128], x1t[:, b, :], start=(b == 0), stop=(b == 1))
                last.then_inc(gh_made, 1)
                pe.wait_ge(ght_made, t + 1)
                for o in range(2):
                    for b in range(2):
                        last = mm(psh[:, o * P:o * P + P], gw2[:, b, 128 * o:128 * o + 128], ght[:, b, :], start=(b == 0), stop=(b == 1))
                last.then_inc(g_made, 1)
                pe.wait_ge(x0t_made, t + 1)
                for b in range(2):
                    last = nc.tensor.transpose(ps0[0:P, 128 * b:128 * b + 128], x0t[:, b, :], ident[:])
                last.then_inc(x0_turned, 1)

            def table(t):
                pe.wait_ge(table_made, 2 * t + 1)
                blocks = [(x0t[:, 0, :], 0), (x0t[:, 1, :], 1), (x1t[:, 0, :], 4), (x1t[:, 1, :], 5)]
                project(nc, pr, blocks).then_inc(projected, 1)

            turn(0)
            with pe.Fori(0, NT - 1) as t:
                gate(t)
                turn(t + 1)
                table(t)
            gate(NT - 1)
            table(NT - 1)

        @block.scalar
        def _(act):
            def gate(t):
                act.wait_ge(gh_made, t + 1)
                for o in range(2):
                    last = nc.scalar.activation(ght[:, o, :], psg[:, o * P:o * P + P], ACT.Relu, bias=gc[:, o:o + 1])
                last.then_inc(ght_made, 1)
                act.wait_ge(g_made, t + 1)
                for o in range(2):
                    last = nc.scalar.activation(gt[:, o, :], psh[:, o * P:o * P + P], ACT.Sigmoid, bias=gb2[:, o:o + 1])
                last.then_inc(gt_made, 1)
                act.wait_ge(table_stored, t + 1)
                act.wait_ge(x0_turned, t + 1)
                nc.scalar.copy(x0[:], ps0[0:P, 0:D]).then_inc(x0_made, 1)

            norm_root(nc, act, nl, 0)
            with act.Fori(0, NT - 1) as t:
                gate(t)
                norm_root(nc, act, nl, t + 1)
            gate(NT - 1)

        @block.vector
        def _(dve):
            vec.memset(ones[:], 1.0)
            dve.wait_ge(landed, 16 * LOADS)
            dve.drain()
            for b in range(2):
                vec.tensor_scalar(qb[:, b, :], ones[:], qc[:, b:b + 1], None, ALU.mult)
            dve.drain()
            dve.nop().then_inc(spread, 1)
            dve.wait_ge(gate_c, 1)
            vec.tensor_tensor(gc[:], psg[:, 0:2], gb1[:], ALU.add)
            dve.wait_ge(gate_c, 2)
            take_score_weights(nc, pr)
            dve.drain()
            for b in range(2):
                vec.tensor_scalar(pr["w"][:, 4 + b], pr["w"][:, 4 + b], qc[:, b:b + 1], None, ALU.mult)
                vec.tensor_scalar(pr["wk"][:, 4 + b], pr["wk"][:, 4 + b], qc[:, b:b + 1], None, ALU.mult)
            dve.drain()
            dve.nop().then_inc(scaled, 1)
            dve.wait_ge(bias_made, 1)
            for r in range(2):
                vec.tensor_copy(xb[:, r, :], pr["psx"][r][0:P, :])
            vec.tensor_copy(kb[:].rearrange("p r s -> p (r s)"), psh[0:P, 0:16])
            dve.drain()
            dve.nop().then_inc(ready, 1)
            dve.nop().then_inc(table_made, 1)

            def residual(t):
                dve.wait_ge(y_made, t + 1)
                vec.tensor_tensor(r1[:], psy[0:P, 0:D], xn[:, bass.ds(t, 1), :].rearrange("p o c -> p (o c)"), ALU.add)
                norm_statistics(nc, dve, nl, r1[:])
                dve.wait_ge(x1_stored, t + 1)
                norm_scale(nc, dve, nl, t, x1[:], r1[:]).then_inc(x1_made, 1)

            def gate(t):
                dve.wait_ge(t_made, t + 1)
                vec.tensor_copy(x1t[:].rearrange("p b n -> p (b n)"), pst[:, 0:2 * P]).then_inc(x1t_made, 1)
                dve.drain()
                dve.wait_ge(gt_made, t + 1)
                vec.tensor_tensor(x0t[:], x1t[:], gt[:], ALU.mult).then_inc(x0t_made, 1)

            def take(t):
                dve.wait_ge(projected, t + 1)
                dve.wait_ge(table_stored, t + 1)
                for r in range(2):
                    vec.tensor_tensor(xsb[:, r, :], pr["psx"][r][0:P, :], xb[:, r, :], ALU.add)
                vec.tensor_tensor(ksb[:].rearrange("p r s -> p (r s)"), pr["psk"][0:P, 0:16], kb[:].rearrange("p r s -> p (r s)"),
                                  ALU.add)
                dve.drain()
                dve.nop().then_inc(table_made, 1)
                dve.nop().then_inc(table_made, 1)

            residual(0)
            with dve.Fori(0, NT - 1) as t:
                gate(t)
                residual(t + 1)
                take(t)
            gate(NT - 1)
            take(NT - 1)


def normalized_heads(nc, dve, out, agg, t, bias, den, width, heads):
    vec, w = nc.vector, width // heads
    vec.tensor_scalar(den[:, 0:heads], agg[:, bass.ds(t, 1), width:width + heads].rearrange("p o h -> p (o h)"), 1e-16,
                      None, ALU.add)
    dve.drain()
    vec.reciprocal(den[:, heads:2 * heads], den[:, 0:heads])
    dve.drain()
    for h in range(heads):
        vec.scalar_tensor_tensor(out[:, h * w:h * w + w], agg[:, bass.ds(t, 1), h * w:h * w + w].rearrange("p o c -> p (o c)"),
                                 den[:, heads + h:heads + h + 1], bias[:, h * w:h * w + w], ALU.mult, ALU.add)
    dve.drain()


def nodes_attend(nc, mem, dr, agg, kept, bias, names, width, heads, first):
    F, H = width, heads
    pr = projection_buffers(mem, 4, F, H)
    den, raw, hc = mem.sb("den", [P, 8]), mem.sb("raw", [P, 512]), mem.sb("hc", [P, 512])
    ht = mem.sb("ht", [128, 4, P])
    bb = mem.sb("bb", [P, 512])
    ident = mem.sb("ident", [128, 128])
    xsb, ksb = mem.sb("xsb", [P, 2, F]), mem.sb("ksb", [P, 2, 2 * H])
    pst = mem.ps("t")
    landed, wk_made, ready, h_made, turned, ht_made, projected, table_made, done, stored = (
        mem.sem(n) for n in ("landed", "wk_made", "ready", "h_made", "turned", "ht_made", "projected", "table_made",
                             "done", "stored"))
    vec = nc.vector
    LOADS = PROJECTION_LOADS + 2

    with nc.Block() as block:
        @block.sync
        def _(sp):
            sp.dma_start(bb[:], dr[bias].partition_broadcast(P)).then_inc(landed, 16)
            sp.dma_start(ident[:], dr["c_ident"]).then_inc(landed, 16)
            projection_load(nc, sp, pr, *(dr[n] for n in names), landed)
            sp.nop().then_inc(stored, 1)
            with sp.Fori(0, NT) as t:
                sp.wait_ge(table_made, 2 * t + 3)
                projection_store(sp, dr, pr, t, xsb, ksb, done)
                sp.wait_ge(done, t * (16 * PROJECTION_STORES) + 16 * PROJECTION_STORES)
                sp.nop().then_inc(stored, 1)

        @block.tensor
        def _(pe):
            pe.wait_ge(landed, 16 * LOADS)
            score_weights(nc, pr).then_inc(wk_made, 1)
            pe.wait_ge(ready, 1)
            with pe.Fori(0, NT) as t:
                pe.wait_ge(h_made, t + 1)
                for b in range(4):
                    last = nc.tensor.transpose(pst[:, b * P:b * P + P], hc[:, 128 * b:128 * b + 128], ident[0:P, 0:P])
                last.then_inc(turned, 1)
                pe.wait_ge(ht_made, t + 1)
                pe.wait_ge(table_made, 2 * t + 1)
                project(nc, pr, [(ht[:, b, :], b) for b in range(4)]).then_inc(projected, 1)

        @block.scalar
        def _(act):
            with act.Fori(0, NT) as t:
                act.wait_ge(turned, t + 1)
                nc.scalar.copy(ht[:].rearrange("p b n -> p (b n)"), pst[:, 0:4 * P]).then_inc(ht_made, 1)
                act.wait_ge(projected, t + 1)
                act.wait_ge(stored, t + 1)
                act.wait_ge(ready, 1)
                nc.scalar.copy(xsb[:, 1, :], pr["psx"][1][0:P, 0:F]).then_inc(table_made, 1)

        @block.vector
        def _(dve):
            dve.wait_ge(wk_made, 1)
            dve.wait_ge(landed, 16 * LOADS)
            take_score_weights(nc, pr)
            dve.drain()
            dve.nop().then_inc(ready, 1)
            dve.nop().then_inc(table_made, 1)

            def attend(t):
                normalized_heads(nc, dve, raw, agg, t, bb, den, 512, 4)
                if not isinstance(t, int):
                    dve.wait_ge(turned, t)
                here = kept[:, bass.ds(t, 1), :].rearrange("p o c -> p (o c)")
                if first:
                    vec.tensor_scalar(hc[:], raw[:], 0.0, None, ALU.max).then_inc(h_made, 1)
                    dve.drain()
                    vec.tensor_copy(here, hc[:])
                else:
                    vec.scalar_tensor_tensor(hc[:], raw[:], 0.0, here, ALU.max, ALU.add).then_inc(h_made, 1)

            def take(t):
                dve.wait_ge(projected, t + 1)
                dve.wait_ge(stored, t + 1)
                vec.tensor_copy(xsb[:, 0, :], pr["psx"][0][0:P, 0:F])
                vec.tensor_copy(ksb[:].rearrange("p r s -> p (r s)"), pr["psk"][0:P, 0:4 * H])
                dve.drain()
                dve.nop().then_inc(table_made, 1)

            attend(0)
            with dve.Fori(0, NT - 1) as t:
                attend(t + 1)
                take(t)
            take(NT - 1)


def nodes_mix(nc, mem, dr, agg):
    nl = norm_buffers(mem)
    den, raw, hc, ht = mem.sb("den", [P, 8]), mem.sb("raw", [P, 128]), mem.sb("hc", [P, 128]), mem.sb("ht", [128, P])
    b3, pb, ab = mem.sb("b3", [P, 128]), mem.sb("pb", [P, D]), mem.sb("ab", [P, D])
    pw, aw = mem.sb("pw", [128, D]), mem.sb("aw", [128, 2, D])
    ident = mem.sb("ident", [128, 128])
    x0, x1 = mem.sb("x0", [P, D]), mem.sb("x1", [P, D])
    o1, o2, sq = mem.sb("o1", [P, D]), mem.sb("o2", [P, D]), mem.sb("sq", [P, D])
    ss, nrm, inv = mem.sb("ss", [P, 1]), mem.sb("nrm", [P, 1]), mem.sb("inv", [P, 2])
    r1, x2, x2t, hsb = mem.sb("r1", [P, D]), mem.sb("x2", [P, D]), mem.sb("x2t", [128, 2, P]), mem.sb("hsb", [P, D])
    pst, pso, psu, psh = (mem.ps(n) for n in ("t", "o", "u", "h"))
    (landed, x_in, used, h_made, turned, ht_made, o_made, ss_made, nrm_made, x2_made, x2_turned, x2t_made, table, made,
     done, stored) = (mem.sem(n) for n in (
         "landed", "x_in", "used", "h_made", "turned", "ht_made", "o_made", "ss_made", "nrm_made", "x2_made",
         "x2_turned", "x2t_made", "table", "made", "done", "stored"))
    vec, mm = nc.vector, nc.tensor.matmul

    with nc.Block() as block:
        @block.sync
        def _(sp):
            for t, name in ((b3, "L1_gnn_b3"), (pb, "L1_gnn_proj_b"), (ab, "L2_gnn_aw_b")):
                sp.dma_start(t[:], dr[name].partition_broadcast(P)).then_inc(landed, 16)
            sp.dma_start(pw[:], dr["L1_gnn_proj_w"]).then_inc(landed, 16)
            sp.dma_start(aw[:], dr["L2_gnn_aw_W"].rearrange("(b p) o -> p b o", p=128)).then_inc(landed, 16)
            sp.dma_start(ident[:], dr["c_ident"]).then_inc(landed, 16)
            sp.nop().then_inc(stored, 1)
            with sp.Fori(0, NT) as t:
                sp.wait_ge(used, t + 1)
                sp.dma_start(x0[:], rows(dr["x0"], t)).then_inc(x_in, 16)
                sp.dma_start(x1[:], rows(dr["x1"], t)).then_inc(x_in, 16)
                sp.wait_ge(made, t + 1)
                sp.dma_start(rows(dr["x2"], t), x2[:]).then_inc(done, 16)
                sp.dma_start(rows(dr["h2"], t), hsb[:]).then_inc(done, 16)
                sp.wait_ge(done, t * 32 + 32)
                sp.nop().then_inc(stored, 1)

        @block.tensor
        def _(pe):
            pe.wait_ge(landed, 16 * 6)
            with pe.Fori(0, NT) as t:
                pe.wait_ge(h_made, t + 1)
                nc.tensor.transpose(pst[:, 0:P], hc[:], ident[0:P, 0:P]).then_inc(turned, 1)
                pe.wait_ge(ht_made, t + 1)
                mm(pso[0:P, 0:D], ht[:], pw[:], start=True, stop=True).then_inc(o_made, 1)
                pe.wait_ge(x2_made, t + 1)
                for b in range(2):
                    last = nc.tensor.transpose(psu[:, b * P:b * P + P], x2[:, 128 * b:128 * b + 128], ident[0:P, 0:P])
                last.then_inc(x2_turned, 1)
                pe.wait_ge(x2t_made, t + 1)
                for b in range(2):
                    last = mm(psh[0:P, 0:D], x2t[:, b, :], aw[:, b, :], start=(b == 0), stop=(b == 1))
                last.then_inc(table, 1)

        @block.scalar
        def _(act):
            with act.Fori(0, NT) as t:
                act.wait_ge(turned, t + 1)
                nc.scalar.copy(ht[:], pst[:, 0:P]).then_inc(ht_made, 1)
                act.wait_ge(ss_made, t + 1)
                nc.scalar.activation(nrm[:], ss[:], ACT.Sqrt).then_inc(nrm_made, 1)
                norm_root(nc, act, nl, t)
                act.wait_ge(x2_turned, t + 1)
                nc.scalar.copy(x2t[:].rearrange("p b n -> p (b n)"), psu[:, 0:2 * P]).then_inc(x2t_made, 1)

        @block.vector
        def _(dve):
            dve.nop().then_inc(used, 1)
            dve.wait_ge(landed, 16 * 6)
            def attend(t):
                normalized_heads(nc, dve, raw, agg, t, b3, den, 128, 1)
                vec.tensor_scalar(hc[:], raw[:], 0.0, None, ALU.max).then_inc(h_made, 1)

            attend(0)
            with dve.Fori(0, NT) as t:
                dve.wait_ge(o_made, t + 1)
                vec.tensor_tensor(o1[:], pso[0:P, 0:D], pb[:], ALU.add)
                dve.drain()
                dve.wait_ge(x_in, t * 32 + 32)
                vec.tensor_tensor(o2[:], o1[:], x0[:], ALU.add)
                dve.drain()
                vec.tensor_tensor_reduce(out=sq[:], in0=o2[:], in1=o2[:], scale=1.0, scalar=0.0, op0=ALU.mult,
                                         op1=ALU.add, accum_out=ss[:]).then_inc(ss_made, 1)
                dve.wait_ge(nrm_made, t + 1)
                vec.tensor_scalar(inv[:, 0:1], nrm[:], 1e-12, None, ALU.max)
                dve.drain()
                vec.reciprocal(inv[:, 1:2], inv[:, 0:1])
                dve.drain()
                vec.scalar_tensor_tensor(r1[:], o2[:], inv[:, 1:2], x1[:], ALU.mult, ALU.add).then_inc(used, 1)
                norm_statistics(nc, dve, nl, r1[:])
                dve.wait_ge(stored, t + 1)
                norm_scale(nc, dve, nl, t, x2[:], r1[:]).then_inc(x2_made, 1)
                attend(t + 1)
                dve.wait_ge(table, t + 1)
                vec.tensor_tensor(hsb[:], psh[0:P, 0:D], ab[:], ALU.add).then_inc(made, 1)


def soft(nc, dve, t_in, neg):
    return nc.vector.scalar_tensor_tensor(neg, t_in, -1.0, t_in, ALU.mult, ALU.min)


def filter_sum(nc, mem, dr, keep, agg):
    C4 = HF * P
    idx, gx = mem.sb("idx", [P, 2 * HF], I32), mem.sb("gx", [P, 2, HF, D])
    ea = mem.sb("ea", [64, 2, HF, P])
    m1, m2, mb = mem.sb("m1", [64, D]), mem.sb("m2", [128, 2, D]), mem.sb("mb", [P, D])
    iota, half = mem.sb("iota", [128, 512]), mem.sb("half", [128, 1])
    lg1, h1 = ([mem.sb(f"{n}{q}", [128, 2, C4]) for q in range(2)] for n in ("lg1", "h1"))
    f2, lg2 = ([mem.sb(f"{n}{q}", [P, HF, D]) for q in range(2)] for n in ("f2", "lg2"))
    ms = mem.sb("ms", [P, HF, D])
    cl, dl, sel = mem.sb("cl", [P, HF]), mem.sb("dl", [P, HF]), mem.sb("sel", [P, HF, P])
    ps1, ps2, ps3 = [mem.ps(f"1{q}", [128, 2, 512]) for q in range(2)], mem.ps("2", [128, HF, D]), mem.ps("3", [128, HF, D])
    (landed, listed, nopped, used, ea_free, hid, log1_made, h1_made, filt, f2_made, log2_made, ms_made,
     summed, added) = (mem.sem(n) for n in (
         "landed", "listed", "nopped", "used", "ea_free", "hid", "log1_made", "h1_made", "filt",
         "f2_made", "log2_made", "ms_made", "summed", "added"))
    x_in, e_in = [mem.sem(f"x{q}") for q in range(2)], [mem.sem(f"e{q}") for q in range(2)]
    vec, mm = nc.vector, nc.tensor.matmul
    TURNS, U2 = KS // (2 * HF), 2 * HF

    with nc.Block() as block:
        @block.gpsimd
        def _(pool):
            pool.wait_ge(landed, 16 * 5)
            with pool.Fori(0, TURNS) as i:
                for q in range(2):
                    pool.wait_ge(used, 2 * i + q + 1)
                    pool.nop().then_inc(nopped, 1)
                    nc.gpsimd.tensor_copy(idx[:, HF * q:HF * q + HF],
                                          keep["src_step"][:, bass.ds(i * U2 + HF * q, HF)]).then_inc(listed, 1)
                    pool.wait_ge(listed, 2 * i + q + 1)
                    pool.nop().then_inc(nopped, 1)
                    for j in range(HF):
                        n = HF * q + j
                        nc.gpsimd.indirect_dma_start(
                            out=gx[:, q, j, :], out_offset=None, in_=dr["h2"],
                            in_offset=bass.IndirectOffsetOnAxis(ap=idx[:, n:n + 1], axis=0)).then_inc(x_in[q], 16)

        @block.sync
        def _(sp):
            sp.dma_start(m1[0:50, :], dr["L2_gnn_m1_W"]).then_inc(landed, 16)
            sp.dma_start(m1[50:51, :], dr["L2_gnn_m1_b"].rearrange("(o c) -> o c", o=1)).then_inc(landed, 16)
            sp.dma_start(m2[:], dr["L2_gnn_m2_W"].rearrange("(b p) o -> p b o", p=128)).then_inc(landed, 16)
            sp.dma_start(iota[:], dr["c_iota"]).then_inc(landed, 16)
            sp.dma_start(mb[:], dr["L2_gnn_m2_b"].partition_broadcast(P)).then_inc(landed, 16)

            def load(first, q):
                for j in range(HF):
                    tile = sp.value_load(keep["etile"][0:1, bass.ds(first + j, 1)], min_val=0, max_val=ET - 1)
                    sp.dma_start(ea[0:50, q, j, :], dr["ea_t"][:, bass.ds(tile * P, P)]).then_inc(e_in[q], 16)
            sp.wait_ge(ea_free, 1)
            load(0, 0)
            load(HF, 1)
            with sp.Fori(0, TURNS) as i:
                for q in range(2):
                    sp.wait_ge(hid, 2 * i + q + 1)
                    load((i + 1) * U2 + q * HF, q)
            sp.wait_ge(hid, 2 * TURNS + 1)
            load(KS + U2, 0)
            for q in range(2):
                sp.wait_ge(e_in[q], 16 * HF * (TURNS + 2 - q))

        @block.tensor
        def _(pe):
            def hidden(n, q, landings):
                pe.wait_ge(e_in[q], landings)
                if not isinstance(n, int) or n > 1:
                    pe.wait_ge(h1_made, n - 1)
                for o in range(2):
                    last = mm(ps1[q][:, o, 0:C4], m1[0:51, 128 * o:128 * o + 128],
                              ea[0:51, q].rearrange("p j e -> p (j e)"), start=True, stop=True)
                last.then_inc(hid, 1)

            def filters(n, q):
                pe.wait_ge(h1_made, n + 1)
                if not isinstance(n, int) or n:
                    pe.wait_ge(f2_made, n)
                for j in range(HF):
                    for b in range(2):
                        last = mm(ps2[0:P, j, :], h1[q][:, b, j * P:j * P + P], m2[:, b, :], start=(b == 0), stop=(b == 1))
                last.then_inc(filt, 1)

            pe.wait_ge(landed, 16 * 5)
            hidden(0, 0, 16 * HF)
            hidden(1, 1, 16 * HF)
            filters(0, 0)
            hidden(2, 0, 32 * HF)
            filters(1, 1)
            with pe.Fori(0, TURNS) as i:
                for q in range(2):
                    n = 2 * i + q
                    hidden(n + 3, 1 - q, (i + 2 + q) * (16 * HF))
                    filters(n + 2, q)
                    pe.wait_ge(ms_made, n + 1)
                    pe.wait_ge(added, n + 1)
                    for j in range(HF):
                        last = mm(ps3[0:P, j, :], sel[:, j, :], ms[:, j, :], start=True, stop=True)
                    last.then_inc(summed, 1)

        @block.scalar
        def _(act):
            def log(parts):
                for x, lg, _ in parts:
                    nc.scalar.activation(lg[:], x, ACT.Abs)
                act.drain()
                for x, lg, _ in parts:
                    nc.scalar.activation(lg[:], lg[:], ACT.Exp, scale=-1.0)
                act.drain()
                for x, lg, made in parts[::-1]:
                    nc.scalar.activation(lg[:], lg[:], ACT.Ln, scale=0.5, bias=half[0:lg.shape[0], :]).then_inc(made, 1)

            hidden = [(ps1[q][:, :, 0:C4], lg1[q], log1_made) for q in range(2)]
            filters = [(f2[q][:], lg2[q], log2_made) for q in range(2)]
            act.wait_ge(ea_free, 1)
            act.wait_ge(hid, 1)
            log([hidden[0]])
            act.wait_ge(hid, 2)
            log([hidden[1]])
            act.wait_ge(h1_made, 1)
            act.wait_ge(hid, 3)
            act.wait_ge(f2_made, 1)
            log([filters[0], hidden[0]])
            with act.Fori(0, TURNS) as i:
                for q in range(2):
                    n = 2 * i + q
                    act.wait_ge(h1_made, n + 2)
                    act.wait_ge(hid, n + 4)
                    act.wait_ge(f2_made, n + 2)
                    log([filters[1 - q], hidden[1 - q]])

        @block.vector
        def _(dve):
            def make_h1(n, q):
                dve.wait_ge(log1_made, n + 1)
                if not isinstance(n, int) or n >= 2:
                    dve.wait_ge(filt, n - 1)
                vec.scalar_tensor_tensor(h1[q][:], ps1[q][:, :, 0:C4], 0.0, lg1[q][:], ALU.max, ALU.add).then_inc(h1_made, 1)

            def make_f2(n, q):
                dve.wait_ge(filt, n + 1)
                for j in range(HF):
                    last = vec.tensor_tensor(f2[q][:, j, :], ps2[0:P, j, :], mb[:], ALU.add)
                last.then_inc(f2_made, 1)

            for q in range(2):
                vec.memset(ea[:, q], 1.0)
            vec.memset(half[:], 0.5)
            for t in range(0, NT + 1, 13):
                vec.memset(agg[:, t:t + 13, 0:D], 0.0)
            dve.drain()
            for sem in (ea_free, added, used, used):
                dve.nop().then_inc(sem, 1)
            dve.wait_ge(landed, 16 * 5)
            make_h1(0, 0)
            make_h1(1, 1)
            make_f2(0, 0)
            make_h1(2, 0)
            make_f2(1, 1)
            with dve.Fori(0, TURNS) as i:
                for q in range(2):
                    n = 2 * i + q
                    vec.tensor_copy(cl[:], keep["cut"][:, bass.ds(i * U2 + q * HF, HF)])
                    vec.tensor_copy(dl[:], keep["dloc"][:, bass.ds(i * U2 + q * HF, HF)])
                    dve.drain()
                    for j in range(HF):
                        vec.tensor_scalar(sel[:, j, :], iota[0:P, 0:P], dl[:, j:j + 1], None, ALU.is_equal)
                    dve.wait_ge(log2_made, n + 1)
                    vec.scalar_tensor_tensor(f2[q][:], f2[q][:], 0.0, lg2[q][:], ALU.max, ALU.add)
                    dve.drain()
                    dve.wait_ge(x_in[q], (i + 1) * (16 * HF))
                    for j in range(HF):
                        vec.scalar_tensor_tensor(ms[:, j, :], f2[q][:, j, :], cl[:, j:j + 1], gx[:, q, j, :], ALU.mult, ALU.mult)
                    dve.drain()
                    dve.nop().then_inc(ms_made, 1)
                    dve.nop().then_inc(used, 1)
                    tiles = node_tiles(nc, keep, i * U2 + q * HF, HF)
                    make_h1(n + 3, 1 - q)
                    make_f2(n + 2, q)
                    dve.wait_ge(summed, n + 1)
                    for j in range(HF):
                        here = agg[:, bass.ds(tiles[j], 1), 0:D].rearrange("p o f -> p (o f)")
                        vec.tensor_tensor(here, ps3[0:P, j, :], here, ALU.add)
                        dve.drain()
                    dve.nop().then_inc(added, 1)


def nodes_filter(nc, mem, dr, agg):
    nl = norm_buffers(mem)
    w1, w2, w3 = (mem.sb(n, [128, 2, D]) for n in ("w1", "w2", "w3"))
    b1, half = mem.sb("b1", [128, 2]), mem.sb("half", [128, 1])
    b2, b3 = mem.sb("b2", [P, D]), mem.sb("b3", [P, D])
    ident = mem.sb("ident", [128, 128])
    at, f1, neg, h1, x3t = (mem.sb(n, [128, 2, P]) for n in ("at", "f1", "neg", "h1", "x3t"))
    x2, o1, r1, x3, hsb = (mem.sb(n, [P, D]) for n in ("x2", "o1", "r1", "x3", "hsb1"))
    hs = mem.sb("hs", [P, D + 1])
    zero = mem.sb("zero", [P, D + 1])
    ag, ag_made = mem.sb("ag", [P, D]), mem.sem("ag_made")
    psa, psf, pso, psu, psh = (mem.ps(n) for n in ("a", "f", "o", "u", "h"))
    (landed, zeroed, x_in, used, turned, at_made, hid, neg_made, log_made, h1_made, o_made, x3_made, x3_turned,
     x3t_made, table, made, done, stored, cleared) = (mem.sem(n) for n in (
         "landed", "zeroed", "x_in", "used", "turned", "at_made", "hid", "neg_made", "log_made", "h1_made", "o_made",
         "x3_made", "x3_turned", "x3t_made", "table", "made", "done", "stored", "cleared"))
    vec, mm = nc.vector, nc.tensor.matmul

    with nc.Block() as block:
        @block.sync
        def _(sp):
            with nc.allow_non_contiguous_dma(reason="a short vector"):
                sp.dma_start(b1[:], dr["L2_gnn_o1_b"].rearrange("(b p) -> p b", p=128)).then_inc(landed, 16)
            for t, name in ((w1, "L2_gnn_o1_W"), (w2, "L2_gnn_o2_W"), (w3, "L3_gnn_W")):
                sp.dma_start(t[:], dr[name].rearrange("(b p) o -> p b o", p=128)).then_inc(landed, 16)
            for t, name in ((b2, "L2_gnn_o2_b"), (b3, "L3_gnn_b")):
                sp.dma_start(t[:], dr[name].partition_broadcast(P)).then_inc(landed, 16)
            sp.dma_start(ident[:], dr["c_ident"]).then_inc(landed, 16)
            sp.nop().then_inc(stored, 1)
            sp.wait_ge(zeroed, 1)
            for j in range(HF):
                for t in range(NT + 1):
                    sp.dma_start(dr["sum"][j][P * t:P * t + P, :], zero[:]).then_inc(cleared, 16)
            with sp.Fori(0, NT) as t:
                sp.wait_ge(used, t + 1)
                sp.dma_start(x2[:], rows(dr["x2"], t)).then_inc(x_in, 16)
                sp.wait_ge(made, t + 1)
                sp.dma_start(rows(dr["x3"], t), x3[:]).then_inc(done, 16)
                sp.dma_start(rows(dr["h3"], t), hs[:]).then_inc(done, 16)
                sp.wait_ge(done, t * 32 + 32)
                sp.nop().then_inc(stored, 1)
            sp.wait_ge(cleared, 16 * HF * (NT + 1))

        @block.tensor
        def _(pe):
            pe.wait_ge(landed, 16 * 7)

            def hidden(t):
                pe.wait_ge(ag_made, t + 1)
                for b in range(2):
                    last = nc.tensor.transpose(psa[:, b * P:b * P + P], ag[:, 128 * b:128 * b + 128], ident[0:P, 0:P])
                last.then_inc(turned, 1)
                pe.wait_ge(at_made, t + 1)
                for o in range(2):
                    for b in range(2):
                        last = mm(psf[:, o * P:o * P + P], w1[:, b, 128 * o:128 * o + 128], at[:, b, :], start=(b == 0), stop=(b == 1))
                last.then_inc(hid, 1)

            def outer(t):
                pe.wait_ge(h1_made, t + 1)
                for b in range(2):
                    last = mm(pso[0:P, 0:D], h1[:, b, :], w2[:, b, :], start=(b == 0), stop=(b == 1))
                last.then_inc(o_made, 1)

            def table_rows(t):
                pe.wait_ge(x3_made, t + 1)
                for b in range(2):
                    last = nc.tensor.transpose(psu[:, b * P:b * P + P], x3[:, 128 * b:128 * b + 128], ident[0:P, 0:P])
                last.then_inc(x3_turned, 1)
                pe.wait_ge(x3t_made, t + 1)
                for b in range(2):
                    last = mm(psh[0:P, 0:D], x3t[:, b, :], w3[:, b, :], start=(b == 0), stop=(b == 1))
                last.then_inc(table, 1)

            hidden(0)
            with pe.Fori(0, NT - 1) as t:
                outer(t)
                hidden(t + 1)
                table_rows(t)
            outer(NT - 1)
            table_rows(NT - 1)

        @block.scalar
        def _(act):
            act.wait_ge(zeroed, 1)
            nc.scalar.copy(ag[:], agg[:, 0, 0:D]).then_inc(ag_made, 1)

            def take_turned(t):
                act.wait_ge(turned, t + 1)
                nc.scalar.copy(at[:].rearrange("p b n -> p (b n)"), psa[:, 0:2 * P]).then_inc(at_made, 1)
                nc.scalar.copy(ag[:], agg[:, bass.ds(t + 1, 1), 0:D].rearrange("p o c -> p (o c)")).then_inc(ag_made, 1)

            def log(t):
                act.wait_ge(neg_made, t + 1)
                nc.scalar.activation(neg[:], neg[:], ACT.Exp)
                act.drain()
                nc.scalar.activation(neg[:], neg[:], ACT.Ln, scale=0.5, bias=half[:]).then_inc(log_made, 1)

            take_turned(0)
            log(0)
            with act.Fori(0, NT - 1) as t:
                take_turned(t + 1)
                norm_root(nc, act, nl, t)
                log(t + 1)
            norm_root(nc, act, nl, NT - 1)

        @block.vector
        def _(dve):
            vec.memset(half[:], 0.5)
            vec.memset(hs[:], 1.0)
            vec.memset(zero[:], 0.0)
            dve.drain()
            dve.nop().then_inc(zeroed, 1)
            dve.nop().then_inc(used, 1)
            dve.wait_ge(landed, 16 * 7)

            def negate(t):
                dve.wait_ge(hid, t + 1)
                for o in range(2):
                    vec.tensor_scalar(f1[:, o, :], psf[:, o * P:o * P + P], b1[:, o:o + 1], None, ALU.add)
                dve.drain()
                soft(nc, dve, f1[:], neg[:]).then_inc(neg_made, 1)

            def make_h1(t):
                dve.wait_ge(log_made, t + 1)
                vec.scalar_tensor_tensor(h1[:], f1[:], 0.0, neg[:], ALU.max, ALU.add).then_inc(h1_made, 1)

            def residual(t):
                dve.wait_ge(o_made, t + 1)
                vec.tensor_tensor(o1[:], pso[0:P, 0:D], b2[:], ALU.add)
                dve.drain()
                dve.wait_ge(x_in, t * 16 + 16)
                vec.tensor_tensor(r1[:], o1[:], x2[:], ALU.add).then_inc(used, 1)
                norm_statistics(nc, dve, nl, r1[:])

            def scale(t):
                dve.wait_ge(stored, t + 1)
                norm_scale(nc, dve, nl, t, x3[:], r1[:]).then_inc(x3_made, 1)
                dve.wait_ge(x3_turned, t + 1)
                vec.tensor_copy(x3t[:].rearrange("p b n -> p (b n)"), psu[:, 0:2 * P]).then_inc(x3t_made, 1)

            def store(t):
                dve.wait_ge(table, t + 1)
                vec.tensor_tensor(hs[:, 0:D], psh[0:P, 0:D], b3[:], ALU.add).then_inc(made, 1)

            negate(0)
            make_h1(0)
            with dve.Fori(0, NT - 1) as t:
                residual(t)
                negate(t + 1)
                scale(t)
                make_h1(t + 1)
                store(t)
            residual(NT - 1)
            scale(NT - 1)
            store(NT - 1)


def source_sum(nc, mem, dr, keep):
    W = D + 1
    U = 2 * HF
    idx, gx = mem.sb("idx", [P, U], I32), mem.sb("gx", [P, U, W])
    si = mem.sb("si", [P, 2, HF, P], I32)
    col = mem.sb("col", [P, U], I32)
    sf, eq, hit = mem.sb("sf", [P, HF]), mem.sb("eq", [P, U, P]), mem.sb("hit", [P, HF, P])
    low, column = mem.sb("low", [128, 128]), mem.sb("column", [128, 3])
    before, off, tgt = mem.sb("before", [P, HF]), mem.sb("off", [P, HF]), mem.sb("tgt", [P, U], I32)
    ms = mem.sb("ms", [P, U, W])
    pss = [mem.ps(f"s{j}") for j in range(HF)]
    (landed, listed, nopped, summed, taken, eq_made, sums_made) = (mem.sem(n) for n in (
        "landed", "listed", "nopped", "summed", "taken", "eq_made", "sums_made"))
    x_in, s_in, free, done = ([mem.sem(f"{n}{q}") for q in range(2)] for n in ("x", "s", "f", "d"))
    vec = nc.vector
    TURNS = ET // U

    with nc.Block() as block:
        @block.sync
        def _(sp):
            sp.dma_start(low[:], dr["c_low"]).then_inc(landed, 16)
            sp.dma_start(column[:], dr["c_column"]).then_inc(landed, 16)
            with sp.Fori(0, TURNS) as i:
                for q in range(2):
                    sp.wait_ge(free[q], i + 1)
                    sp.dma_start(si[:, q].rearrange("p j e -> p (j e)"),
                                 dr["src"][bass.ds(i * (U * P) + q * HF * P, HF * P)].partition_broadcast(P)).then_inc(s_in[q], 16)

        @block.gpsimd
        def _(pool):
            def gather(i, q):
                pool.wait_ge(sums_made, 2 * i + q + 1)
                pool.nop().then_inc(nopped, 1)
                nc.gpsimd.tensor_copy(idx[:, HF * q:HF * q + HF],
                                      keep["dst_tile"][:, bass.ds(i * U + HF * q, HF)]).then_inc(listed, 1)
                pool.wait_ge(listed, 2 * i + q + 1)
                pool.nop().then_inc(nopped, 1)
                for j in range(HF * q, HF * q + HF):
                    nc.gpsimd.indirect_dma_start(
                        out=gx[:, j, :], out_offset=None, in_=dr["h3"],
                        in_offset=bass.IndirectOffsetOnAxis(ap=idx[:, j:j + 1], axis=0)).then_inc(x_in[q], 16)

            def scatter(i, q):
                pool.wait_ge(sums_made, 2 * i + q + 3)
                if not (isinstance(i, int) and i + q == 0):
                    pool.wait_ge(done[1 - q], (i + q) * (16 * HF))
                    pool.nop().then_inc(nopped, 1)
                for j in range(HF):
                    n = HF * q + j
                    nc.gpsimd.indirect_dma_start(
                        out=dr["sum"][j], out_offset=bass.IndirectOffsetOnAxis(ap=tgt[:, n:n + 1], axis=0),
                        in_=ms[:, n, :], in_offset=None, compute_op=ALU.add).then_inc(done[q], 16)

            pool.wait_ge(landed, 32)
            gather(0, 0)
            gather(0, 1)
            scatter(0, 0)
            with pool.Fori(1, TURNS) as i:
                gather(i, 0)
                scatter(i - 1, 1)
                gather(i, 1)
                scatter(i, 0)
            scatter(TURNS - 1, 1)
            for q in range(2):
                pool.wait_ge(done[q], TURNS * 16 * HF)

        @block.tensor
        def _(pe):
            for j in range(HF):
                pe.nop().then_inc(taken, 1)
            with pe.Fori(0, TURNS) as i:
                for q in range(2):
                    pe.wait_ge(eq_made, 2 * i + q + 1)
                    pe.wait_ge(x_in[q], i * (16 * HF) + 16 * HF)
                    for j in range(HF):
                        pe.wait_ge(taken, i * U + q * HF + j + 1)
                        nc.tensor.matmul(pss[j][0:P, 0:W], eq[:, HF * q + j, :], gx[:, HF * q + j, :], start=True,
                                         stop=True).then_inc(summed, 1)

        @block.vector
        def _(dve):
            for q in range(2):
                dve.nop().then_inc(sums_made, 1)
                dve.nop().then_inc(free[q], 1)
            dve.wait_ge(landed, 32)
            def tiles(i, first):
                for q in range(2):
                    half = slice(HF * q, HF * q + HF)
                    vec.tensor_copy(sf[:], keep["src_tile"][:, bass.ds(i * U + HF * q, HF)])
                    dve.drain()
                    dve.wait_ge(s_in[q], i * 16 + 16)
                    for j in range(HF):
                        vec.tensor_scalar(eq[:, HF * q + j, :], si[:, q, j, :], sf[:, j:j + 1], None, ALU.is_equal)
                    dve.drain()
                    dve.nop().then_inc(eq_made, 1)
                    dve.nop().then_inc(free[q], 1)
                    for j in range(HF):
                        vec.tensor_tensor_reduce(out=hit[:, j, :], in0=eq[:, HF * q + j, :], in1=low[0:P, 0:P], scale=1.0,
                                                 scalar=0.0, op0=ALU.mult, op1=ALU.add, accum_out=before[:, j:j + 1])
                    dve.drain()
                    vec.tensor_scalar(before[:], before[:], 1.0, None, ALU.min)
                    vec.tensor_scalar(off[:], sf[:], column[0:P, 2:3], -1.0, ALU.subtract, ALU.mult)
                    dve.drain()
                    vec.tensor_tensor(off[:], off[:], before[:], ALU.mult)
                    dve.drain()
                    if not first:
                        dve.wait_ge(done[q], i * (16 * HF))
                    vec.tensor_tensor(tgt[:, half], off[:], sf[:], ALU.add)
                    for j in range(HF):
                        dve.wait_ge(summed, i * U + q * HF + j + 1)
                        vec.tensor_copy(ms[:, HF * q + j, :], pss[j][0:P, 0:W]).then_inc(taken, 1)
                    dve.drain()
                    dve.nop().then_inc(sums_made, 1)

            tiles(0, True)
            with dve.Fori(1, TURNS) as i:
                tiles(i, False)


def nodes_mean(nc, mem, dr):
    nl = norm_buffers(mem)
    W = D + 1
    sm, x3 = mem.sb("sm", [P, 2, HF, W]), mem.sb("x3", [P, 2, D])
    s1, s2 = mem.sb("s1", [P, 2, W]), mem.sb("s2", [P, W])
    cnt, r1, res = mem.sb("cnt", [P, 2]), mem.sb("r1", [P, D]), mem.sb("res", [P, D])
    used, made, done, stored = (mem.sem(n) for n in ("used", "made", "done", "stored"))
    x_in = [mem.sem(f"x_in{q}") for q in range(2)]
    vec = nc.vector

    with nc.Block() as block:
        @block.sync
        def _(sp):
            def load(t, q):
                for j in range(HF):
                    sp.dma_start(sm[:, q, j, :], rows(dr["sum"][j], t)).then_inc(x_in[q], 16)
                sp.dma_start(x3[:, q, :], rows(dr["x3"], t)).then_inc(x_in[q], 16)

            load(0, 0)
            with sp.Fori(0, (NT - 1) // 2) as i:
                for q in range(2):
                    sp.wait_ge(used, 2 * i + q + 1)
                    load(2 * i + q + 1, 1 - q)
            sp.wait_ge(used, NT + 1)

        @block.scalar
        def _(act):
            with act.Fori(0, NT) as t:
                norm_root(nc, act, nl, t)
                act.wait_ge(made, t + 1)
                act.dma_start(rows(dr["out"], t), res[:]).then_inc(done, 16)
                act.wait_ge(done, t * 16 + 16)
                act.nop().then_inc(stored, 1)

        @block.vector
        def _(dve):
            dve.nop().then_inc(used, 1)
            dve.nop().then_inc(stored, 1)

            def tile(t, q, landings):
                dve.wait_ge(x_in[q], landings)
                vec.tensor_tensor(s1[:], sm[:, q, 0:2, :], sm[:, q, 2:4, :], ALU.add)
                dve.drain()
                vec.tensor_tensor(s2[:], s1[:, 0, :], s1[:, 1, :], ALU.add)
                dve.drain()
                vec.tensor_scalar(cnt[:, 0:1], s2[:, D:W], 1.0, None, ALU.max)
                dve.drain()
                vec.reciprocal(cnt[:, 1:2], cnt[:, 0:1])
                dve.drain()
                vec.scalar_tensor_tensor(r1[:], s2[:, 0:D], cnt[:, 1:2], x3[:, q, :], ALU.mult, ALU.add).then_inc(used, 1)
                norm_statistics(nc, dve, nl, r1[:])
                dve.wait_ge(stored, t + 1)
                norm_scale(nc, dve, nl, t, res[:], r1[:]).then_inc(made, 1)
                dve.drain()

            with dve.Fori(0, (NT - 1) // 2) as i:
                for q in range(2):
                    tile(2 * i + q, q, i * 80 + 80)
            tile(NT - 1, 0, 80 * ((NT + 1) // 2))


def build(nc, dr):
    for name, shape in (("ordered", (E, 3)), ("rho", (NCOL, R)), ("ends", (2, ET)), ("carry", (4, 4, ET)), ("x0", (N, D)), ("x1", (N, D)),
                        ("x2", (N, D)), ("x3", (N, D)), ("xw", (2 * N, 512)), ("xw1", (2 * N, 128)), ("kt", (2 * N, 4)),
                        ("qt", (2 * N, 4)), ("kt1", (2 * N, 1)), ("qt1", (2 * N, 1)), ("qe", (E + N, 8)), ("qe1", (E + N, 2)), ("h2", (N, D)), ("h3", (N, D + 1))):
        dr[name] = nc.dram_tensor("scratch_" + name, shape, F32, kind="Internal").ap()
    dr["sum"] = [nc.dram_tensor(f"scratch_sum{j}", (N + P, D + 1), F32, kind="Internal").ap() for j in range(HF)]

    def phase(name):
        return Mem(nc, name)

    with phase("turned") as outer:
        mt = outer.sb("mt", [128, 2, D])
        with phase("steps") as columns:
            col = columns.sb("col", [128, 4, NCOL])
            turns = columns.sb("turns", [1, 1], I32)
            with phase("sorted") as mem:
                layer0_order(nc, mem, dr, turns)
            with phase("prepare") as mem:
                layer0_prepare(nc, mem, dr, col)
            with phase("turn") as mem:
                layer0_turn(nc, mem, dr, col, turns, mt)
        with phase("gate") as mem:
            nodes_gate(nc, mem, dr, mt)
    with phase("keep") as keeper:
        keep = edge_lists(keeper)
        agg = keeper.sb("agg", [P, NT + 1, 516])
        with phase("order") as mem:
            edge_order(nc, mem, dr, keep)
        with phase("kept") as outer:
            kept = outer.sb("h", [P, NT, 512])
            with phase("weights1") as mem:
                attention_weights(nc, mem, dr, keep, 4, 1)
            with phase("sum1") as mem:
                attention_sum(nc, mem, dr, keep, agg, dr["xw"], 4, 512, 1)
            with phase("attend1") as mem:
                nodes_attend(nc, mem, dr, agg, kept, "L1_gnn_b1", ("L1_gnn_W2", "W2_t", "L1_gnn_k2", "L1_gnn_q2"),
                             512, 4, True)
            with phase("weights2") as mem:
                attention_weights(nc, mem, dr, keep, 4, 2)
            with phase("sum2") as mem:
                attention_sum(nc, mem, dr, keep, agg, dr["xw"], 4, 512, 2)
            with phase("attend2") as mem:
                nodes_attend(nc, mem, dr, agg, kept, "L1_gnn_b2", ("L1_gnn_W3", "W3_t", "L1_gnn_k3", "L1_gnn_q3"),
                             128, 1, False)
        with phase("weights3") as mem:
            attention_weights(nc, mem, dr, keep, 1, 3)
        with phase("sum3") as mem:
            attention_sum(nc, mem, dr, keep, agg, dr["xw1"], 1, 128, 3)
        with phase("mix") as mem:
            nodes_mix(nc, mem, dr, agg)
        with phase("filter") as mem:
            filter_sum(nc, mem, dr, keep, agg)
        with phase("filtered") as mem:
            nodes_filter(nc, mem, dr, agg)
        with phase("source") as mem:
            source_sum(nc, mem, dr, keep)
        with phase("mean") as mem:
            nodes_mean(nc, mem, dr)


_INS = [
    "x", "src", "dst", "edge_type_2", "edge_weight", "L1_gnn_query", "L1_gnn_gate_w1", "L1_gnn_gate_b1",
    "L1_gnn_gate_w2", "L1_gnn_gate_b2", "L1_gnn_W1", "L1_gnn_q1", "L1_gnn_k1", "L1_gnn_b1", "L1_gnn_W2", "L1_gnn_q2",
    "L1_gnn_k2", "L1_gnn_b2", "L1_gnn_W3", "L1_gnn_q3", "L1_gnn_k3", "L1_gnn_b3", "L1_gnn_proj_w", "L1_gnn_proj_b",
    "L2_gnn_aw_W", "L2_gnn_aw_b", "L2_gnn_m1_W", "L2_gnn_m1_b", "L2_gnn_m2_W", "L2_gnn_m2_b", "L2_gnn_o1_W",
    "L2_gnn_o1_b", "L2_gnn_o2_W", "L2_gnn_o2_b", "L3_gnn_W", "L3_gnn_b"]


def kernel(**inputs):
    import concourse.bacc as bacc
    from concourse.bass_utils import run_bass_kernel_spmd

    arrays = {name: np.ascontiguousarray(inputs[name]) for name in _INS}
    arrays["x_t2"] = np.ascontiguousarray(np.pad(np.asarray(inputs["x"]).T, ((0, 0), (0, P))))
    arrays["ea_t"] = np.ascontiguousarray(np.asarray(inputs["edge_attr_50"]).T)
    for n in (1, 2, 3):
        arrays[f"W{n}_t"] = np.ascontiguousarray(np.asarray(inputs[f"L1_gnn_W{n}"]).transpose(0, 2, 1))
    arrays.update(host_constants())
    nc = bacc.Bacc("TRN2", target_bir_lowering=False, num_devices=1)
    dr = {n: nc.dram_tensor("in_" + n, a.shape, mybir.dt.from_np(a.dtype), kind="ExternalInput").ap()
          for n, a in arrays.items()}
    dr["out"] = nc.dram_tensor("out_x", (N, D), F32, kind="ExternalOutput").ap()
    build(nc, dr)
    r = run_bass_kernel_spmd(nc, [{"in_" + n: a for n, a in arrays.items()}], core_ids=[0])
    return r.results[0]["out_x"]
```
